# Optimizing a Trainium2 kernel written in Bass

```python
import numpy as np
import jax
import jax.numpy as jnp

def _softmax(x, axis=-1):
    return jax.nn.softmax(x, axis=axis)

def _gelu(x):
    return jax.nn.gelu(x, approximate=True)

def _silu(x):
    return jax.nn.silu(x)

def _sigmoid(x):
    return jax.nn.sigmoid(x)

def _layernorm(x, axis=-1, eps=1e-05):
    m = jnp.mean(x, axis=axis, keepdims=True)
    v = jnp.var(x, axis=axis, keepdims=True)
    return (x - m) / jnp.sqrt(v + eps)

def _scatter_add(tgt, idx, src, axis=0):
    return tgt.at[idx].add(src)

def _segment_sum(src, seg, n):
    return jax.ops.segment_sum(src, seg, n)
kernel_name = 'mk_xattn_ffn_d2_seqx_r8_440429'

def setup_inputs(seed: int=0):
    np.random.seed(seed)
    _w = jnp.asarray

    def _rec_inputs():
        import jax
        import jax.numpy as jnp
        _rk = jax.random.key(seed)
        x = -0.000125 + 0.9999 * jax.random.normal(jax.random.fold_in(_rk, 1), (32, 64, 512), jnp.float32)
        _lenS = 64 - jax.random.randint(jax.random.fold_in(_rk, 7), (32,), 0, max(1, 64 // 4) + 1, jnp.int32)
        _lenS2 = 64 - jax.random.randint(jax.random.fold_in(_rk, 8), (32,), 0, max(1, 64 // 4) + 1, jnp.int32)
        _ctx_4096P = jax.random.normal(jax.random.fold_in(_rk, 11), (32, 16, 512), jnp.float32)
        _ctx_4096c = jax.random.dirichlet(jax.random.fold_in(_rk, 511), 0.3 * jnp.ones((16,), jnp.float32), (32, 64))
        _ctx_4096t = jnp.einsum('bsk,bkd->bsd', _ctx_4096c, _ctx_4096P)
        _ctx_4096t = _ctx_4096t * jax.lax.rsqrt(jnp.mean(jnp.square(_ctx_4096t)) + 1e-12) * 0.953939
        ctx_4096 = -1.52775e-05 + 0.999936 * (_ctx_4096t + 0.3 * jax.random.normal(jax.random.fold_in(_rk, 611), (32, 64, 512), jnp.float32))
        return (x, ctx_4096)
    x, ctx_4096 = _rec_inputs()

    def _L0_xattn_setup():
        import jax, jax.numpy as jnp
        import numpy as np
        NUM_HEADS = 8

        def _proj(W, b, x):
            return jnp.einsum('oi,bil->bol', W, x) + b[:, None]
        key = jax.random.key(seed)
        ks = jax.random.split(key, 11)
        B, D, L = (16, 64, 512)
        s = 1.0 / np.sqrt(D).astype(np.float32)
        return {'x_query': jax.random.normal(ks[0], (B, D, L), jnp.float32), 'x_key': jax.random.normal(ks[1], (B, D, L), jnp.float32), 'x_value': jax.random.normal(ks[2], (B, D, L), jnp.float32), 'Wq': jax.random.normal(ks[3], (D, D), jnp.float32) * s, 'bq': jax.random.normal(ks[4], (D,), jnp.float32) * 0.01, 'Wk': jax.random.normal(ks[5], (D, D), jnp.float32) * s, 'bk': jax.random.normal(ks[6], (D,), jnp.float32) * 0.01, 'Wv': jax.random.normal(ks[7], (D, D), jnp.float32) * s, 'bv': jax.random.normal(ks[8], (D,), jnp.float32) * 0.01, 'Wo': jax.random.normal(ks[9], (D, D), jnp.float32) * s, 'bo': jax.random.normal(ks[10], (D,), jnp.float32) * 0.01}
    _L0_xattn_all = _L0_xattn_setup()
    _L0_xattn_in = {k: v for k, v in _L0_xattn_all.items() if k in ('Wq', 'bq', 'Wk', 'bk', 'Wv', 'bv', 'Wo', 'bo')}
    del _L0_xattn_all

    def _L0_ffn_setup():
        import jax, jax.numpy as jnp
        import numpy as np
        TOP_K = 2
        key = jax.random.key(seed)
        k0, k1, k2 = jax.random.split(key, 3)
        B, S, D, H, E = (4, 256, 512, 512, 8)
        sc = 1.0 / np.sqrt(D).astype(np.float32)
        x = jax.random.normal(k0, (B, S, D), dtype=jnp.float32)
        W_gate = jax.random.normal(k1, (D, E), dtype=jnp.float32) * sc
        b_gate = jnp.zeros((E,), dtype=jnp.float32)
        W_e = jax.random.normal(k2, (E, D, H), dtype=jnp.float32) * sc
        b_e = jnp.zeros((E, H), dtype=jnp.float32)
        return {'x': x, 'W_gate': W_gate, 'b_gate': b_gate, 'W_e': W_e, 'b_e': b_e}
    _L0_ffn_all = _L0_ffn_setup()
    _L0_ffn_in = {k: v for k, v in _L0_ffn_all.items() if k in ('W_gate', 'b_gate', 'W_e', 'b_e')}
    del _L0_ffn_all

    def _L1_xattn_setup():
        import jax, jax.numpy as jnp
        import numpy as np
        EMBED = 512
        HEADS = 32
        GROUP = 4
        KV_HEADS = HEADS // GROUP
        HEAD_DIM = EMBED // HEADS
        B, S = (2, 256)
        key = jax.random.key(seed)
        ks = jax.random.split(key, 7)
        scale = 0.02
        return {'queries': jax.random.normal(ks[0], (B, S, EMBED), dtype=jnp.float32), 'keys': jax.random.normal(ks[1], (B, S, EMBED), dtype=jnp.float32), 'values': jax.random.normal(ks[2], (B, S, EMBED), dtype=jnp.float32), 'Wq': jax.random.normal(ks[3], (EMBED, EMBED), dtype=jnp.float32) * scale, 'Wk': jax.random.normal(ks[4], (EMBED, KV_HEADS * HEAD_DIM), dtype=jnp.float32) * scale, 'Wv': jax.random.normal(ks[5], (EMBED, KV_HEADS * HEAD_DIM), dtype=jnp.float32) * scale, 'Wo': jax.random.normal(ks[6], (EMBED, EMBED), dtype=jnp.float32) * scale}
    _L1_xattn_all = _L1_xattn_setup()
    _L1_xattn_in = {k: v for k, v in _L1_xattn_all.items() if k in ('Wq', 'Wk', 'Wv', 'Wo')}
    del _L1_xattn_all

    def _L1_ffn_setup():
        import jax, jax.numpy as jnp
        import numpy as np
        HIDDEN = 512
        INTER = 1376
        BATCH, SEQ = (2, 256)
        key = jax.random.key(seed)
        ks = jax.random.split(key, 7)
        s_h = 1.0 / np.sqrt(HIDDEN)
        s_i = 1.0 / np.sqrt(INTER)
        return {'hidden_states': jax.random.normal(ks[0], (BATCH, SEQ, HIDDEN), dtype=jnp.float32), 'w_gate': jax.random.uniform(ks[1], (INTER, HIDDEN), jnp.float32, -s_h, s_h), 'b_gate': jax.random.uniform(ks[2], (INTER,), jnp.float32, -s_h, s_h), 'w_up': jax.random.uniform(ks[3], (INTER, HIDDEN), jnp.float32, -s_h, s_h), 'b_up': jax.random.uniform(ks[4], (INTER,), jnp.float32, -s_h, s_h), 'w_down': jax.random.uniform(ks[5], (HIDDEN, INTER), jnp.float32, -s_i, s_i), 'b_down': jax.random.uniform(ks[6], (HIDDEN,), jnp.float32, -s_i, s_i)}
    _L1_ffn_all = _L1_ffn_setup()
    _L1_ffn_in = {k: v for k, v in _L1_ffn_all.items() if k in ('w_gate', 'b_gate', 'w_up', 'b_up', 'w_down', 'b_down')}
    del _L1_ffn_all
    return {'x': x, 'ctx_4096': ctx_4096, 'L0_xattn_Wq': _L0_xattn_in['Wq'], 'L0_xattn_bq': _L0_xattn_in['bq'], 'L0_xattn_Wk': _L0_xattn_in['Wk'], 'L0_xattn_bk': _L0_xattn_in['bk'], 'L0_xattn_Wv': _L0_xattn_in['Wv'], 'L0_xattn_bv': _L0_xattn_in['bv'], 'L0_xattn_Wo': _L0_xattn_in['Wo'], 'L0_xattn_bo': _L0_xattn_in['bo'], 'L0_ffn_W_gate': _L0_ffn_in['W_gate'], 'L0_ffn_b_gate': _L0_ffn_in['b_gate'], 'L0_ffn_W_e': _L0_ffn_in['W_e'], 'L0_ffn_b_e': _L0_ffn_in['b_e'], 'L1_xattn_Wq': _L1_xattn_in['Wq'], 'L1_xattn_Wk': _L1_xattn_in['Wk'], 'L1_xattn_Wv': _L1_xattn_in['Wv'], 'L1_xattn_Wo': _L1_xattn_in['Wo'], 'L1_ffn_w_gate': _L1_ffn_in['w_gate'], 'L1_ffn_b_gate': _L1_ffn_in['b_gate'], 'L1_ffn_w_up': _L1_ffn_in['w_up'], 'L1_ffn_b_up': _L1_ffn_in['b_up'], 'L1_ffn_w_down': _L1_ffn_in['w_down'], 'L1_ffn_b_down': _L1_ffn_in['b_down']}

def reference(x, ctx_4096, L0_xattn_Wq, L0_xattn_bq, L0_xattn_Wk, L0_xattn_bk, L0_xattn_Wv, L0_xattn_bv, L0_xattn_Wo, L0_xattn_bo, L0_ffn_W_gate, L0_ffn_b_gate, L0_ffn_W_e, L0_ffn_b_e, L1_xattn_Wq, L1_xattn_Wk, L1_xattn_Wv, L1_xattn_Wo, L1_ffn_w_gate, L1_ffn_b_gate, L1_ffn_w_up, L1_ffn_b_up, L1_ffn_w_down, L1_ffn_b_down):
    import jax
    import jax.numpy as jnp

    def _L0_xattn_ref(x_query, x_key, x_value, Wq, bq, Wk, bk, Wv, bv, Wo, bo):
        import jax, jax.numpy as jnp
        import numpy as np
        NUM_HEADS = 8

        def _proj(W, b, x):
            return jnp.einsum('oi,bil->bol', W, x) + b[:, None]
        B, D, L = x_query.shape
        h = NUM_HEADS
        Lh = L // h
        q = _proj(Wq, bq, x_query)
        k = _proj(Wk, bk, x_key)
        v = _proj(Wv, bv, x_value)
        qh = q.reshape(B, D, h, Lh).transpose(2, 0, 1, 3)
        kh = k.reshape(B, D, h, Lh).transpose(2, 0, 1, 3)
        vh = v.reshape(B, D, h, Lh).transpose(2, 0, 1, 3)
        scale = 1.0 / jnp.sqrt(jnp.asarray(Lh, x_query.dtype))
        scores = jnp.einsum('hbdk,hbek->hbde', qh, kh) * scale
        p = jax.nn.softmax(scores, axis=-1)
        xh = jnp.einsum('hbde,hbek->hbdk', p, vh)
        x = xh.transpose(1, 2, 0, 3).reshape(B, D, L)
        return _proj(Wo, bo, x)

    def _L0_ffn_ref(x, W_gate, b_gate, W_e, b_e):
        import jax, jax.numpy as jnp
        import numpy as np
        TOP_K = 2
        logits = x @ W_gate + b_gate
        _, top_idx = jax.lax.top_k(logits, TOP_K)
        y_all = jax.nn.relu(jnp.einsum('bsd,edh->bseh', x, W_e) + b_e)
        y = jnp.take_along_axis(y_all, top_idx[..., None], axis=2)
        return y.mean(axis=2)

    def _L1_xattn_ref(queries, keys, values, Wq, Wk, Wv, Wo):
        import jax, jax.numpy as jnp
        import numpy as np
        EMBED = 512
        HEADS = 32
        GROUP = 4
        KV_HEADS = HEADS // GROUP
        HEAD_DIM = EMBED // HEADS
        B, S = (2, 256)
        b, s, _ = queries.shape
        q = (queries @ Wq).reshape(b, s, KV_HEADS, GROUP, HEAD_DIM)
        k = (keys @ Wk).reshape(b, s, KV_HEADS, HEAD_DIM)
        v = (values @ Wv).reshape(b, s, KV_HEADS, HEAD_DIM)
        scale = 1.0 / jnp.sqrt(jnp.asarray(HEAD_DIM, dtype=q.dtype))
        scores = jnp.einsum('bqhgd,bkhd->bhgqk', q, k) * scale
        attn = jax.nn.softmax(scores, axis=-1)
        out = jnp.einsum('bhgqk,bkhd->bqhgd', attn, v)
        out = out.reshape(b, s, EMBED)
        return out @ Wo

    def _L1_ffn_ref(hidden_states, w_gate, b_gate, w_up, b_up, w_down, b_down):
        import jax, jax.numpy as jnp
        import numpy as np
        HIDDEN = 512
        INTER = 1376
        BATCH, SEQ = (2, 256)
        gate = jax.nn.silu(jnp.einsum('bsh,ih->bsi', hidden_states, w_gate) + b_gate)
        up = jnp.einsum('bsh,ih->bsi', hidden_states, w_up) + b_up
        return jnp.einsum('bsi,hi->bsh', gate * up, w_down) + b_down
    x = x + _L0_xattn_ref(_layernorm(x, axis=-1), ctx_4096, ctx_4096, L0_xattn_Wq, L0_xattn_bq, L0_xattn_Wk, L0_xattn_bk, L0_xattn_Wv, L0_xattn_bv, L0_xattn_Wo, L0_xattn_bo)
    x = x + _L0_ffn_ref(_layernorm(x, axis=-1), L0_ffn_W_gate, L0_ffn_b_gate, L0_ffn_W_e, L0_ffn_b_e)
    x = x + _L1_xattn_ref(_layernorm(x, axis=-1), ctx_4096, ctx_4096, L1_xattn_Wq, L1_xattn_Wk, L1_xattn_Wv, L1_xattn_Wo)
    x = x + _L1_ffn_ref(_layernorm(x, axis=-1), L1_ffn_w_gate, L1_ffn_b_gate, L1_ffn_w_up, L1_ffn_b_up, L1_ffn_w_down, L1_ffn_b_down)
    return x

_drawn_inputs = setup_inputs


def setup_inputs(seed=0):
    import zlib

    import numpy as np

    out = dict(_drawn_inputs(seed))
    spreads = {'L0_ffn_b_gate': (0.0, 0.1), 'L0_ffn_b_e': (0.0, 0.1)}
    factors = {'L0_xattn_bq': 4.033,
     'L0_xattn_bk': 2.949,
     'L0_xattn_bv': 4.588,
     'L0_xattn_bo': 6.045,
     'L1_xattn_Wq': 8.0,
     'L1_xattn_Wk': 8.0,
     'L1_ffn_b_gate': 8.0,
     'L1_ffn_b_up': 8.0,
     'L1_ffn_b_down': 4.284}
    for name, (base, spread) in spreads.items():
        noise = np.random.default_rng([zlib.crc32(name.encode()), seed]).standard_normal(out[name].shape)
        drawn = base * np.exp(spread * noise) if base else spread * noise
        out[name] = jnp.asarray(drawn.astype(out[name].dtype))
    for name, factor in factors.items():
        out[name] = (out[name] * factor).astype(out[name].dtype)
    return out
```

```python
import concourse.bass as bass
from concourse import mybir
from contextlib import ExitStack

F32 = mybir.dt.float32
F32R = mybir.dt.float32r
BF16 = mybir.dt.bfloat16
I32 = mybir.dt.int32
U32 = mybir.dt.uint32
ALU = mybir.AluOpType
ACT = mybir.ActivationFunctionType
AX = mybir.AxisListType

P = 128
BATCH, SEQ, DIM = 32, 64, 512
TILES = BATCH * SEQ // P
KD = DIM // P
EPS = 1e-5

H0 = 8
LH = DIM // H0
SCALE0 = LH ** -0.5

EXPERTS = 8
EW = KD * DIM
REGION = BATCH * SEQ + P
BLOCKS = 2 * TILES + EXPERTS - 1

KVH, GROUP, HD = 8, 4, 16
SCALE1 = HD ** -0.5
INTER = 1376
NI = -(-INTER // P)
TG = 4


def after(eng, *counts, tick):
    for n, (sem, value) in enumerate(counts):
        if not isinstance(value, int):
            eng.wait_ge(sem, value)
            if n == len(counts) - 1 or eng.engine == mybir.EngineType.SP:
                eng.sem_inc(tick, 1)
        elif value > 0:
            eng.wait_ge(sem, value)


def slot_full(t, par):
    return 16 * (t // 2 + 1) if isinstance(t, int) else t * 8 + (16 - 8 * par)


def upto(t, tiles):
    return min(t, tiles) if isinstance(t, int) else t


def pipelined(eng, tiles, stages):
    last_lag = max(lag for _, lag in stages)
    first = last_lag + 2 + last_lag % 2
    until = first + (tiles - first) // 2 * 2

    def peeled(s):
        for stage, lag in stages:
            if 0 <= s - lag < tiles:
                stage(s - lag, (s - lag) % 2)

    for s in range(first):
        peeled(s)
    with eng.Fori(first // 2, until // 2) as i:
        for odd in range(2):
            for stage, lag in stages:
                stage(2 * i + (odd - lag), (odd - lag) % 2)
    for s in range(until, tiles + last_lag):
        peeled(s)


class Ctx:

    def __init__(self, nc, stack, prefix):
        self.nc, self.stack, self.prefix = nc, stack, prefix
        self.sems = []

    def sb(self, name, shape, dt=F32):
        return self.stack.enter_context(self.nc.sbuf_tensor(self.prefix + name, shape, dt))

    def pb(self, name):
        return self.stack.enter_context(self.nc.psum_tensor(self.prefix + name, [P, 512], F32))

    def sem(self, name):
        self.sems.append(self.stack.enter_context(self.nc.semaphore(self.prefix + name)))
        return self.sems[-1]

    def clear(self):
        with self.nc.Block() as block:
            @block.gpsimd
            def _(pool):
                numbers = sorted(s.num for s in self.sems)
                first = 0
                for n in range(1, len(numbers) + 1):
                    if n == len(numbers) or numbers[n] != numbers[n - 1] + 1:
                        pool.sem_clear(range(numbers[first], numbers[n - 1] + 1))
                        first = n


def block_diagonal(ap):
    return ap[0:64, 0:64], ap[64:128, 64:128]


def layer0_phase(nc, shared, a):
    with ExitStack() as stack:
        c = Ctx(nc, stack, "a_")
        sb, pb, sem = c.sb, c.pb, c.sem
        wq, wk, wv, wo = (sb(n, [P, P]) for n in ("wq", "wk", "wv", "wo"))
        bq, bk = sb("bq", [P, 2, 64]), sb("bk", [P, 2, 64])
        bv, bo = sb("bv", [P, 1]), sb("bo", [P, 1])
        wg, bg = sb("wg", [P, KD, EXPERTS]), sb("bg", [P, EXPERTS])
        ident = sb("ident", [P, P])
        ctx_in, x_in, x_res, xn, xn2 = (sb(n, [P, 2, DIM]) for n in ("ctx_in", "x_in", "x_res", "xn", "xn2"))
        qT, kT, score, probT, attn, xT = (sb(n, [P, 2, DIM]) for n in ("qT", "kT", "score", "probT", "attn", "xT"))
        minus_half = sb("minus_half", [P, 1])
        v = sb("v", [P, 2, H0, LH + 1])
        wstage = sb("wstage", [P, 2, 1024])
        stats, mv, rstd = sb("stats", [P, 2, 6]), sb("mv", [P, 2, 2]), sb("rstd", [P, 2, 2])
        stats2, mv2, rstd2 = sb("stats2", [P, 2, 6]), sb("mv2", [P, 2, 2]), sb("rstd2", [P, 2, 2])
        smax = sb("smax", [P, 2, 8])
        rsum = sb("rsum", [P, 2, 2, 4, 1])
        logit, peak8, turn = sb("logit", [P, 2, 8]), sb("peak8", [P, 2, 2]), sb("turn", [P, 2, 8])
        both, rank = sb("both", [P, 2, 8], BF16), sb("rank", [P, 2, 8])
        picked = sb("picked", [P, 2, 2, 8])
        ati = sb("ati", [P, 2, 2], I32)
        seen = sb("seen", [P, 8])
        seenb = sb("seenb", [P, 8], BF16)
        from_last, region_at = sb("from_last", [P, 8]), sb("region_at", [P, 8])
        before, ones = sb("before", [P, P], BF16), sb("ones", [P, P], BF16)
        zero_rows = sb("zero_rows", [P, DIM])
        k128, below = sb("k128", [P, 8, 16]), sb("below", [P, 8, 8])
        counts, nblk, start, end = sb("counts", [P, 8]), sb("nblk", [P, 8]), sb("start", [P, 8]), sb("end", [P, 8])
        over, lower = sb("over", [P, 8, 16]), sb("lower", [P, 8, 8])
        blk, passed, bstart = sb("blk", [P, BLOCKS]), sb("passed", [P, BLOCKS, 8]), sb("bstart", [P, BLOCKS])
        bexp, table = sb("bexp", [P, BLOCKS]), sb("table", [P, 2, BLOCKS])
        padf, padi, shift = sb("padf", [P, 8]), sb("padi", [P, 8], I32), sb("shift", [P, 8])
        at_kept2 = sb("at_kept2", [P, 2 * TILES])
        moved = sb("moved", [P, TILES * 2, 8])
        at_kept, hot_kept = sb("at_kept", [P, TILES, 2]), sb("hot_kept", [P, TILES, 2, 8])

        pk, pq, pv, ps, pt, py = (pb(n) for n in ("pk", "pq", "pv", "ps", "pt", "py"))
        po = stack.enter_context(nc.psum_tensor("a_po", [P, 2, 512], F32))
        N_CONST = 13

        consts_loaded, zeroed, ident0, made_const = sem("consts_loaded"), sem("zeroed"), sem("ident0"), sem("made_const")
        ctx_loaded = [sem(f"ctx_loaded{i}") for i in range(2)]
        x_loaded = [sem(f"x_loaded{i}") for i in range(2)]
        res_loaded = [sem(f"res_loaded{i}") for i in range(2)]
        w_loaded = [sem(f"w_loaded{i}") for i in range(2)]
        x1_stored = [sem(f"x1_stored{i}") for i in range(2)]
        scattered = [sem(f"scattered{i}") for i in range(2)]
        w_hi, w_lo = sem("w_hi"), sem("w_lo")
        k_made, k_kept, q_made, q_kept = sem("k_made"), sem("k_kept"), sem("q_made"), sem("q_kept")
        v_made, v_kept, s_made, s_shifted, exp_done = sem("v_made"), sem("v_kept"), sem("s_made"), sem("s_shifted"), sem("exp_done")
        pt_made, pt_kept, o_made, o_kept = sem("pt_made"), sem("pt_kept"), sem("o_made"), sem("o_kept")
        y_made, x1_ready, xn_ready, xn2_ready = sem("y_made"), sem("x1_ready"), sem("xn_ready"), sem("xn2_ready")
        xt_made, xt_kept, l_made, both_ready = sem("xt_made"), sem("xt_kept"), sem("l_made"), sem("both_ready")
        r_made, at_ready, count_made, pad_ready, padded = sem("r_made"), sem("at_ready"), sem("count_made"), sem("pad_ready"), sem("padded")
        norm_step, norm2_step, max_step, sum_step = sem("norm_step"), sem("norm2_step"), sem("max_step"), sem("sum_step")
        mv_ready, mv2_ready, rs_step, rs2_step, rs_ready, rs2_ready = (sem(n) for n in ("mv_ready", "mv2_ready", "rs_step", "rs2_step", "rs_ready", "rs2_ready"))
        choose_step, place_step, table_step = sem("choose_step"), sem("place_step"), sem("table_step")
        sp_tick, act_tick, pool_tick, pe_tick, dve_tick = (sem(e + "_tick") for e in ("sp", "act", "pool", "pe", "dve"))
        stack.callback(c.clear)
        block = stack.enter_context(nc.Block())

        x_v = a["x"].rearrange("(t b) s d -> t (b s) d", b=2)
        c_v = a["ctx"].rearrange("(t b) s d -> t (b s) d", b=2)
        w_v = a["W_e"].rearrange("e (k p) h -> p (e k) h", p=P)
        loaded_consts = [0]

        @block.sync
        def _(sp):
            def const(dst, src):
                sp.dma_start(dst, src).then_inc(consts_loaded, 16)
                loaded_consts[0] += 16

            sp.wait_ge(zeroed, 4)
            for buf, w in ((wk, "Wk"), (wv, "Wv"), (wq, "Wq"), (wo, "Wo")):
                for part in block_diagonal(buf):
                    const(part, a[w])
            for buf, b in ((bk, "bk"), (bq, "bq")):
                for half in range(2):
                    const(buf[:, half, :], a[b].partition_broadcast(P))
            for buf, b in ((bv, "bv"), (bo, "bo")):
                for half in range(2):
                    const(buf[64 * half:64 * half + 64, :], a[b].rearrange("(p a) -> p a", a=1))
            const(bg[:, :], a["b_gate"].partition_broadcast(P))
            const(wg[:, :, :], a["W_gate"].rearrange("(k p) e -> p k e", p=P))

            def load_ctx(t, p):
                after(sp, (v_made, t - 1), tick=sp_tick)
                sp.dma_start(ctx_in[:, p, :], c_v[t, :, :]).then_inc(ctx_loaded[p], 16)

            def load_x(t, p):
                after(sp, (xn_ready, t - 1), tick=sp_tick)
                sp.dma_start(x_in[:, p, :], x_v[t, :, :]).then_inc(x_loaded[p], 16)

            def load_weights(t, p):
                after(sp, (w_lo, t - 1), tick=sp_tick)
                sp.dma_start(wstage[:, p, :].rearrange("p (k h) -> p k h", k=2), w_v[:, bass.ds(2 * t, 2), :]).then_inc(w_loaded[p], 16)

            def load_residual(t, p):
                after(sp, (xn2_ready, t - 1), (x1_stored[p], slot_full(t, p) - 16), tick=sp_tick)
                sp.dma_start(x_res[:, p, :], x_v[t, :, :]).then_inc(res_loaded[p], 16)

            def store_x1(t, p):
                after(sp, (x1_ready, t + 1), tick=sp_tick)
                sp.dma_start(shared["x1"][t, :, :], x_res[:, p, :]).then_inc(x1_stored[p], 16)

            pipelined(sp, TILES, [(load_x, 0), (load_ctx, 1), (load_weights, 1), (store_x1, 5), (load_residual, 3)])
            sp.wait_ge(pad_ready, 1)
            for e in range(EXPERTS):
                row = sp.value_load(padi[0:1, e:e + 1], min_val=0, max_val=EXPERTS * REGION - P)
                sp.dma_start(shared["xs"][bass.ds(row, P), :], zero_rows[:, :]).then_inc(padded, 16)
            sp.wait_ge(padded, 16 * EXPERTS)
            for i in range(2):
                sp.wait_ge(x1_stored[i], 8 * TILES)

        @block.gpsimd
        def _(pool):
            for buf in (wk, wv, wq, wo):
                pool.memset(buf[:, :], 0.0).then_inc(zeroed, 1)
            pool.memset(v[:, :, :, LH:LH + 1], 1.0).then_inc(made_const, 1)
            pool.memset(zero_rows[:, :], 0.0).then_inc(made_const, 1)
            pool.memset(ones[:, :], 1.0).then_inc(made_const, 1)
            pool.memset(seenb[:, :], 0.0).then_inc(made_const, 1)
            pool.memset(seen[:, :], 0.0).then_inc(made_const, 1)
            for buf, pattern, base in ((from_last, [[-1, 8]], 8), (region_at, [[REGION, 8]], 0),
                                       (k128, [[0, 8], [P, 16]], 0), (blk, [[1, BLOCKS]], 0)):
                pool.iota(buf[:], pattern, base=base, channel_multiplier=0,
                          allow_small_or_imprecise_dtypes=True).then_inc(made_const, 1)
            pool.memset(minus_half[:, :], -0.5).then_inc(made_const, 1)
            pool.memset(ident[:, :], 0.0).then_inc(ident0, 1)
            pool.memset(before[:, :], 1.0).then_inc(ident0, 1)
            pool.memset(below[:, :, :], 1.0).then_inc(ident0, 1)
            pool.wait_ge(ident0, 3)
            pool.affine_select(out=ident[:, :], in_=ident[:, :], compare_op=ALU.not_equal, fill=1.0,
                               base=0, pattern=[[-1, P]], channel_multiplier=1).then_inc(made_const, 1)
            pool.affine_select(out=before[:, :], in_=before[:, :], compare_op=ALU.is_ge, fill=0.0,
                               base=-1, pattern=[[1, P]], channel_multiplier=-1).then_inc(made_const, 1)
            pool.affine_select(out=below[:, :, :], in_=below[:, :, :], compare_op=ALU.is_ge, fill=0.0,
                               base=-1, pattern=[[1, 8], [-1, 8]], channel_multiplier=0).then_inc(made_const, 1)

            def inverse_deviation(t, m, r, step, done):
                pool.tensor_scalar(m[:, 1:2], m[:, 1:2], EPS, None, ALU.add).then_inc(step, 1)
                after(pool, (step, 2 * t + 1), tick=pool_tick)
                pool.tensor_tensor(r[:, 0:1], m[:, 1:2], minus_half[:, :], ALU.pow).then_inc(step, 1)
                after(pool, (step, 2 * t + 2), tick=pool_tick)
                pool.tensor_scalar(r[:, 1:2], m[:, 0:1], -1.0, r[:, 0:1], ALU.mult, ALU.mult).then_inc(done, 1)

            def scale_x(t, p):
                after(pool, (mv_ready, t + 1), (xn_ready, t - 1), tick=pool_tick)
                inverse_deviation(t, mv[:, p, :], rstd[:, p, :], rs_step, rs_ready)

            def scale_x1(t, p):
                after(pool, (mv2_ready, t + 1), (xn2_ready, t - 1), tick=pool_tick)
                inverse_deviation(t, mv2[:, p, :], rstd2[:, p, :], rs2_step, rs2_ready)

            def low_part(t, p):
                after(pool, (w_hi, t + 1), tick=pool_tick)
                dst = bass.ds(1024 * t, 1024)
                pool.tensor_tensor(shared["w_lo"][:, dst], wstage[:, p, :], shared["w_hi"][:, dst].bitcast(F32), ALU.subtract).then_inc(w_lo, 1)

            def scatter(t, p):
                after(pool, (at_ready, t + 1), tick=pool_tick)
                for k in range(2):
                    pool.indirect_dma_start(out=shared["xs"], out_offset=bass.IndirectOffsetOnAxis(ap=ati[:, p, k:k + 1], axis=0),
                                            in_=xn2[:, p, :], in_offset=None).then_inc(scattered[p], 16)

            pipelined(pool, TILES, [(scale_x, 0), (scale_x1, 3), (scatter, 4), (low_part, 2)])
            for i in range(2):
                pool.wait_ge(scattered[i], 16 * TILES)

        @block.scalar
        def _(act):
            act.wait_ge(consts_loaded, loaded_consts[0])
            act.wait_ge(made_const, N_CONST)

            def keep_v(t, p):
                after(act, (v_made, t + 1), (o_made, t - 1), tick=act_tick)
                act.activation(v[:, p, :, 0:LH], pv[:, :].rearrange("p (h l) -> p h l", h=H0), ACT.Identity, bias=bv[:, 0:1]).then_inc(v_kept, 1)

            def norm_x(t, p):
                after(act, (rs_ready, t + 1), (q_made, t - 1), tick=act_tick)
                act.activation(xn[:, p, :], x_in[:, p, :], ACT.Identity, scale=rstd[:, p, 0:1], bias=rstd[:, p, 1:2]).then_inc(xn_ready, 1)

            def norm_x1(t, p):
                after(act, (rs2_ready, t + 1), (xt_made, t - 1), (scattered[p], 2 * slot_full(t, p) - 32), tick=act_tick)
                act.activation(xn2[:, p, :], x_res[:, p, :], ACT.Identity, scale=rstd2[:, p, 0:1], bias=rstd2[:, p, 1:2]).then_inc(xn2_ready, 1)

            def exponent(t, p):
                after(act, (s_shifted, t + 1), tick=act_tick)
                act.activation(score[:, p, :], score[:, p, :], ACT.Exp, scale=SCALE0).then_inc(exp_done, 1)

            def keep_probT(t, p):
                after(act, (pt_made, t + 1), (o_made, t - 1), tick=act_tick)
                act.activation(probT[:, p, :], pt[:, :], ACT.Copy).then_inc(pt_kept, 1)

            def keep_xT(t, p):
                after(act, (xt_made, t + 1), (l_made, t - 1), tick=act_tick)
                act.activation(xT[:, p, :], pt[:, :], ACT.Copy).then_inc(xt_kept, 1)

            def high_part(t, p):
                after(act, (w_loaded[p], slot_full(t, p)), tick=act_tick)
                act.activation(shared["w_hi"][:, bass.ds(1024 * t, 1024)], wstage[:, p, :], ACT.Copy).then_inc(w_hi, 1)

            pipelined(act, TILES, [(keep_v, 1), (keep_probT, 2), (norm_x1, 3), (exponent, 1), (norm_x, 0), (keep_xT, 3), (high_part, 1)])

        @block.tensor
        def _(pe):
            pe.wait_ge(consts_loaded, loaded_consts[0])
            pe.wait_ge(made_const, N_CONST)

            def make_k(t, p):
                after(pe, (ctx_loaded[p], slot_full(t, p)), (k_kept, t), tick=pe_tick)
                for j in range(4):
                    mm = pe.matmul(pk[:, P * j:P * j + P], ctx_in[:, p, P * j:P * j + P], wk[:, :], start=True, stop=True)
                mm.then_inc(k_made, 1)

            def make_v(t, p):
                after(pe, (v_kept, t), tick=pe_tick)
                pe.matmul(pv[:, :], wv[:, :], ctx_in[:, p, :], start=True, stop=True).then_inc(v_made, 1)

            def make_q(t, p):
                after(pe, (xn_ready, t + 1), (q_kept, t), tick=pe_tick)
                for j in range(4):
                    mm = pe.matmul(pq[:, P * j:P * j + P], xn[:, p, P * j:P * j + P], wq[:, :], start=True, stop=True)
                mm.then_inc(q_made, 1)

            def make_scores(t, p):
                after(pe, (q_kept, t + 1), (k_kept, t + 1), (s_shifted, t), tick=pe_tick)
                for j in range(4):
                    for b in range(2):
                        for r in range(2):
                            rows, cols = slice(64 * r, 64 * r + 64), slice(P * j + 64 * b, P * j + 64 * b + 64)
                            mm = pe.matmul(ps[rows, cols], qT[rows, p, cols], kT[rows, p, cols], start=True, stop=True)
                mm.then_inc(s_made, 1)

            def transpose_probs(t, p):
                after(pe, (exp_done, t + 1), (xt_kept, t - 1), tick=pe_tick)
                for j in range(4):
                    mm = pe.transpose(pt[:, P * j:P * j + P], score[:, p, P * j:P * j + P], ident[:, :])
                mm.then_inc(pt_made, 1)

            def make_attn(t, p):
                after(pe, (pt_kept, t + 1), (v_kept, t + 1), (o_kept, t), tick=pe_tick)
                for h in range(H0):
                    for b in range(2):
                        rows = slice(64 * b, 64 * b + 64)
                        mm = pe.matmul(po[rows, h // 4, 65 * (h % 4):65 * (h % 4) + 65], probT[rows, p, 64 * h:64 * h + 64],
                                       v[rows, p, h, :], start=True, stop=True)
                mm.then_inc(o_made, 1)

            def project(t, p):
                after(pe, (o_kept, t + 1), (both_ready, t), tick=pe_tick)
                pe.matmul(py[:, :], wo[:, :], attn[:, p, :], start=True, stop=True).then_inc(y_made, 1)

            def transpose_x(t, p):
                after(pe, (xn2_ready, t + 1), (pt_kept, upto(t + 2, TILES)), tick=pe_tick)
                for j in range(4):
                    mm = pe.transpose(pt[:, P * j:P * j + P], xn2[:, p, P * j:P * j + P], ident[:, :])
                mm.then_inc(xt_made, 1)

            def make_logits(t, p):
                after(pe, (xt_kept, t + 1), (at_ready, t), tick=pe_tick)
                for j in range(4):
                    mm = pe.matmul(py[:, 0:8], xT[:, p, P * j:P * j + P], wg[:, j, :], start=j == 0, stop=j == 3)
                mm.then_inc(l_made, 1)

            def make_rank(t, p):
                after(pe, (both_ready, t + 1), (at_ready, t), (x1_ready, upto(t + 2, TILES)), tick=pe_tick)
                pe.matmul(py[:, 0:8], before[:, :], both[:, p, :], start=True, stop=False)
                pe.matmul(py[:, 0:8], ones[:, :], seenb[:, :], start=False, stop=True).then_inc(r_made, 1)

            pipelined(pe, TILES, [(make_k, 1), (make_v, 1), (make_q, 1), (project, 3), (transpose_probs, 2),
                                  (make_scores, 1), (make_rank, 4), (transpose_x, 3), (make_attn, 2), (make_logits, 3)])
            pe.wait_ge(at_ready, TILES)
            pe.matmul(py[:, 0:8], ones[:, :], seenb[:, :], start=True, stop=True).then_inc(count_made, 1)

        @block.vector
        def _(dve):
            dve.wait_ge(consts_loaded, loaded_consts[0])
            dve.wait_ge(made_const, N_CONST)
            def statistics(t, x, st, m, step, done):
                dve.bn_stats(st, x).then_inc(step, 1)
                after(dve, (step, t + 1), tick=dve_tick)
                dve.bn_aggr(m, st).then_inc(done, 1)

            def norm_x(t, p):
                after(dve, (x_loaded[p], slot_full(t, p)), (rs_ready, t - 1), tick=dve_tick)
                statistics(t, x_in[:, p, :], stats[:, p, :], mv[:, p, :], norm_step, mv_ready)

            def by_chunk(ap):
                return ap.rearrange("p (j o) -> p j o", j=4)

            def keep_k(t, p):
                after(dve, (k_made, t + 1), (s_made, t - 1), tick=dve_tick)
                dve.tensor_tensor(by_chunk(kT[:, p, :]), by_chunk(pk[:, :]), bk4, ALU.add).then_inc(k_kept, 1)

            def keep_q(t, p):
                after(dve, (q_made, t + 1), (s_made, t - 1), tick=dve_tick)
                dve.tensor_tensor(by_chunk(qT[:, p, :]), by_chunk(pq[:, :]), bq4, ALU.add).then_inc(q_kept, 1)

            bk4, bq4 = (b[:, :, :].rearrange("p (x a) o -> p x (a o)", x=1).to_broadcast([P, 4, P]) for b in (bk, bq))

            def shift_scores(t, p):
                after(dve, (s_made, t + 1), tick=dve_tick)
                rows = ps[:, :].rearrange("p (g e) -> p g e", g=8)
                dve.tensor_reduce(smax[:, p, :], rows, AX.X, ALU.max).then_inc(max_step, 1)
                after(dve, (pt_made, t - 1), (max_step, t + 1), tick=dve_tick)
                peak = smax[:, p, :].rearrange("p (g x) -> p g x", x=1).to_broadcast([P, 8, 64])
                dve.tensor_tensor(score[:, p, :].rearrange("p (g e) -> p g e", g=8), rows, peak, ALU.subtract).then_inc(s_shifted, 1)

            def keep_attn(t, p):
                after(dve, (o_made, t + 1), tick=dve_tick)
                heads = po[:, :, 0:260].rearrange("p b (h l) -> p b h l", h=4)
                dve.reciprocal(rsum[:, p, :, :], heads[:, :, :, 64:65]).then_inc(sum_step, 1)
                after(dve, (y_made, t - 1), (sum_step, t + 1), tick=dve_tick)
                dve.tensor_tensor(attn[:, p, :].rearrange("p (b h l) -> p b h l", b=2, h=4), heads[:, :, :, 0:64],
                                  rsum[:, p, :, :].to_broadcast([P, 2, 4, 64]), ALU.mult).then_inc(o_kept, 1)

            def add_residual(t, p):
                after(dve, (y_made, t + 1), (res_loaded[p], slot_full(t, p)), tick=dve_tick)
                dve.scalar_tensor_tensor(x_res[:, p, :], py[:, :], bo[:, 0:1], x_res[:, p, :], ALU.add, ALU.add).then_inc(x1_ready, 1)
                after(dve, (x1_ready, t + 1), (rs2_ready, t - 1), tick=dve_tick)
                statistics(t, x_res[:, p, :], stats2[:, p, :], mv2[:, p, :], norm2_step, mv2_ready)

            def choose(t, p):
                after(dve, (l_made, t + 1), tick=dve_tick)
                base = t * CHOOSE_STEPS
                dve.tensor_tensor(logit[:, p, :], py[:, 0:8], bg[:, :], ALU.add).then_inc(choose_step, 1)
                for k in range(2):
                    after(dve, (choose_step, base + 5 * k + 1), tick=dve_tick)
                    dve.tensor_reduce(peak8[:, p, 0:1], logit[:, p, :], AX.X, ALU.max).then_inc(choose_step, 1)
                    after(dve, (choose_step, base + 5 * k + 2), tick=dve_tick)
                    dve.scalar_tensor_tensor(turn[:, p, :], logit[:, p, :], peak8[:, p, 0:1], from_last[:, :], ALU.is_ge, ALU.mult).then_inc(choose_step, 1)
                    after(dve, (choose_step, base + 5 * k + 3), tick=dve_tick)
                    dve.tensor_reduce(peak8[:, p, 1:2], turn[:, p, :], AX.X, ALU.max).then_inc(choose_step, 1)
                    after(dve, (choose_step, base + 5 * k + 4), tick=dve_tick)
                    dve.tensor_scalar(hot_kept[:, t, k, :], from_last[:, :], peak8[:, p, 1:2], None, ALU.is_equal).then_inc(choose_step, 1)
                    after(dve, (choose_step, base + 5 * k + 5), tick=dve_tick)
                    if k == 0:
                        dve.scalar_tensor_tensor(logit[:, p, :], hot_kept[:, t, 0, :], -3.0e38, logit[:, p, :], ALU.mult, ALU.add).then_inc(choose_step, 1)
                dve.tensor_tensor(both[:, p, :], hot_kept[:, t, 0, :], hot_kept[:, t, 1, :], ALU.add).then_inc(both_ready, 1)

            def place(t, p):
                after(dve, (r_made, t + 1), tick=dve_tick)
                base = t * PLACE_STEPS
                dve.tensor_tensor(rank[:, p, :], py[:, 0:8], region_at[:, :], ALU.add).then_inc(place_step, 1)
                dve.tensor_tensor(seen[:, :], seen[:, :], both[:, p, :], ALU.add).then_inc(place_step, 1)
                after(dve, (place_step, base + 2), tick=dve_tick)
                dve.tensor_copy(seenb[:, :], seen[:, :]).then_inc(place_step, 1)
                dve.tensor_tensor(picked[:, p, :, :], hot_kept[:, t, :, :], rank[:, p, :].rearrange("p (x e) -> p x e", x=1).to_broadcast([P, 2, 8]), ALU.mult).then_inc(place_step, 1)
                after(dve, (place_step, base + 4), tick=dve_tick)
                dve.tensor_reduce(at_kept[:, t, :], picked[:, p, :, :], AX.X, ALU.add).then_inc(place_step, 1)
                after(dve, (place_step, base + 5), (scattered[p], 2 * slot_full(t, p) - 32), tick=dve_tick)
                dve.tensor_copy(ati[:, p, :], at_kept[:, t, :]).then_inc(at_ready, 1)

            CHOOSE_STEPS, PLACE_STEPS = 10, 5
            pipelined(dve, TILES, [(keep_k, 1), (keep_q, 1), (choose, 4), (add_residual, 3), (norm_x, 0),
                                   (shift_scores, 1), (place, 4), (keep_attn, 2)])

            steps = [0]

            def then(ins):
                steps[0] += 1
                ins.then_inc(table_step, 1)
                dve.wait_ge(table_step, steps[0])

            def spread(ap, rows):
                return ap.rearrange("p (x e) -> p x e", x=1).to_broadcast([P, rows, 8])

            def each(ap, n):
                return ap.rearrange("p (e x) -> p e x", x=1).to_broadcast([P, ap.shape[1], n])

            dve.wait_ge(count_made, 1)
            then(dve.tensor_copy(counts[:, :], py[:, 0:8]))
            then(dve.tensor_tensor(padf[:, :], counts[:, :], region_at[:, :], ALU.add))
            dve.tensor_copy(padi[:, :], padf[:, :]).then_inc(pad_ready, 1)
            then(dve.tensor_tensor(over[:, :, :], each(counts[:, :], 16), k128[:, :, :], ALU.is_gt))
            then(dve.tensor_reduce(nblk[:, :], over[:, :, :], AX.X, ALU.add))
            then(dve.tensor_tensor(lower[:, :, :], below[:, :, :], spread(nblk[:, :], 8), ALU.mult))
            then(dve.tensor_reduce(start[:, :], lower[:, :, :], AX.X, ALU.add))
            then(dve.tensor_tensor(end[:, :], start[:, :], nblk[:, :], ALU.add))
            then(dve.tensor_scalar(shared["last"][:, :], end[:, 7:8], -1.0, None, ALU.add))
            then(dve.tensor_scalar(blk[:, :], blk[:, :], shared["last"][:, 0:1], None, ALU.min))
            then(dve.tensor_tensor(passed[:, :, :], each(blk[:, :], 8), spread(end[:, :], BLOCKS), ALU.is_ge))
            then(dve.tensor_reduce(bexp[:, :], passed[:, :, :], AX.X, ALU.add))
            then(dve.tensor_tensor(passed[:, :, :], passed[:, :, :], spread(nblk[:, :], BLOCKS), ALU.mult))
            then(dve.tensor_reduce(bstart[:, :], passed[:, :, :], AX.X, ALU.add))
            then(dve.tensor_tensor(bstart[:, :], blk[:, :], bstart[:, :], ALU.subtract))
            then(dve.tensor_scalar(bstart[:, :], bstart[:, :], float(P), None, ALU.mult))
            then(dve.scalar_tensor_tensor(table[:, 0, :], bexp[:, :], float(REGION), bstart[:, :], ALU.mult, ALU.add))
            then(dve.tensor_scalar(table[:, 1, :], bexp[:, :], float(DIM), None, ALU.mult))
            then(dve.tensor_copy(shared["table"][:, :, :], table[:, :, :]))
            then(dve.scalar_tensor_tensor(shift[:, :], start[:, :], float(P), region_at[:, :], ALU.mult, ALU.subtract))
            then(dve.tensor_tensor(moved[:, :, :], hot_kept[:, :, :, :].rearrange("p t k e -> p (t k) e"), spread(shift[:, :], 2 * TILES), ALU.mult))
            then(dve.tensor_reduce(at_kept2[:, :], moved[:, :, :], AX.X, ALU.add))
            then(dve.tensor_tensor(at_kept2[:, :], at_kept2[:, :], at_kept[:, :, :].rearrange("p t k -> p (t k)"), ALU.add))
            then(dve.tensor_copy(shared["y_at"][:, :], at_kept2[:, :]))


def identity(pool, buf, zeroed, made):
    pool.memset(buf[:, :], 0.0).then_inc(zeroed, 1)
    pool.wait_ge(zeroed, 1)
    pool.affine_select(out=buf[:, :], in_=buf[:, :], compare_op=ALU.not_equal, fill=1.0,
                       base=0, pattern=[[-1, P]], channel_multiplier=1).then_inc(made, 1)


def expert_phase(nc, shared, b_e):
    with ExitStack() as stack:
        c = Ctx(nc, stack, "b_")
        sb, pb, sem = c.sb, c.pb, c.sem
        bias, ident = sb("bias", [P, EXPERTS * DIM]), sb("ident", [P, P])
        rows, biased, result = sb("rows", [P, 2, DIM]), sb("biased", [P, 2, DIM]), sb("result", [P, 2, DIM])
        rowsT_hi, rowsT_lo = sb("rowsT_hi", [P, 2, DIM], F32R), sb("rowsT_lo", [P, 2, DIM], F32R)
        pt, py = [pb(f"pt{i}") for i in range(2)], [pb(f"py{i}") for i in range(2)]
        bias_loaded, zeroed, ident_made = sem("bias_loaded"), sem("zeroed"), sem("ident_made")
        rows_loaded, stored = [sem(f"rows_loaded{i}") for i in range(2)], [sem(f"stored{i}") for i in range(2)]
        t_made, hi_kept, lo_kept, y_made = sem("t_made"), sem("hi_kept"), sem("lo_kept"), sem("y_made")
        biased_made, result_made = sem("biased_made"), sem("result_made")
        sp_tick, act_tick, pe_tick, dve_tick = (sem(e + "_tick") for e in ("sp", "act", "pe", "dve"))
        w_hi, w_lo, table = shared["w_hi"], shared["w_lo"], shared["table"]
        y_v = shared["ys"].rearrange("(b p) h -> b p h", p=P)
        stack.callback(c.clear)
        block = stack.enter_context(nc.Block())

        @block.sync
        def _(sp):
            def load(b, p):
                row = sp.value_load(table[0:1, 0, bass.ds(b, 1)], min_val=0, max_val=EXPERTS * REGION - P)
                after(sp, (t_made, b - 1), tick=sp_tick)
                sp.dma_start(rows[:, p, :], shared["xs"][bass.ds(row, P), :]).then_inc(rows_loaded[p], 16)
                if isinstance(b, int) and b == 1:
                    sp.dma_start(bias[:, :], b_e.rearrange("e h -> (e h)").partition_broadcast(P)).then_inc(bias_loaded, 16)

            def store(b, p):
                after(sp, (result_made, b + 1), tick=sp_tick)
                sp.dma_start(y_v[b, :, :], result[:, p, :]).then_inc(stored[p], 16)

            pipelined(sp, BLOCKS, [(load, 0), (store, 3)])
            for i in range(2):
                sp.wait_ge(stored[i], 16 * ((BLOCKS + 1 - i) // 2))

        @block.gpsimd
        def _(pool):
            identity(pool, ident, zeroed, ident_made)

        @block.tensor
        def _(pe):
            pe.wait_ge(ident_made, 1)

            def transpose_rows(b, p):
                after(pe, (rows_loaded[p], slot_full(b, p)), (lo_kept, b - 1), tick=pe_tick)
                for k in range(KD):
                    mm = pe.transpose(pt[p][:, P * k:P * k + P], rows[:, p, P * k:P * k + P], ident[:, :])
                mm.then_inc(t_made, 1)

            def multiply(b, p):
                at = pe.value_load(table[0:1, 1, bass.ds(b, 1)], min_val=0, max_val=(EXPERTS - 1) * DIM)
                after(pe, (hi_kept, b + 1), (lo_kept, b + 1), (biased_made, b - 1), tick=pe_tick)
                for k in range(KD):
                    hi, lo = rowsT_hi[:, p, P * k:P * k + P], rowsT_lo[:, p, P * k:P * k + P]
                    cols = bass.ds(at * KD + k * DIM, DIM)
                    pe.matmul(py[p][:, :], hi, w_hi[:, cols], start=k == 0, stop=False)
                    pe.matmul(py[p][:, :], hi, w_lo[:, cols], start=False, stop=False)
                    mm = pe.matmul(py[p][:, :], lo, w_hi[:, cols], start=False, stop=k == KD - 1)
                mm.then_inc(y_made, 1)

            pipelined(pe, BLOCKS, [(transpose_rows, 0), (multiply, 1)])

        @block.scalar
        def _(act):
            def keep_high(b, p):
                after(act, (t_made, b + 1), (y_made, b - 1), tick=act_tick)
                act.activation(rowsT_hi[:, p, :], pt[p][:, :], ACT.Copy).then_inc(hi_kept, 1)

            def rectify(b, p):
                after(act, (biased_made, b + 1), (stored[p], slot_full(b, p) - 16), tick=act_tick)
                act.activation(result[:, p, :], biased[:, p, :], ACT.Relu, scale=0.5).then_inc(result_made, 1)

            pipelined(act, BLOCKS, [(keep_high, 0), (rectify, 1)])

        @block.vector
        def _(dve):
            dve.wait_ge(bias_loaded, 16)

            def keep_low(b, p):
                after(dve, (hi_kept, b + 1), (y_made, b - 1), tick=dve_tick)
                dve.tensor_tensor(rowsT_lo[:, p, :], pt[p][:, :], rowsT_hi[:, p, :].bitcast(F32), ALU.subtract).then_inc(lo_kept, 1)

            def add_bias(b, p):
                at = dve.value_load(table[0:1, 1, bass.ds(b, 1)], min_val=0, max_val=(EXPERTS - 1) * DIM)
                after(dve, (y_made, b + 1), (result_made, b - 1), tick=dve_tick)
                dve.tensor_tensor(biased[:, p, :], py[p][:, :], bias[:, bass.ds(at, DIM)], ALU.add).then_inc(biased_made, 1)

            pipelined(dve, BLOCKS, [(keep_low, 0), (add_bias, 1)])


GUC = 2 * KD * INTER // TILES


def layer1_phase(nc, shared, a):
    with ExitStack() as stack:
        c = Ctx(nc, stack, "c_")
        sb, pb, sem = c.sb, c.pb, c.sem
        proj_hi, proj_lo = sb("proj_hi", [P, 2, KD * DIM], F32R), sb("proj_lo", [P, 2, KD * DIM], F32R)
        wk, wv = sb("wk", [P, KD, P]), sb("wv", [P, KD, P])
        ident, minus_half, own_head = sb("ident", [P, P]), sb("minus_half", [P, 1]), sb("own_head", [P, KVH])
        stage = sb("stage", [P, 2, 1024])
        x_in, x_out, xn, qT, attn, ctxT = (sb(n, [P, 2, DIM]) for n in ("x_in", "x_out", "xn", "qT", "attn", "ctxT"))
        y_in, y_at = sb("y_in", [P, 2, 2, DIM]), sb("y_at", [P, 2, 2], I32)
        xT_hi, xT_lo, aT_hi, aT_lo = (sb(n, [P, 2, DIM], F32R) for n in ("xT_hi", "xT_lo", "aT_hi", "aT_lo"))
        kT, keys, values = sb("kT", [P, 2, P]), sb("keys", [P, 2, 2, DIM]), sb("values", [P, 2, 2, 4, 2, HD + 1])
        score, probT = sb("score", [P, 2, DIM]), sb("probT", [P, 2, DIM])
        smax, rsum = sb("smax", [P, 2, KVH]), sb("rsum", [P, 2, 2, KVH, 1])
        stats, mv, rstd = sb("stats", [P, 2, 6]), sb("mv", [P, 2, 2]), sb("rstd", [P, 2, 2])
        n_out, stats3, mv3, rstd3 = sb("n_out", [P, 2, DIM]), sb("stats3", [P, 2, 6]), sb("mv3", [P, 2, 2]), sb("rstd3", [P, 2, 2])
        ps, pt, po = ([pb(f"{n}{i}") for i in range(2)] for n in ("ps", "pt", "po"))
        pg, ph = pb("pg"), pb("ph")

        names = ("zeroed const_made weights_loaded proj_hi_made proj_lo_made gu_hi gu_lo x2_added x2_ready stat_step mv_ready rs_step "
                 "rs_ready xn_ready xt_made xhi_kept xlo_kept q_made q_kept kv_made kt_kept v_kept keys_ready s_made max_step "
                 "s_shifted exp_done pt_made pt_kept o_made sum_step o_kept at_made ahi_kept alo_kept w_made x3_ready yat_ready")
        (zeroed, const_made, weights_loaded, proj_hi_made, proj_lo_made, gu_hi, gu_lo, x2_added, x2_ready, stat_step, mv_ready, rs_step,
         rs_ready, xn_ready, xt_made, xhi_kept, xlo_kept, q_made, q_kept, kv_made, kt_kept, v_kept, keys_ready, s_made, max_step,
         s_shifted, exp_done, pt_made, pt_kept, o_made, sum_step, o_kept, at_made, ahi_kept, alo_kept, w_made, x3_ready,
         yat_ready) = (sem(n) for n in names.split())
        stat3_step, mv3_ready, rs3_step, rs3_ready, n_ready = (sem(n) for n in ("stat3_step", "mv3_ready", "rs3_step", "rs3_ready", "n_ready"))
        n_stored = [sem(f"n_stored{i}") for i in range(2)]
        proj_loaded = [sem(f"proj_loaded{i}") for i in range(4)]
        x1_loaded, ctx_loaded, y_loaded, gu_loaded, x2_stored, x2_loaded, x3_stored = (
            [sem(f"{n}{i}") for i in range(2)] for n in ("x1_loaded", "ctx_loaded", "y_loaded", "gu_loaded", "x2_stored", "x2_loaded", "x3_stored"))
        sp_tick, act_tick, pool_tick, pe_tick, dve_tick = (sem(e + "_tick") for e in ("sp", "act", "pool", "pe", "dve"))
        N_CONST = 6
        stack.callback(c.clear)
        block = stack.enter_context(nc.Block())
        wq_v = a["Wq"].rearrange("(k p) n -> p k n", p=P)
        wo_v = a["Wo"].rearrange("(k p) n -> p k n", p=P)

        @block.sync
        def _(sp):
            for n in range(4):
                if n >= 2:
                    sp.wait_ge(proj_lo_made, n - 1)
                src = (wq_v, wo_v)[n // 2][:, 2 * (n % 2):2 * (n % 2) + 2, :]
                sp.dma_start(stage[:, n % 2, :].rearrange("p (k n) -> p k n", k=2), src).then_inc(proj_loaded[n], 16)
                if n == 1:
                    sp.dma_start(wk[:, :, :], a["Wk"].rearrange("(k p) n -> p k n", p=P)).then_inc(weights_loaded, 16)
                    sp.dma_start(wv[:, :, :], a["Wv"].rearrange("(k p) n -> p k n", p=P)).then_inc(weights_loaded, 16)

            def load_x1(t, p):
                after(sp, (xn_ready, t - 1), (x2_stored[p], slot_full(t, p) - 16), tick=sp_tick)
                sp.dma_start(x_in[:, p, :], shared["x1"][t, :, :]).then_inc(x1_loaded[p], 16)

            def load_ctx(t, p):
                after(sp, (kv_made, t - 1), tick=sp_tick)
                sp.dma_start(ctxT[:, p, :], a["ctxT"][t, :, :]).then_inc(ctx_loaded[p], 16)

            def load_gate_up(t, p):
                after(sp, (gu_lo, t - 1), tick=sp_tick)
                if isinstance(t, int) and t < 2:
                    sp.wait_ge(proj_lo_made, 3 + t)
                sp.dma_start(stage[:, p, 0:GUC], a["gate_up"][t, :, :]).then_inc(gu_loaded[p], 16)

            def store_x2(t, p):
                after(sp, (x2_ready, t + 1), tick=sp_tick)
                sp.dma_start(shared["x2"][t, :, :], x_in[:, p, :]).then_inc(x2_stored[p], 16)

            def load_x2(t, p):
                after(sp, (x2_stored[p], slot_full(t, p)), (x3_stored[p], slot_full(t, p) - 16), (n_ready, t - 1), tick=sp_tick)
                sp.dma_start(x_out[:, p, :], shared["x2"][t, :, :]).then_inc(x2_loaded[p], 16)

            def store_x3(t, p):
                after(sp, (x3_ready, t + 1), tick=sp_tick)
                sp.dma_start(shared["x3"][t, :, :], x_out[:, p, :]).then_inc(x3_stored[p], 16)

            def store_norm(t, p):
                after(sp, (n_ready, t + 1), tick=sp_tick)
                sp.dma_start(shared["n3"][t, :, :], n_out[:, p, :]).then_inc(n_stored[p], 16)

            pipelined(sp, TILES, [(load_ctx, 1), (load_gate_up, 1), (store_x2, 2), (load_x1, 0), (store_x3, 5), (store_norm, 5), (load_x2, 3)])
            for i in range(2):
                sp.wait_ge(n_stored[i], 8 * TILES)
                sp.wait_ge(x3_stored[i], 8 * TILES)

        @block.gpsimd
        def _(pool):
            pool.memset(keys[:], 0.0).then_inc(const_made, 1)
            pool.memset(minus_half[:, :], -0.5).then_inc(const_made, 1)
            pool.memset(values[:], 0.0).then_inc(zeroed, 1)
            pool.memset(ident[:, :], 0.0).then_inc(zeroed, 1)
            pool.memset(own_head[:, :], 1.0).then_inc(zeroed, 1)
            pool.wait_ge(zeroed, 3)
            for r in range(2):
                pool.memset(values[64 * r:64 * r + 64, :, :, :, r, HD:HD + 1], 1.0).then_inc(const_made, 1)
                pool.wait_ge(const_made, 3 + r)
            pool.affine_select(out=ident[:, :], in_=ident[:, :], compare_op=ALU.not_equal, fill=1.0,
                               base=0, pattern=[[-1, P]], channel_multiplier=1).then_inc(const_made, 1)
            pool.affine_select(out=own_head[:, :], in_=own_head[:, :], compare_op=ALU.is_ge, fill=0.0,
                               base=0, pattern=[[-HD, KVH]], channel_multiplier=1).then_inc(zeroed, 1)
            pool.wait_ge(zeroed, 4)
            pool.affine_select(out=own_head[:, :], in_=own_head[:, :], compare_op=ALU.is_ge, fill=0.0,
                               base=HD - 1, pattern=[[HD, KVH]], channel_multiplier=-1).then_inc(const_made, 1)
            pool.wait_ge(const_made, N_CONST)

            def gather(t, p):
                after(pool, (x2_ready, t - 1), (y_loaded[p], 2 * slot_full(t, p) - 32), tick=pool_tick)
                pool.tensor_copy(y_at[:, p, :], shared["y_at"][:, bass.ds(2 * t, 2)]).then_inc(yat_ready, 1)
                after(pool, (yat_ready, t + 1), tick=pool_tick)
                for k in range(2):
                    pool.indirect_dma_start(out=y_in[:, p, k, :], out_offset=None, in_=shared["ys"],
                                            in_offset=bass.IndirectOffsetOnAxis(ap=y_at[:, p, k:k + 1], axis=0)).then_inc(y_loaded[p], 16)

            def add_first(t, p):
                after(pool, (x1_loaded[p], slot_full(t, p)), (y_loaded[p], 2 * slot_full(t, p)), tick=pool_tick)
                pool.tensor_tensor(x_in[:, p, :], x_in[:, p, :], y_in[:, p, 0, :], ALU.add).then_inc(x2_added, 1)

            def inverse_deviation(t, m, r, step, done):
                pool.tensor_scalar(m[:, 1:2], m[:, 1:2], EPS, None, ALU.add).then_inc(step, 1)
                after(pool, (step, 2 * t + 1), tick=pool_tick)
                pool.tensor_tensor(r[:, 0:1], m[:, 1:2], minus_half[:, :], ALU.pow).then_inc(step, 1)
                after(pool, (step, 2 * t + 2), tick=pool_tick)
                pool.tensor_scalar(r[:, 1:2], m[:, 0:1], -1.0, r[:, 0:1], ALU.mult, ALU.mult).then_inc(done, 1)

            def scale_x2(t, p):
                after(pool, (mv_ready, t + 1), (xn_ready, t - 1), tick=pool_tick)
                inverse_deviation(t, mv[:, p, :], rstd[:, p, :], rs_step, rs_ready)

            def scale_x3(t, p):
                after(pool, (mv3_ready, t + 1), (n_ready, t - 1), tick=pool_tick)
                inverse_deviation(t, mv3[:, p, :], rstd3[:, p, :], rs3_step, rs3_ready)

            def spread_keys(t, p):
                after(pool, (kt_kept, t + 1), (s_made, 4 * t - 4), tick=pool_tick)
                for b in range(2):
                    pool.tensor_tensor(keys[:, p, b, :].rearrange("p (h e) -> p h e", h=KVH),
                                       kT[:, p, 64 * b:64 * b + 64].rearrange("p (x e) -> p x e", x=1).to_broadcast([P, KVH, 64]),
                                       own_head[:, :].rearrange("p (h x) -> p h x", x=1).to_broadcast([P, KVH, 64]), ALU.mult).then_inc(keys_ready, 1)

            def low_part(t, p):
                after(pool, (gu_hi, t + 1), tick=pool_tick)
                dst = bass.ds(GUC * t, GUC)
                pool.tensor_tensor(shared["gu_lo"][:, dst], stage[:, p, 0:GUC], shared["gu_hi"][:, dst].bitcast(F32), ALU.subtract).then_inc(gu_lo, 1)

            pipelined(pool, TILES, [(gather, 0), (add_first, 1), (low_part, 2), (scale_x2, 1), (scale_x3, 4), (spread_keys, 2)])

        @block.scalar
        def _(act):
            for n in range(4):
                act.wait_ge(proj_loaded[n], 16)
                act.activation(proj_hi[:, n // 2, 1024 * (n % 2):1024 * (n % 2) + 1024], stage[:, n % 2, :], ACT.Copy).then_inc(proj_hi_made, 1)

            def keep_kT(t, p):
                after(act, (kv_made, t + 1), (keys_ready, 2 * t - 2), tick=act_tick)
                act.activation(kT[:, p, :], pg[:, 0:P], ACT.Copy).then_inc(kt_kept, 1)

            def norm_x(t, p):
                after(act, (rs_ready, t + 1), (xt_made, t - 1), tick=act_tick)
                act.activation(xn[:, p, :], x_in[:, p, :], ACT.Identity, scale=rstd[:, p, 0:1], bias=rstd[:, p, 1:2]).then_inc(xn_ready, 1)

            def norm_x3(t, p):
                after(act, (rs3_ready, t + 1), (n_stored[p], slot_full(t, p) - 16), tick=act_tick)
                act.activation(n_out[:, p, :], x_out[:, p, :], ACT.Identity, scale=rstd3[:, p, 0:1], bias=rstd3[:, p, 1:2]).then_inc(n_ready, 1)

            def keep_high_x(t, p):
                after(act, (xt_made, t + 1), (q_made, t - 1), tick=act_tick)
                act.activation(xT_hi[:, p, :], pg[:, :], ACT.Copy).then_inc(xhi_kept, 1)

            def keep_q(t, p):
                after(act, (q_made, t + 1), (s_made, 4 * t - 4), tick=act_tick)
                act.activation(qT[:, p, :].rearrange("p (b g q) -> p g b q", b=2, g=GROUP),
                               ph[:, :].rearrange("p (g b q) -> p g b q", g=GROUP, b=2), ACT.Copy).then_inc(q_kept, 1)

            def exponent(i):
                def stage_(t, p):
                    after(act, (s_shifted, 4 * t + i + 1), tick=act_tick)
                    act.activation(score[:, i % 2, :], score[:, i % 2, :], ACT.Exp, scale=SCALE1).then_inc(exp_done, 1)
                return stage_

            def keep_probT(i):
                def stage_(t, p):
                    after(act, (pt_made, 4 * t + i + 1), (o_made, 4 * t + i - 1), tick=act_tick)
                    act.activation(probT[:, i % 2, :], pt[i % 2][:, :], ACT.Copy).then_inc(pt_kept, 1)
                return stage_

            def keep_high_attn(t, p):
                after(act, (at_made, t + 1), (w_made, t - 1), tick=act_tick)
                act.activation(aT_hi[:, p, :].rearrange("p (g b q) -> p b g q", g=GROUP, b=2),
                               pg[:, :].rearrange("p (b g q) -> p b g q", b=2, g=GROUP), ACT.Copy).then_inc(ahi_kept, 1)

            def high_part(t, p):
                after(act, (gu_loaded[p], slot_full(t, p)), tick=act_tick)
                act.activation(shared["gu_hi"][:, bass.ds(GUC * t, GUC)], stage[:, p, 0:GUC], ACT.Copy).then_inc(gu_hi, 1)

            pipelined(act, TILES, [(exponent(0), 3), (exponent(1), 3), (keep_high_attn, 4), (keep_probT(0), 3), (exponent(2), 3),
                                   (keep_probT(1), 3), (exponent(3), 3), (keep_kT, 2), (norm_x, 1), (keep_high_x, 2),
                                   (keep_probT(2), 3), (norm_x3, 4), (keep_probT(3), 3), (keep_q, 2), (high_part, 1)])

        @block.tensor
        def _(pe):
            pe.wait_ge(const_made, N_CONST)
            pe.wait_ge(weights_loaded, 32)
            pe.wait_ge(proj_lo_made, 4)

            def transpose_x(t, p):
                after(pe, (xn_ready, t + 1), (kt_kept, t + 1), (v_kept, 4 * t + 4), tick=pe_tick)
                for k in range(KD):
                    mm = pe.transpose(pg[:, P * k:P * k + P], xn[:, p, P * k:P * k + P], ident[:, :])
                mm.then_inc(xt_made, 1)

            def make_q(t, p):
                after(pe, (xhi_kept, t + 1), (xlo_kept, t + 1), (x3_ready, t - 1), tick=pe_tick)
                for g in range(GROUP):
                    out = ph[:, P * g:P * g + P]
                    for k in range(KD):
                        cols, xs = slice(DIM * k + P * g, DIM * k + P * g + P), slice(P * k, P * k + P)
                        pe.matmul(out, proj_hi[:, 0, cols], xT_hi[:, p, xs], start=k == 0, stop=False)
                        pe.matmul(out, proj_hi[:, 0, cols], xT_lo[:, p, xs], start=False, stop=False)
                        mm = pe.matmul(out, proj_lo[:, 0, cols], xT_hi[:, p, xs], start=False, stop=k == KD - 1)
                mm.then_inc(q_made, 1)

            def make_kv(t, p):
                after(pe, (ctx_loaded[p], slot_full(t, p)), (alo_kept, t - 1), tick=pe_tick)
                rows = ctxT[:, p, :].rearrange("p (k n) -> p k n", k=KD)
                for k in range(KD):
                    pe.matmul(pg[:, 0:P], wk[:, k, :], rows[:, k, :], start=k == 0, stop=k == KD - 1)
                for k in range(KD):
                    mm = pe.matmul(pg[:, P:2 * P], rows[:, k, :], wv[:, k, :], start=k == 0, stop=k == KD - 1)
                mm.then_inc(kv_made, 1)

            def scores(i):
                def stage_(t, p):
                    after(pe, (q_kept, t + 1), (keys_ready, 2 * t + 2), (s_shifted, 4 * t + i - 1), tick=pe_tick)
                    pe.matmul(ps[i % 2][:, :], qT[:, p, P * i:P * i + P], keys[:, p, i // 2, :], start=True, stop=True).then_inc(s_made, 1)
                return stage_

            def transpose_probs(i):
                def stage_(t, p):
                    after(pe, (exp_done, 4 * t + i + 1), (pt_kept, 4 * t + i - 1), tick=pe_tick)
                    for j in range(4):
                        mm = pe.transpose(pt[i % 2][:, P * j:P * j + P], score[:, i % 2, P * j:P * j + P], ident[:, :])
                    mm.then_inc(pt_made, 1)
                return stage_

            def attend(i):
                def stage_(t, p):
                    b = i // 2
                    after(pe, (pt_kept, 4 * t + i + 1), (o_kept, 2 * t + b - 1), tick=pe_tick)
                    for j in range(4):
                        at = 136 * (i % 2) + 34 * j
                        mm = pe.matmul(po[b][:, at:at + 34], probT[:, i % 2, P * j:P * j + P],
                                       values[:, p, b, j, :, :].rearrange("p r d -> p (r d)"), start=True, stop=True)
                    mm.then_inc(o_made, 1)
                return stage_

            def transpose_attn(t, p):
                after(pe, (o_kept, 2 * t + 2), (xlo_kept, upto(t + 2, TILES)), tick=pe_tick)
                for i in range(4):
                    mm = pe.transpose(pg[:, P * i:P * i + P], attn[:, p, P * i:P * i + P], ident[:, :])
                mm.then_inc(at_made, 1)

            def project(t, p):
                after(pe, (ahi_kept, t + 1), (alo_kept, t + 1), (q_kept, upto(t + 2, TILES)), tick=pe_tick)
                for g in range(GROUP):
                    hi, lo = aT_hi[:, p, P * g:P * g + P], aT_lo[:, p, P * g:P * g + P]
                    cols = slice(DIM * g, DIM * g + DIM)
                    pe.matmul(ph[:, :], hi, proj_hi[:, 1, cols], start=g == 0, stop=False)
                    pe.matmul(ph[:, :], hi, proj_lo[:, 1, cols], start=False, stop=False)
                    mm = pe.matmul(ph[:, :], lo, proj_hi[:, 1, cols], start=False, stop=g == GROUP - 1)
                mm.then_inc(w_made, 1)

            pipelined(pe, TILES, [(scores(0), 3), (scores(1), 3), (transpose_attn, 4), (transpose_probs(0), 3), (scores(2), 3),
                                  (transpose_probs(1), 3), (scores(3), 3), (project, 4), (make_kv, 2), (attend(0), 3), (attend(1), 3),
                                  (transpose_x, 2), (transpose_probs(2), 3), (transpose_probs(3), 3), (make_q, 2), (attend(2), 3), (attend(3), 3)])

        @block.vector
        def _(dve):
            dve.wait_ge(const_made, N_CONST)
            for n in range(4):
                dve.wait_ge(proj_hi_made, n + 1)
                cols = slice(1024 * (n % 2), 1024 * (n % 2) + 1024)
                dve.tensor_tensor(proj_lo[:, n // 2, cols], stage[:, n % 2, :], proj_hi[:, n // 2, cols].bitcast(F32), ALU.subtract).then_inc(proj_lo_made, 1)

            def add_second(t, p):
                after(dve, (x2_added, t + 1), (rs_ready, t - 1), tick=dve_tick)
                dve.tensor_tensor(x_in[:, p, :], x_in[:, p, :], y_in[:, p, 1, :], ALU.add).then_inc(x2_ready, 1)
                after(dve, (x2_ready, t + 1), tick=dve_tick)
                dve.bn_stats(stats[:, p, :], x_in[:, p, :]).then_inc(stat_step, 1)
                after(dve, (stat_step, t + 1), tick=dve_tick)
                dve.bn_aggr(mv[:, p, :], stats[:, p, :]).then_inc(mv_ready, 1)

            def keep_low_x(t, p):
                after(dve, (xhi_kept, t + 1), (q_made, t - 1), tick=dve_tick)
                dve.tensor_tensor(xT_lo[:, p, :], pg[:, :], xT_hi[:, p, :].bitcast(F32), ALU.subtract).then_inc(xlo_kept, 1)

            def keep_values(t, p):
                after(dve, (kt_kept, t + 1), (o_made, 4 * t - 4), tick=dve_tick)
                for r in range(2):
                    for b in range(2):
                        made = pg[64 * b:64 * b + 64, P:2 * P].rearrange("p (j r d) -> p j r d", j=4, r=2)
                        dve.tensor_copy(values[64 * r:64 * r + 64, p, b, :, r, 0:HD], made[:, :, r, :]).then_inc(v_kept, 1)

            def shift_scores(i):
                def stage_(t, p):
                    n = 4 * t + i
                    after(dve, (s_made, n + 1), tick=dve_tick)
                    rows = ps[i % 2][:, :].rearrange("p (h e) -> p h e", h=KVH)
                    dve.tensor_reduce(smax[:, i % 2, :], rows, AX.X, ALU.max).then_inc(max_step, 1)
                    after(dve, (max_step, n + 1), (pt_made, n - 1), tick=dve_tick)
                    peak = smax[:, i % 2, :].rearrange("p (h x) -> p h x", x=1).to_broadcast([P, KVH, 64])
                    dve.tensor_tensor(score[:, i % 2, :].rearrange("p (h e) -> p h e", h=KVH), rows, peak, ALU.subtract).then_inc(s_shifted, 1)
                return stage_

            def keep_attn(b):
                def stage_(t, p):
                    n = 2 * t + b
                    after(dve, (o_made, 4 * t + 2 * b + 2), tick=dve_tick)
                    heads = po[b][:, 0:272].rearrange("p (c h d) -> p c h d", c=2, h=KVH)
                    dve.reciprocal(rsum[:, b, :, :, :], heads[:, :, :, HD:HD + 1]).then_inc(sum_step, 1)
                    after(dve, (sum_step, n + 1), (at_made, t - 1), tick=dve_tick)
                    dve.tensor_tensor(attn[:, p, 256 * b:256 * b + 256].rearrange("p (c h d) -> p c h d", c=2, h=KVH), heads[:, :, :, 0:HD],
                                      rsum[:, b, :, :, :].to_broadcast([P, 2, KVH, HD]), ALU.mult).then_inc(o_kept, 1)
                return stage_

            def keep_low_attn(t, p):
                after(dve, (ahi_kept, t + 1), (w_made, t - 1), tick=dve_tick)
                order = "p (g b q) -> p b g q"
                dve.tensor_tensor(aT_lo[:, p, :].rearrange(order, g=GROUP, b=2), pg[:, :].rearrange("p (b g q) -> p b g q", b=2, g=GROUP),
                                  aT_hi[:, p, :].bitcast(F32).rearrange(order, g=GROUP, b=2), ALU.subtract).then_inc(alo_kept, 1)

            def add_attn(t, p):
                after(dve, (w_made, t + 1), (x2_loaded[p], slot_full(t, p)), tick=dve_tick)
                dve.tensor_tensor(x_out[:, p, :], ph[:, :], x_out[:, p, :], ALU.add).then_inc(x3_ready, 1)
                after(dve, (x3_ready, t + 1), (rs3_ready, t - 1), tick=dve_tick)
                dve.bn_stats(stats3[:, p, :], x_out[:, p, :]).then_inc(stat3_step, 1)
                after(dve, (stat3_step, t + 1), tick=dve_tick)
                dve.bn_aggr(mv3[:, p, :], stats3[:, p, :]).then_inc(mv3_ready, 1)

            pipelined(dve, TILES, [(shift_scores(0), 3), (shift_scores(1), 3), (keep_low_attn, 4), (shift_scores(2), 3), (add_second, 1),
                                   (shift_scores(3), 3), (add_attn, 4), (keep_values, 2), (keep_attn(0), 3), (keep_low_x, 2), (keep_attn(1), 3)])


def ffn_phase(nc, shared, a, out):
    TOK, GROUPS, LAST = TG * P, TILES // TG, NI - 1
    with ExitStack() as stack:
        c = Ctx(nc, stack, "d_")
        sb, pb, sem = c.sb, c.pb, c.sem
        down_hi, down_lo = sb("down_hi", [P, NI, DIM], F32R), sb("down_lo", [P, NI, DIM], F32R)
        ident = sb("ident", [P, P])
        b_gate, b_up, minus_gate, b_down = sb("b_gate", [P, NI]), sb("b_up", [P, NI]), sb("minus_gate", [P, NI]), sb("b_down", [P, DIM])
        stage, n_in, x_res = sb("stage", [P, 2, DIM]), sb("n_in", [P, TG, DIM]), sb("x_res", [P, TG, DIM])
        nT_hi, nT_lo = sb("nT_hi", [P, KD, TOK], F32R), sb("nT_lo", [P, KD, TOK], F32R)
        expo, hid = sb("expo", [P, 2, TOK]), sb("hid", [P, 2, TOK])
        hid_hi, hid_lo = sb("hid_hi", [P, 2, TOK], F32R), sb("hid_lo", [P, 2, TOK], F32R)
        pgate, pup = [pb(f"pgate{i}") for i in range(2)], [pb(f"pup{i}") for i in range(2)]
        pdown = [pb(f"pdown{i}") for i in range(TG)]
        tbank = (pgate[1], pup[1])
        names = ("zeroed ident_made bias_loaded minus_made down_hi_made down_lo_made t_made nhi_kept nlo_kept gate_made up_made "
                 "expo_made expo_step gated hid_made hi_made lo_made down_done res_biased y_ready")
        (zeroed, ident_made, bias_loaded, minus_made, down_hi_made, down_lo_made, t_made, nhi_kept, nlo_kept, gate_made, up_made,
         expo_made, expo_step, gated, hid_made, hi_made, lo_made, down_done, res_biased, y_ready) = (sem(n) for n in names.split())
        n_loaded, res_loaded, stored = ([sem(f"{n}{i}") for i in range(TG)] for n in ("n_loaded", "res_loaded", "stored"))
        down_loaded = [sem(f"down_loaded{i}") for i in range(2)]
        sp_tick, act_tick, pool_tick, pe_tick, dve_tick = (sem(e + "_tick") for e in ("sp", "act", "pool", "pe", "dve"))
        stack.callback(c.clear)
        block = stack.enter_context(nc.Block())
        out_v = out.rearrange("(t b) s d -> t (b s) d", b=2)
        gu_hi, gu_lo = shared["gu_hi"], shared["gu_lo"]

        def width(i):
            return min(P, INTER - P * i)

        def read_before(g, i):
            return NI * g + i - (1 if i else 0)

        @block.sync
        def _(sp):
            def load(g):
                for n in range(TG):
                    after(sp, (t_made, TG * (g - 1) + n + 1), tick=sp_tick)
                    sp.dma_start(n_in[:, n, :], shared["n3"][TG * g + n, :, :]).then_inc(n_loaded[n], 16)

            def load_residual(g):
                for n in range(TG):
                    after(sp, (stored[n], 16 * g), tick=sp_tick)
                    sp.dma_start(x_res[:, n, :], shared["x3"][TG * g + n, :, :]).then_inc(res_loaded[n], 16)

            load(0)
            for buf, b in ((b_gate, "b_gate"), (b_up, "b_up")):
                sp.dma_start(buf[:, 0:LAST], a[b + "_main"]).then_inc(bias_loaded, 16)
                sp.dma_start(buf[0:width(LAST), LAST:NI], a[b + "_rest"]).then_inc(bias_loaded, 16)
            sp.dma_start(b_down[:, :], a["b_down"].partition_broadcast(P)).then_inc(bias_loaded, 16)
            for i in range(NI):
                if i >= 2:
                    sp.wait_ge(down_lo_made, i - 1)
                sp.dma_start(stage[0:width(i), i % 2, :], a["w_down"][P * i:P * i + width(i), :]).then_inc(down_loaded[i % 2], 16)
            load_residual(0)
            with sp.Fori(1, GROUPS) as g:
                load(g)
                load_residual(g)

        @block.gpsimd
        def _(pool):
            identity(pool, ident, zeroed, ident_made)
            pool.wait_ge(bias_loaded, 80)
            pool.tensor_scalar(minus_gate[:, 0:LAST], b_gate[:, 0:LAST], -1.0, None, ALU.mult).then_inc(minus_made, 1)
            pool.wait_ge(minus_made, 1)
            pool.tensor_scalar(minus_gate[0:width(LAST), LAST:NI], b_gate[0:width(LAST), LAST:NI], -1.0, None, ALU.mult).then_inc(minus_made, 1)
            for i in range(NI):
                pool.wait_ge(down_hi_made, i + 1)
                w = width(i)
                pool.tensor_tensor(down_lo[0:w, i, :], stage[0:w, i % 2, :], down_hi[0:w, i, :].bitcast(F32), ALU.subtract).then_inc(down_lo_made, 1)

            def group(g):
                for n in range(TG):
                    after(pool, (res_loaded[n], 16 * g + 16), tick=pool_tick)
                    pool.tensor_tensor(x_res[:, n, :], x_res[:, n, :], b_down[:, :], ALU.add).then_inc(res_biased, 1)
                for n in range(TG):
                    after(pool, (y_ready, TG * g + n + 1), tick=pool_tick)
                    pool.dma_start(out_v[TG * g + n, :, :], x_res[:, n, :]).then_inc(stored[n], 16)

            pool.wait_ge(minus_made, 2)
            with pool.Fori(0, GROUPS) as g:
                group(g)
            for n in range(TG):
                pool.wait_ge(stored[n], 16 * GROUPS)

        @block.scalar
        def _(act):
            act.wait_ge(minus_made, 2)

            def keep_high_n(g, n):
                after(act, (t_made, TG * g + n + 1), tick=act_tick)
                act.activation(nT_hi[:, :, P * n:P * n + P], tbank[n % 2][:, :].rearrange("p (k n) -> p k n", k=KD), ACT.Copy).then_inc(nhi_kept, 1)

            def exponent(g, i):
                w = width(i)
                after(act, (gate_made, NI * g + i + 1), (gated, read_before(g, i)), tick=act_tick)
                act.activation(expo[0:w, i % 2, :], pgate[i % 2][0:w, :], ACT.Exp, scale=-1.0, bias=minus_gate[0:w, i:i + 1]).then_inc(expo_made, 1)

            def keep_high(g, i):
                w = width(i)
                after(act, (hid_made, NI * g + i + 1), (down_done, read_before(g, i)), tick=act_tick)
                act.activation(hid_hi[0:w, i % 2, :], hid[0:w, i % 2, :], ACT.Copy).then_inc(hi_made, 1)

            def group(g):
                keep_high_n(g, 0)
                keep_high_n(g, 1)
                if not isinstance(g, int):
                    keep_high(g - 1, LAST)
                keep_high_n(g, 2)
                keep_high_n(g, 3)
                for i in range(NI):
                    if isinstance(g, int):
                        w = width(i)
                        act.wait_ge(down_loaded[i % 2], 16 * (i // 2 + 1))
                        act.activation(down_hi[0:w, i, :], stage[0:w, i % 2, :], ACT.Copy).then_inc(down_hi_made, 1)
                    exponent(g, i)
                    if i:
                        keep_high(g, i - 1)

            group(0)
            with act.Fori(1, GROUPS) as g:
                group(g)
            keep_high(GROUPS - 1, LAST)

        @block.tensor
        def _(pe):
            pe.wait_ge(ident_made, 1)

            def transpose_n(g, n):
                free = (nlo_kept, TG * g + n - 1) if n >= 2 else ((gated, hid_made)[n], NI * g - 1)
                after(pe, (n_loaded[n], 16 * g + 16), free, tick=pe_tick)
                for k in range(KD):
                    mm = pe.transpose(tbank[n % 2][:, P * k:P * k + P], n_in[:, n, P * k:P * k + P], ident[:, :])
                mm.then_inc(t_made, 1)

            def product(g, i, which, bank, read, made):
                w = width(i)
                after(pe, (read, read_before(g, i)), tick=pe_tick)
                for k in range(KD):
                    cols = slice((which * KD + k) * INTER + P * i, (which * KD + k) * INTER + P * i + w)
                    pe.matmul(bank[0:w, :], gu_hi[:, cols], nT_hi[:, k, :], start=k == 0, stop=False)
                    pe.matmul(bank[0:w, :], gu_hi[:, cols], nT_lo[:, k, :], start=False, stop=False)
                    mm = pe.matmul(bank[0:w, :], gu_lo[:, cols], nT_hi[:, k, :], start=False, stop=k == KD - 1)
                mm.then_inc(made, 1)

            def down(g, i):
                w = width(i)
                after(pe, (hi_made, NI * g + i + 1), (lo_made, NI * g + i + 1), tick=pe_tick)
                if isinstance(g, int) and g == 0:
                    pe.wait_ge(down_lo_made, i + 1)
                for n in range(TG):
                    if i == 0:
                        after(pe, (y_ready, TG * (g - 1) + n + 1), tick=pe_tick)
                    hi, lo = hid_hi[0:w, i % 2, P * n:P * n + P], hid_lo[0:w, i % 2, P * n:P * n + P]
                    pe.matmul(pdown[n][:, :], hi, down_hi[0:w, i, :], start=i == 0, stop=False)
                    pe.matmul(pdown[n][:, :], hi, down_lo[0:w, i, :], start=False, stop=False)
                    mm = pe.matmul(pdown[n][:, :], lo, down_hi[0:w, i, :], start=False, stop=i == LAST)
                mm.then_inc(down_done, 1)

            def group(g):
                for n in range(TG):
                    transpose_n(g, n)
                if not isinstance(g, int):
                    down(g - 1, LAST)
                after(pe, (nlo_kept, TG * g + TG), tick=pe_tick)
                for i in range(NI):
                    product(g, i, 0, pgate[i % 2], gated, gate_made)
                    product(g, i, 1, pup[i % 2], hid_made, up_made)
                    if i:
                        down(g, i - 1)

            group(0)
            pe.wait_ge(down_lo_made, NI)
            with pe.Fori(1, GROUPS) as g:
                group(g)
            down(GROUPS - 1, LAST)

        @block.vector
        def _(dve):
            dve.wait_ge(minus_made, 2)

            def keep_low_n(g, n):
                after(dve, (nhi_kept, TG * g + n + 1), tick=dve_tick)
                cols = slice(P * n, P * n + P)
                dve.tensor_tensor(nT_lo[:, :, cols], tbank[n % 2][:, :].rearrange("p (k n) -> p k n", k=KD), nT_hi[:, :, cols].bitcast(F32),
                                  ALU.subtract).then_inc(nlo_kept, 1)

            def activate(g, i):
                w, n = width(i), NI * g + i
                e, h = expo[0:w, i % 2, :], hid[0:w, i % 2, :]
                after(dve, (expo_made, n + 1), tick=dve_tick)
                dve.tensor_scalar(e, e, 1.0, None, ALU.add).then_inc(expo_step, 1)
                after(dve, (expo_step, 2 * n + 1), tick=dve_tick)
                dve.reciprocal(e, e).then_inc(expo_step, 1)
                after(dve, (expo_step, 2 * n + 2), (hi_made, read_before(g, i)), (lo_made, read_before(g, i)), tick=dve_tick)
                dve.scalar_tensor_tensor(h, pgate[i % 2][0:w, :], b_gate[0:w, i:i + 1], e, ALU.add, ALU.mult).then_inc(gated, 1)
                after(dve, (gated, n + 1), (up_made, n + 1), tick=dve_tick)
                dve.scalar_tensor_tensor(h, pup[i % 2][0:w, :], b_up[0:w, i:i + 1], h, ALU.add, ALU.mult).then_inc(hid_made, 1)

            def keep_low(g, i):
                w = width(i)
                after(dve, (hi_made, NI * g + i + 1), (down_done, read_before(g, i)), tick=dve_tick)
                dve.tensor_tensor(hid_lo[0:w, i % 2, :], hid[0:w, i % 2, :], hid_hi[0:w, i % 2, :].bitcast(F32), ALU.subtract).then_inc(lo_made, 1)

            def finish(g):
                after(dve, (down_done, NI * g + NI), tick=dve_tick)
                for n in range(TG):
                    after(dve, (res_biased, TG * g + n + 1), tick=dve_tick)
                    dve.tensor_tensor(x_res[:, n, :], pdown[n][:, :], x_res[:, n, :], ALU.add).then_inc(y_ready, 1)

            def group(g):
                keep_low_n(g, 0)
                keep_low_n(g, 1)
                if not isinstance(g, int):
                    keep_low(g - 1, LAST)
                keep_low_n(g, 2)
                keep_low_n(g, 3)
                if not isinstance(g, int):
                    finish(g - 1)
                for i in range(NI):
                    activate(g, i)
                    keep_low(g, i) if i < LAST else None

            group(0)
            with dve.Fori(1, GROUPS) as g:
                group(g)
            keep_low(GROUPS - 1, LAST)
            finish(GROUPS - 1)


def build(nc, a, out, phases=4):
    with ExitStack() as stack:
        def sb(name, shape, dt=F32):
            return stack.enter_context(nc.sbuf_tensor(name, shape, dt))

        def dram(name, shape):
            return nc.dram_tensor(name, shape, F32, kind="Internal").ap()

        shared = {
            "xs": dram("expert_rows", [EXPERTS * REGION, DIM]), "ys": dram("expert_results", [BLOCKS * P, DIM]),
            "x1": dram("x_after_attention0", [TILES, P, DIM]), "x3": dram("x_after_attention1", [TILES, P, DIM]),
            "n3": dram("norm_after_attention1", [TILES, P, DIM]),
            "last": sb("last", [P, 1]), "table": sb("table", [P, 2, BLOCKS], I32), "y_at": sb("y_at", [P, 2 * TILES], I32),
        }
        shared["x2"] = dram("x_after_experts", [TILES, P, DIM])
        with ExitStack() as moe:
            shared["w_hi"] = moe.enter_context(nc.sbuf_tensor("expert_w_hi", [P, EXPERTS * EW], F32R))
            shared["w_lo"] = moe.enter_context(nc.sbuf_tensor("expert_w_lo", [P, EXPERTS * EW], F32R))
            layer0_phase(nc, shared, {k: a[v] for k, v in dict(
                x="x", ctx="ctx_4096", Wq="L0_xattn_Wq", bq="L0_xattn_bq", Wk="L0_xattn_Wk", bk="L0_xattn_bk",
                Wv="L0_xattn_Wv", bv="L0_xattn_bv", Wo="L0_xattn_Wo", bo="L0_xattn_bo",
                W_gate="L0_ffn_W_gate", b_gate="L0_ffn_b_gate", W_e="L0_ffn_W_e").items()})
            if phases < 2:
                return
            expert_phase(nc, shared, a["L0_ffn_b_e"])
        if phases < 3:
            return
        shared["gu_hi"] = sb("gate_up_hi", [P, 2 * KD * INTER], F32R)
        shared["gu_lo"] = sb("gate_up_lo", [P, 2 * KD * INTER], F32R)
        layer1_phase(nc, shared, {"ctxT": a["ctxT"], "gate_up": a["gate_up"], "Wq": a["L1_xattn_Wq"], "Wk": a["L1_xattn_Wk"],
                                  "Wv": a["L1_xattn_Wv"], "Wo": a["L1_xattn_Wo"]})
        if phases < 4:
            return
        ffn_phase(nc, shared, {"w_down": a["L1_ffn_w_down"], "b_down": a["L1_ffn_b_down"],
                               **{k: a[k] for k in ("b_gate_main", "b_gate_rest", "b_up_main", "b_up_rest")}}, out)


TRANSPOSED = ("L0_xattn_Wq", "L0_xattn_Wk", "L0_xattn_Wv", "L0_xattn_Wo", "L1_ffn_w_gate", "L1_ffn_w_up", "L1_ffn_w_down")


def layout(inputs):
    import numpy as np
    a = {n: np.asarray(x) for n, x in inputs.items()}
    a = {n: x.T if n in TRANSPOSED else x for n, x in a.items()}
    a["ctxT"] = a["ctx_4096"].reshape(TILES, P, KD, P).transpose(0, 3, 2, 1).reshape(TILES, P, DIM)
    a["L1_xattn_Wq"] = a["L1_xattn_Wq"].reshape(DIM, KVH, GROUP, HD).transpose(0, 2, 1, 3).reshape(DIM, DIM)
    a["L1_xattn_Wo"] = a["L1_xattn_Wo"].reshape(KVH, GROUP, HD, DIM).transpose(1, 0, 2, 3).reshape(DIM, DIM)
    both = np.stack([a.pop("L1_ffn_w_gate"), a.pop("L1_ffn_w_up")])
    a["gate_up"] = both.reshape(2, KD, P, 2, INTER // 2).transpose(0, 1, 3, 2, 4).reshape(TILES, P, INTER // 2)
    for b in ("gate", "up"):
        bias, full = a.pop("L1_ffn_b_" + b), INTER // P
        a[f"b_{b}_main"] = bias[:full * P].reshape(full, P).T
        a[f"b_{b}_rest"] = bias[full * P:].reshape(-1, 1)
    return {n: np.ascontiguousarray(x) for n, x in a.items()}


def kernel(**inputs):
    import numpy as np
    from concourse import bacc
    from concourse.bass_utils import run_bass_kernel_spmd

    nc = bacc.Bacc("TRN2", target_bir_lowering=False, num_devices=1)
    arrays = layout(inputs)
    args = {n: nc.dram_tensor(n, x.shape, mybir.dt.from_np(x.dtype), kind="ExternalInput").ap() for n, x in arrays.items()}
    out = nc.dram_tensor("out", (BATCH, SEQ, DIM), F32, kind="ExternalOutput").ap()
    build(nc, args, out)
    result = run_bass_kernel_spmd(nc, [arrays], core_ids=[0])
    return result.results[0]["out"]
```

```python
import concourse.bass as bass
from concourse import mybir
from contextlib import ExitStack

F32 = mybir.dt.float32
F32R = mybir.dt.float32r
BF16 = mybir.dt.bfloat16
I32 = mybir.dt.int32
U32 = mybir.dt.uint32
ALU = mybir.AluOpType
ACT = mybir.ActivationFunctionType
AX = mybir.AxisListType

P = 128
BATCH, SEQ, DIM = 32, 64, 512
TILES = BATCH * SEQ // P
KD = DIM // P
EPS = 1e-5

H0 = 8
LH = DIM // H0
SCALE0 = LH ** -0.5

EXPERTS = 8
EW = KD * DIM
REGION = BATCH * SEQ + P
BLOCKS = 2 * TILES + EXPERTS - 1

KVH, GROUP, HD = 8, 4, 16
SCALE1 = HD ** -0.5
INTER = 1376
NI = -(-INTER // P)
TG = 4


def after(eng, *counts, tick):
    for n, (sem, value) in enumerate(counts):
        if not isinstance(value, int):
            eng.wait_ge(sem, value)
            if n == len(counts) - 1 or eng.engine == mybir.EngineType.SP:
                eng.sem_inc(tick, 1)
        elif value > 0:
            eng.wait_ge(sem, value)


def slot_full(t, par):
    return 16 * (t // 2 + 1) if isinstance(t, int) else t * 8 + (16 - 8 * par)


def upto(t, tiles):
    return min(t, tiles) if isinstance(t, int) else t


def pipelined(eng, tiles, stages):
    last_lag = max(lag for _, lag in stages)
    first = last_lag + 2 + last_lag % 2
    until = first + (tiles - first) // 2 * 2

    def peeled(s):
        for stage, lag in stages:
            if 0 <= s - lag < tiles:
                stage(s - lag, (s - lag) % 2)

    for s in range(first):
        peeled(s)
    with eng.Fori(first // 2, until // 2) as i:
        for odd in range(2):
            for stage, lag in stages:
                stage(2 * i + (odd - lag), (odd - lag) % 2)
    for s in range(until, tiles + last_lag):
        peeled(s)


class Ctx:

    def __init__(self, nc, stack, prefix):
        self.nc, self.stack, self.prefix = nc, stack, prefix
        self.sems = []

    def sb(self, name, shape, dt=F32):
        return self.stack.enter_context(self.nc.sbuf_tensor(self.prefix + name, shape, dt))

    def pb(self, name):
        return self.stack.enter_context(self.nc.psum_tensor(self.prefix + name, [P, 512], F32))

    def sem(self, name):
        self.sems.append(self.stack.enter_context(self.nc.semaphore(self.prefix + name)))
        return self.sems[-1]

    def clear(self):
        with self.nc.Block() as block:
            @block.gpsimd
            def _(pool):
                numbers = sorted(s.num for s in self.sems)
                first = 0
                for n in range(1, len(numbers) + 1):
                    if n == len(numbers) or numbers[n] != numbers[n - 1] + 1:
                        pool.sem_clear(range(numbers[first], numbers[n - 1] + 1))
                        first = n


def block_diagonal(ap):
    return ap[0:64, 0:64], ap[64:128, 64:128]


def layer0_phase(nc, shared, a):
    with ExitStack() as stack:
        c = Ctx(nc, stack, "a_")
        sb, pb, sem = c.sb, c.pb, c.sem
        wq, wk, wv, wo = (sb(n, [P, P]) for n in ("wq", "wk", "wv", "wo"))
        bq, bk = sb("bq", [P, 2, 64]), sb("bk", [P, 2, 64])
        bv, bo = sb("bv", [P, 1]), sb("bo", [P, 1])
        wg, bg = sb("wg", [P, KD, EXPERTS]), sb("bg", [P, EXPERTS])
        ident = sb("ident", [P, P])
        ctx_in, x_in, x_res, xn, xn2 = (sb(n, [P, 2, DIM]) for n in ("ctx_in", "x_in", "x_res", "xn", "xn2"))
        qT, kT, score, probT, attn, xT = (sb(n, [P, 2, DIM]) for n in ("qT", "kT", "score", "probT", "attn", "xT"))
        minus_half = sb("minus_half", [P, 1])
        v = sb("v", [P, 2, H0, LH + 1])
        wstage = sb("wstage", [P, 2, 1024])
        stats, mv, rstd = sb("stats", [P, 2, 6]), sb("mv", [P, 2, 2]), sb("rstd", [P, 2, 2])
        stats2, mv2, rstd2 = sb("stats2", [P, 2, 6]), sb("mv2", [P, 2, 2]), sb("rstd2", [P, 2, 2])
        smax = sb("smax", [P, 2, 8])
        rsum = sb("rsum", [P, 2, 2, 4, 1])
        logit, top8, chosen = sb("logit", [P, 2, 8]), sb("top8", [P, 2, 8]), sb("chosen", [P, 2, 8], U32)
        both, rank = sb("both", [P, 2, 8], BF16), sb("rank", [P, 2, 8])
        picked = sb("picked", [P, 2, 2, 8])
        ati = sb("ati", [P, 2, 2], I32)
        seen = sb("seen", [P, 8])
        seenb = sb("seenb", [P, 8], BF16)
        expert_no, region_at = sb("expert_no", [P, 8]), sb("region_at", [P, 8])
        before, ones = sb("before", [P, P], BF16), sb("ones", [P, P], BF16)
        zero_rows = sb("zero_rows", [P, DIM])
        k128, below = sb("k128", [P, 8, 16]), sb("below", [P, 8, 8])
        counts, nblk, start, end = sb("counts", [P, 8]), sb("nblk", [P, 8]), sb("start", [P, 8]), sb("end", [P, 8])
        over, lower = sb("over", [P, 8, 16]), sb("lower", [P, 8, 8])
        blk, passed, bstart = sb("blk", [P, BLOCKS]), sb("passed", [P, BLOCKS, 8]), sb("bstart", [P, BLOCKS])
        bexp, table = sb("bexp", [P, BLOCKS]), sb("table", [P, 2, BLOCKS])
        padf, padi, shift = sb("padf", [P, 8]), sb("padi", [P, 8], I32), sb("shift", [P, 8])
        at_kept2 = sb("at_kept2", [P, 2 * TILES])
        moved = sb("moved", [P, TILES * 2, 8])
        at_kept, hot_kept = sb("at_kept", [P, TILES, 2]), sb("hot_kept", [P, TILES, 2, 8])

        pkq, pv, ps, pt, py, pr = (pb(n) for n in ("pkq", "pv", "ps", "pt", "py", "pr"))
        po = stack.enter_context(nc.psum_tensor("a_po", [P, 2, 512], F32))
        N_CONST = 13

        consts_loaded, zeroed, ident0, made_const = sem("consts_loaded"), sem("zeroed"), sem("ident0"), sem("made_const")
        ctx_loaded = [sem(f"ctx_loaded{i}") for i in range(2)]
        x_loaded = [sem(f"x_loaded{i}") for i in range(2)]
        res_loaded = [sem(f"res_loaded{i}") for i in range(2)]
        w_loaded = [sem(f"w_loaded{i}") for i in range(2)]
        x1_stored = [sem(f"x1_stored{i}") for i in range(2)]
        scattered = [sem(f"scattered{i}") for i in range(2)]
        w_hi, w_lo = sem("w_hi"), sem("w_lo")
        k_made, k_kept, q_made, q_kept = sem("k_made"), sem("k_kept"), sem("q_made"), sem("q_kept")
        v_made, v_kept, s_made, s_shifted, exp_done = sem("v_made"), sem("v_kept"), sem("s_made"), sem("s_shifted"), sem("exp_done")
        pt_made, pt_kept, o_made, o_kept = sem("pt_made"), sem("pt_kept"), sem("o_made"), sem("o_kept")
        y_made, x1_ready, xn_ready, xn2_ready = sem("y_made"), sem("x1_ready"), sem("xn_ready"), sem("xn2_ready")
        xt_made, xt_kept, l_made, both_ready = sem("xt_made"), sem("xt_kept"), sem("l_made"), sem("both_ready")
        r_made, at_ready, count_made, pad_ready, padded = sem("r_made"), sem("at_ready"), sem("count_made"), sem("pad_ready"), sem("padded")
        norm_step, norm2_step, max_step, sum_step = sem("norm_step"), sem("norm2_step"), sem("max_step"), sem("sum_step")
        mv_ready, mv2_ready, rs_step, rs2_step, rs_ready, rs2_ready = (sem(n) for n in ("mv_ready", "mv2_ready", "rs_step", "rs2_step", "rs_ready", "rs2_ready"))
        choose_step, place_step, table_step = sem("choose_step"), sem("place_step"), sem("table_step")
        sp_tick, act_tick, pool_tick, pe_tick, dve_tick = (sem(e + "_tick") for e in ("sp", "act", "pool", "pe", "dve"))
        stack.callback(c.clear)
        block = stack.enter_context(nc.Block())

        x_v = a["x"].rearrange("(t b) s d -> t (b s) d", b=2)
        c_v = a["ctx"].rearrange("(t b) s d -> t (b s) d", b=2)
        w_v = a["W_e"].rearrange("e (k p) h -> p (e k) h", p=P)
        loaded_consts = [0]

        @block.sync
        def _(sp):
            def const(dst, src):
                sp.dma_start(dst, src).then_inc(consts_loaded, 16)
                loaded_consts[0] += 16

            sp.wait_ge(zeroed, 4)
            for buf, w in ((wk, "Wk"), (wv, "Wv"), (wq, "Wq"), (wo, "Wo")):
                for part in block_diagonal(buf):
                    const(part, a[w])
            for buf, b in ((bk, "bk"), (bq, "bq")):
                for half in range(2):
                    const(buf[:, half, :], a[b].partition_broadcast(P))
            for buf, b in ((bv, "bv"), (bo, "bo")):
                for half in range(2):
                    const(buf[64 * half:64 * half + 64, :], a[b].rearrange("(p a) -> p a", a=1))
            const(bg[:, :], a["b_gate"].partition_broadcast(P))
            const(wg[:, :, :], a["W_gate"].rearrange("(k p) e -> p k e", p=P))

            def load_ctx(t, p):
                after(sp, (v_made, t - 1), tick=sp_tick)
                sp.dma_start(ctx_in[:, p, :], c_v[t, :, :]).then_inc(ctx_loaded[p], 16)

            def load_x(t, p):
                after(sp, (xn_ready, t - 1), tick=sp_tick)
                sp.dma_start(x_in[:, p, :], x_v[t, :, :]).then_inc(x_loaded[p], 16)

            def load_weights(t, p):
                after(sp, (w_lo, t - 1), tick=sp_tick)
                sp.dma_start(wstage[:, p, :].rearrange("p (k h) -> p k h", k=2), w_v[:, bass.ds(2 * t, 2), :]).then_inc(w_loaded[p], 16)

            def load_residual(t, p):
                after(sp, (xn2_ready, t - 1), (x1_stored[p], slot_full(t, p) - 16), tick=sp_tick)
                sp.dma_start(x_res[:, p, :], x_v[t, :, :]).then_inc(res_loaded[p], 16)

            def store_x1(t, p):
                after(sp, (x1_ready, t + 1), tick=sp_tick)
                sp.dma_start(shared["x1"][t, :, :], x_res[:, p, :]).then_inc(x1_stored[p], 16)

            pipelined(sp, TILES, [(load_residual, 3), (load_x, 0), (load_ctx, 0), (load_weights, 1), (store_x1, 4)])
            sp.wait_ge(pad_ready, 1)
            for e in range(EXPERTS):
                row = sp.value_load(padi[0:1, e:e + 1], min_val=0, max_val=EXPERTS * REGION - P)
                sp.dma_start(shared["xs"][bass.ds(row, P), :], zero_rows[:, :]).then_inc(padded, 16)
            sp.wait_ge(padded, 16 * EXPERTS)
            for i in range(2):
                sp.wait_ge(x1_stored[i], 8 * TILES)

        @block.gpsimd
        def _(pool):
            for buf in (wk, wv, wq, wo):
                pool.memset(buf[:, :], 0.0).then_inc(zeroed, 1)
            pool.memset(v[:, :, :, LH:LH + 1], 1.0).then_inc(made_const, 1)
            pool.memset(zero_rows[:, :], 0.0).then_inc(made_const, 1)
            pool.memset(ones[:, :], 1.0).then_inc(made_const, 1)
            pool.memset(seenb[:, :], 0.0).then_inc(made_const, 1)
            pool.memset(seen[:, :], 0.0).then_inc(made_const, 1)
            for buf, pattern, base in ((expert_no, [[1, 8]], 0), (region_at, [[REGION, 8]], 0),
                                       (k128, [[0, 8], [P, 16]], 0), (blk, [[1, BLOCKS]], 0)):
                pool.iota(buf[:], pattern, base=base, channel_multiplier=0,
                          allow_small_or_imprecise_dtypes=True).then_inc(made_const, 1)
            pool.memset(minus_half[:, :], -0.5).then_inc(made_const, 1)
            pool.memset(ident[:, :], 0.0).then_inc(ident0, 1)
            pool.memset(before[:, :], 1.0).then_inc(ident0, 1)
            pool.memset(below[:, :, :], 1.0).then_inc(ident0, 1)
            pool.wait_ge(ident0, 3)
            pool.affine_select(out=ident[:, :], in_=ident[:, :], compare_op=ALU.not_equal, fill=1.0,
                               base=0, pattern=[[-1, P]], channel_multiplier=1).then_inc(made_const, 1)
            pool.affine_select(out=before[:, :], in_=before[:, :], compare_op=ALU.is_ge, fill=0.0,
                               base=-1, pattern=[[1, P]], channel_multiplier=-1).then_inc(made_const, 1)
            pool.affine_select(out=below[:, :, :], in_=below[:, :, :], compare_op=ALU.is_ge, fill=0.0,
                               base=-1, pattern=[[1, 8], [-1, 8]], channel_multiplier=0).then_inc(made_const, 1)

            def inverse_deviation(t, m, r, step, done):
                pool.tensor_scalar(m[:, 1:2], m[:, 1:2], EPS, None, ALU.add).then_inc(step, 1)
                after(pool, (step, 2 * t + 1), tick=pool_tick)
                pool.tensor_tensor(r[:, 0:1], m[:, 1:2], minus_half[:, :], ALU.pow).then_inc(step, 1)
                after(pool, (step, 2 * t + 2), tick=pool_tick)
                pool.tensor_scalar(r[:, 1:2], m[:, 0:1], -1.0, r[:, 0:1], ALU.mult, ALU.mult).then_inc(done, 1)

            def scale_x(t, p):
                after(pool, (mv_ready, t + 1), (xn_ready, t - 1), tick=pool_tick)
                inverse_deviation(t, mv[:, p, :], rstd[:, p, :], rs_step, rs_ready)

            def scale_x1(t, p):
                after(pool, (mv2_ready, t + 1), (xn2_ready, t - 1), tick=pool_tick)
                inverse_deviation(t, mv2[:, p, :], rstd2[:, p, :], rs2_step, rs2_ready)

            def low_part(t, p):
                after(pool, (w_hi, t + 1), tick=pool_tick)
                dst = bass.ds(1024 * t, 1024)
                pool.tensor_tensor(shared["w_lo"][:, dst], wstage[:, p, :], shared["w_hi"][:, dst].bitcast(F32), ALU.subtract).then_inc(w_lo, 1)

            def scatter(t, p):
                after(pool, (at_ready, t + 1), tick=pool_tick)
                for k in range(2):
                    pool.indirect_dma_start(out=shared["xs"], out_offset=bass.IndirectOffsetOnAxis(ap=ati[:, p, k:k + 1], axis=0),
                                            in_=xn2[:, p, :], in_offset=None).then_inc(scattered[p], 16)

            pipelined(pool, TILES, [(scatter, 5), (scale_x, 0), (scale_x1, 3), (low_part, 2)])
            for i in range(2):
                pool.wait_ge(scattered[i], 16 * TILES)

        @block.scalar
        def _(act):
            act.wait_ge(consts_loaded, loaded_consts[0])
            act.wait_ge(made_const, N_CONST)

            def keep_v(t, p):
                after(act, (v_made, t + 1), (o_made, t - 1), tick=act_tick)
                act.activation(v[:, p, :, 0:LH], pv[:, :].rearrange("p (h l) -> p h l", h=H0), ACT.Identity, bias=bv[:, 0:1]).then_inc(v_kept, 1)

            def norm_x(t, p):
                after(act, (rs_ready, t + 1), (q_made, t - 1), tick=act_tick)
                act.activation(xn[:, p, :], x_in[:, p, :], ACT.Identity, scale=rstd[:, p, 0:1], bias=rstd[:, p, 1:2]).then_inc(xn_ready, 1)

            def norm_x1(t, p):
                after(act, (rs2_ready, t + 1), (xt_made, t - 1), (scattered[p], 2 * slot_full(t, p) - 32), tick=act_tick)
                act.activation(xn2[:, p, :], x_res[:, p, :], ACT.Identity, scale=rstd2[:, p, 0:1], bias=rstd2[:, p, 1:2]).then_inc(xn2_ready, 1)

            def exponent(t, p):
                after(act, (s_shifted, t + 1), tick=act_tick)
                act.activation(score[:, p, :], score[:, p, :], ACT.Exp, scale=SCALE0).then_inc(exp_done, 1)

            def keep_probT(t, p):
                after(act, (pt_made, t + 1), (o_made, t - 1), tick=act_tick)
                act.activation(probT[:, p, :], pt[:, :], ACT.Copy).then_inc(pt_kept, 1)

            def keep_xT(t, p):
                after(act, (xt_made, t + 1), (l_made, t - 1), tick=act_tick)
                act.activation(xT[:, p, :], pt[:, :], ACT.Copy).then_inc(xt_kept, 1)

            def high_part(t, p):
                after(act, (w_loaded[p], slot_full(t, p)), tick=act_tick)
                act.activation(shared["w_hi"][:, bass.ds(1024 * t, 1024)], wstage[:, p, :], ACT.Copy).then_inc(w_hi, 1)

            pipelined(act, TILES, [(keep_xT, 4), (keep_probT, 2), (keep_v, 1), (norm_x, 0), (norm_x1, 3), (exponent, 1), (high_part, 1)])

        @block.tensor
        def _(pe):
            pe.wait_ge(consts_loaded, loaded_consts[0])
            pe.wait_ge(made_const, N_CONST)

            def make_k(t, p):
                after(pe, (ctx_loaded[p], slot_full(t, p)), (q_kept, t), tick=pe_tick)
                for j in range(4):
                    mm = pe.matmul(pkq[:, P * j:P * j + P], ctx_in[:, p, P * j:P * j + P], wk[:, :], start=True, stop=True)
                mm.then_inc(k_made, 1)

            def make_v(t, p):
                after(pe, (v_kept, t), tick=pe_tick)
                pe.matmul(pv[:, :], wv[:, :], ctx_in[:, p, :], start=True, stop=True).then_inc(v_made, 1)

            def make_q(t, p):
                after(pe, (xn_ready, t + 1), (k_kept, t + 1), tick=pe_tick)
                for j in range(4):
                    mm = pe.matmul(pkq[:, P * j:P * j + P], xn[:, p, P * j:P * j + P], wq[:, :], start=True, stop=True)
                mm.then_inc(q_made, 1)

            def make_scores(t, p):
                after(pe, (q_kept, t + 1), (s_shifted, t), tick=pe_tick)
                for j in range(4):
                    for b in range(2):
                        for r in range(2):
                            rows, cols = slice(64 * r, 64 * r + 64), slice(P * j + 64 * b, P * j + 64 * b + 64)
                            mm = pe.matmul(ps[rows, cols], qT[rows, p, cols], kT[rows, p, cols], start=True, stop=True)
                mm.then_inc(s_made, 1)

            def transpose_probs(t, p):
                after(pe, (exp_done, t + 1), (xt_kept, t - 1), tick=pe_tick)
                for j in range(4):
                    mm = pe.transpose(pt[:, P * j:P * j + P], score[:, p, P * j:P * j + P], ident[:, :])
                mm.then_inc(pt_made, 1)

            def make_attn(t, p):
                after(pe, (pt_kept, t + 1), (v_kept, t + 1), (o_kept, t), tick=pe_tick)
                for h in range(H0):
                    for b in range(2):
                        rows = slice(64 * b, 64 * b + 64)
                        mm = pe.matmul(po[rows, h // 4, 65 * (h % 4):65 * (h % 4) + 65], probT[rows, p, 64 * h:64 * h + 64],
                                       v[rows, p, h, :], start=True, stop=True)
                mm.then_inc(o_made, 1)

            def project(t, p):
                after(pe, (o_kept, t + 1), (x1_ready, t), tick=pe_tick)
                pe.matmul(py[:, :], wo[:, :], attn[:, p, :], start=True, stop=True).then_inc(y_made, 1)

            def transpose_x(t, p):
                after(pe, (xn2_ready, t + 1), (pt_kept, upto(t + 2, TILES)), tick=pe_tick)
                for j in range(4):
                    mm = pe.transpose(pt[:, P * j:P * j + P], xn2[:, p, P * j:P * j + P], ident[:, :])
                mm.then_inc(xt_made, 1)

            def make_logits(t, p):
                after(pe, (xt_kept, t + 1), (place_step, 5 * t - 4), tick=pe_tick)
                for j in range(4):
                    mm = pe.matmul(pr[:, 0:8], xT[:, p, P * j:P * j + P], wg[:, j, :], start=j == 0, stop=j == 3)
                mm.then_inc(l_made, 1)

            def make_rank(t, p):
                after(pe, (both_ready, t + 1), (place_step, 5 * t - 2), tick=pe_tick)
                pe.matmul(pr[:, 0:8], before[:, :], both[:, p, :], start=True, stop=False)
                pe.matmul(pr[:, 0:8], ones[:, :], seenb[:, :], start=False, stop=True).then_inc(r_made, 1)

            pipelined(pe, TILES, [(make_q, 1), (transpose_x, 4), (make_rank, 5), (project, 3), (transpose_probs, 2), (make_logits, 4), (make_v, 1), (make_scores, 1), (make_attn, 2), (make_k, 0)])
            pe.wait_ge(at_ready, TILES)
            pe.matmul(pr[:, 0:8], ones[:, :], seenb[:, :], start=True, stop=True).then_inc(count_made, 1)

        @block.vector
        def _(dve):
            dve.wait_ge(consts_loaded, loaded_consts[0])
            dve.wait_ge(made_const, N_CONST)
            def sum_x(t, p):
                after(dve, (x_loaded[p], slot_full(t, p)), tick=dve_tick)
                dve.bn_stats(stats[:, p, :], x_in[:, p, :]).then_inc(norm_step, 1)

            def average_x(t, p):
                after(dve, (norm_step, t + 1), (rs_ready, t - 1), tick=dve_tick)
                dve.bn_aggr(mv[:, p, :], stats[:, p, :]).then_inc(mv_ready, 1)

            def by_chunk(ap):
                return ap.rearrange("p (j o) -> p j o", j=4)

            def keep_k(t, p):
                after(dve, (k_made, t + 1), (s_made, t - 1), tick=dve_tick)
                dve.tensor_tensor(by_chunk(kT[:, p, :]), by_chunk(pkq[:, :]), bk4, ALU.add).then_inc(k_kept, 1)

            def keep_q(t, p):
                after(dve, (q_made, t + 1), (s_made, t - 1), tick=dve_tick)
                dve.tensor_tensor(by_chunk(qT[:, p, :]), by_chunk(pkq[:, :]), bq4, ALU.add).then_inc(q_kept, 1)

            bk4, bq4 = (b[:, :, :].rearrange("p (x a) o -> p x (a o)", x=1).to_broadcast([P, 4, P]) for b in (bk, bq))

            def max_scores(t, p):
                after(dve, (s_made, t + 1), tick=dve_tick)
                dve.tensor_reduce(smax[:, p, :], ps[:, :].rearrange("p (g e) -> p g e", g=8), AX.X, ALU.max).then_inc(max_step, 1)

            def shift_scores(t, p):
                after(dve, (pt_made, t - 1), (max_step, t + 1), tick=dve_tick)
                peak = smax[:, p, :].rearrange("p (g x) -> p g x", x=1).to_broadcast([P, 8, 64])
                dve.tensor_tensor(score[:, p, :].rearrange("p (g e) -> p g e", g=8), ps[:, :].rearrange("p (g e) -> p g e", g=8), peak, ALU.subtract).then_inc(s_shifted, 1)

            def heads():
                return po[:, :, 0:260].rearrange("p b (h l) -> p b h l", h=4)

            def invert_sums(t, p):
                after(dve, (o_made, t + 1), tick=dve_tick)
                dve.reciprocal(rsum[:, p, :, :], heads()[:, :, :, 64:65]).then_inc(sum_step, 1)

            def keep_attn(t, p):
                after(dve, (y_made, t - 1), (sum_step, t + 1), tick=dve_tick)
                dve.tensor_tensor(attn[:, p, :].rearrange("p (b h l) -> p b h l", b=2, h=4), heads()[:, :, :, 0:64],
                                  rsum[:, p, :, :].to_broadcast([P, 2, 4, 64]), ALU.mult).then_inc(o_kept, 1)

            def add_residual(t, p):
                after(dve, (y_made, t + 1), (res_loaded[p], slot_full(t, p)), tick=dve_tick)
                dve.scalar_tensor_tensor(x_res[:, p, :], py[:, :], bo[:, 0:1], x_res[:, p, :], ALU.add, ALU.add).then_inc(x1_ready, 1)

            def sum_x1(t, p):
                after(dve, (x1_ready, t + 1), tick=dve_tick)
                dve.bn_stats(stats2[:, p, :], x_res[:, p, :]).then_inc(norm2_step, 1)

            def average_x1(t, p):
                after(dve, (norm2_step, t + 1), (rs2_ready, t - 1), tick=dve_tick)
                dve.bn_aggr(mv2[:, p, :], stats2[:, p, :]).then_inc(mv2_ready, 1)

            def add_gate_bias(t, p):
                after(dve, (l_made, t + 1), tick=dve_tick)
                dve.tensor_tensor(logit[:, p, :], pr[:, 0:8], bg[:, :], ALU.add).then_inc(choose_step, 1)

            def sort_logits(t, p):
                after(dve, (choose_step, 4 * t + 1), tick=dve_tick)
                dve.max(top8[:, p, :], logit[:, p, :]).then_inc(choose_step, 1)

            def find_experts(t, p):
                after(dve, (choose_step, 4 * t + 2), tick=dve_tick)
                dve.max_index(chosen[:, p, :], top8[:, p, :], logit[:, p, :]).then_inc(choose_step, 1)

            def mark_experts(t, p):
                after(dve, (choose_step, 4 * t + 3), tick=dve_tick)
                dve.tensor_tensor(hot_kept[:, t, :, :], chosen[:, p, 0:2].rearrange("p (k x) -> p k x", x=1).to_broadcast([P, 2, 8]),
                                  expert_no[:, :].rearrange("p (x e) -> p x e", x=1).to_broadcast([P, 2, 8]), ALU.is_equal).then_inc(choose_step, 1)

            def add_marks(t, p):
                after(dve, (choose_step, 4 * t + 4), (r_made, t), tick=dve_tick)
                dve.tensor_tensor(both[:, p, :], hot_kept[:, t, 0, :], hot_kept[:, t, 1, :], ALU.add).then_inc(both_ready, 1)

            def add_region(t, p):
                after(dve, (r_made, t + 1), tick=dve_tick)
                dve.tensor_tensor(rank[:, p, :], pr[:, 0:8], region_at[:, :], ALU.add).then_inc(place_step, 1)
                dve.tensor_tensor(seen[:, :], seen[:, :], both[:, p, :], ALU.add).then_inc(place_step, 1)

            def pick_ranks(t, p):
                after(dve, (place_step, 5 * t + 2), tick=dve_tick)
                dve.tensor_copy(seenb[:, :], seen[:, :]).then_inc(place_step, 1)
                dve.tensor_tensor(picked[:, p, :, :], hot_kept[:, t, :, :], rank[:, p, :].rearrange("p (x e) -> p x e", x=1).to_broadcast([P, 2, 8]), ALU.mult).then_inc(place_step, 1)

            def sum_ranks(t, p):
                after(dve, (place_step, 5 * t + 4), tick=dve_tick)
                dve.tensor_reduce(at_kept[:, t, :], picked[:, p, :, :], AX.X, ALU.add).then_inc(place_step, 1)

            def round_ranks(t, p):
                after(dve, (place_step, 5 * t + 5), (scattered[p], 2 * slot_full(t, p) - 32), tick=dve_tick)
                dve.tensor_copy(ati[:, p, :], at_kept[:, t, :]).then_inc(at_ready, 1)

            pipelined(dve, TILES, [(keep_q, 1), (add_region, 5), (pick_ranks, 5), (add_residual, 3), (sum_ranks, 5), (sum_x, 0), (round_ranks, 5), (sum_x1, 3), (average_x, 0), (average_x1, 3), (add_gate_bias, 4), (max_scores, 1), (sort_logits, 4), (shift_scores, 1), (find_experts, 4), (invert_sums, 2), (keep_attn, 2), (mark_experts, 4), (keep_k, 0), (add_marks, 4)])

            steps = [0]

            def then(ins):
                steps[0] += 1
                ins.then_inc(table_step, 1)
                dve.wait_ge(table_step, steps[0])

            def spread(ap, rows):
                return ap.rearrange("p (x e) -> p x e", x=1).to_broadcast([P, rows, 8])

            def each(ap, n):
                return ap.rearrange("p (e x) -> p e x", x=1).to_broadcast([P, ap.shape[1], n])

            dve.wait_ge(count_made, 1)
            then(dve.tensor_copy(counts[:, :], pr[:, 0:8]))
            then(dve.tensor_tensor(padf[:, :], counts[:, :], region_at[:, :], ALU.add))
            dve.tensor_copy(padi[:, :], padf[:, :]).then_inc(pad_ready, 1)
            then(dve.tensor_tensor(over[:, :, :], each(counts[:, :], 16), k128[:, :, :], ALU.is_gt))
            then(dve.tensor_reduce(nblk[:, :], over[:, :, :], AX.X, ALU.add))
            then(dve.tensor_tensor(lower[:, :, :], below[:, :, :], spread(nblk[:, :], 8), ALU.mult))
            then(dve.tensor_reduce(start[:, :], lower[:, :, :], AX.X, ALU.add))
            then(dve.tensor_tensor(end[:, :], start[:, :], nblk[:, :], ALU.add))
            then(dve.tensor_scalar(shared["last"][:, :], end[:, 7:8], -1.0, None, ALU.add))
            then(dve.tensor_scalar(blk[:, :], blk[:, :], shared["last"][:, 0:1], None, ALU.min))
            then(dve.tensor_tensor(passed[:, :, :], each(blk[:, :], 8), spread(end[:, :], BLOCKS), ALU.is_ge))
            then(dve.tensor_reduce(bexp[:, :], passed[:, :, :], AX.X, ALU.add))
            then(dve.tensor_tensor(passed[:, :, :], passed[:, :, :], spread(nblk[:, :], BLOCKS), ALU.mult))
            then(dve.tensor_reduce(bstart[:, :], passed[:, :, :], AX.X, ALU.add))
            then(dve.tensor_tensor(bstart[:, :], blk[:, :], bstart[:, :], ALU.subtract))
            then(dve.tensor_scalar(bstart[:, :], bstart[:, :], float(P), None, ALU.mult))
            then(dve.scalar_tensor_tensor(table[:, 0, :], bexp[:, :], float(REGION), bstart[:, :], ALU.mult, ALU.add))
            then(dve.tensor_scalar(table[:, 1, :], bexp[:, :], float(DIM), None, ALU.mult))
            then(dve.tensor_copy(shared["table"][:, :, :], table[:, :, :]))
            then(dve.scalar_tensor_tensor(shift[:, :], start[:, :], float(P), region_at[:, :], ALU.mult, ALU.subtract))
            then(dve.tensor_tensor(moved[:, :, :], hot_kept[:, :, :, :].rearrange("p t k e -> p (t k) e"), spread(shift[:, :], 2 * TILES), ALU.mult))
            then(dve.tensor_reduce(at_kept2[:, :], moved[:, :, :], AX.X, ALU.add))
            then(dve.tensor_tensor(at_kept2[:, :], at_kept2[:, :], at_kept[:, :, :].rearrange("p t k -> p (t k)"), ALU.add))
            then(dve.tensor_copy(shared["y_at"][:, :], at_kept2[:, :]))


def identity(pool, buf, zeroed, made):
    pool.memset(buf[:, :], 0.0).then_inc(zeroed, 1)
    pool.wait_ge(zeroed, 1)
    pool.affine_select(out=buf[:, :], in_=buf[:, :], compare_op=ALU.not_equal, fill=1.0,
                       base=0, pattern=[[-1, P]], channel_multiplier=1).then_inc(made, 1)


def expert_phase(nc, shared, b_e):
    with ExitStack() as stack:
        c = Ctx(nc, stack, "b_")
        sb, pb, sem = c.sb, c.pb, c.sem
        bias, ident = sb("bias", [P, EXPERTS * DIM]), sb("ident", [P, P])
        rows, biased, result = sb("rows", [P, 2, DIM]), sb("biased", [P, 2, DIM]), sb("result", [P, 2, DIM])
        rowsT_hi, rowsT_lo = sb("rowsT_hi", [P, 2, DIM], F32R), sb("rowsT_lo", [P, 2, DIM], F32R)
        pt, py = [pb(f"pt{i}") for i in range(2)], [pb(f"py{i}") for i in range(2)]
        bias_loaded, zeroed, ident_made = sem("bias_loaded"), sem("zeroed"), sem("ident_made")
        rows_loaded, stored = [sem(f"rows_loaded{i}") for i in range(2)], [sem(f"stored{i}") for i in range(2)]
        t_made, hi_kept, lo_kept, y_made = sem("t_made"), sem("hi_kept"), sem("lo_kept"), sem("y_made")
        biased_made, result_made = sem("biased_made"), sem("result_made")
        sp_tick, act_tick, pe_tick, dve_tick = (sem(e + "_tick") for e in ("sp", "act", "pe", "dve"))
        w_hi, w_lo, table = shared["w_hi"], shared["w_lo"], shared["table"]
        y_v = shared["ys"].rearrange("(b p) h -> b p h", p=P)
        stack.callback(c.clear)
        block = stack.enter_context(nc.Block())

        @block.sync
        def _(sp):
            def load(b, p):
                row = sp.value_load(table[0:1, 0, bass.ds(b, 1)], min_val=0, max_val=EXPERTS * REGION - P)
                after(sp, (t_made, b - 1), tick=sp_tick)
                sp.dma_start(rows[:, p, :], shared["xs"][bass.ds(row, P), :]).then_inc(rows_loaded[p], 16)
                if isinstance(b, int) and b == 1:
                    sp.dma_start(bias[:, :], b_e.rearrange("e h -> (e h)").partition_broadcast(P)).then_inc(bias_loaded, 16)

            def store(b, p):
                after(sp, (result_made, b + 1), tick=sp_tick)
                sp.dma_start(y_v[b, :, :], result[:, p, :]).then_inc(stored[p], 16)

            pipelined(sp, BLOCKS, [(load, 0), (store, 3)])
            for i in range(2):
                sp.wait_ge(stored[i], 16 * ((BLOCKS + 1 - i) // 2))

        @block.gpsimd
        def _(pool):
            identity(pool, ident, zeroed, ident_made)

        @block.tensor
        def _(pe):
            pe.wait_ge(ident_made, 1)

            def transpose_rows(b, p):
                after(pe, (rows_loaded[p], slot_full(b, p)), (lo_kept, b - 1), tick=pe_tick)
                for k in range(KD):
                    mm = pe.transpose(pt[p][:, P * k:P * k + P], rows[:, p, P * k:P * k + P], ident[:, :])
                mm.then_inc(t_made, 1)

            def multiply(b, p):
                at = pe.value_load(table[0:1, 1, bass.ds(b, 1)], min_val=0, max_val=(EXPERTS - 1) * DIM)
                after(pe, (hi_kept, b + 1), (lo_kept, b + 1), (biased_made, b - 1), tick=pe_tick)
                for k in range(KD):
                    hi, lo = rowsT_hi[:, p, P * k:P * k + P], rowsT_lo[:, p, P * k:P * k + P]
                    cols = bass.ds(at * KD + k * DIM, DIM)
                    pe.matmul(py[p][:, :], hi, w_hi[:, cols], start=k == 0, stop=False)
                    pe.matmul(py[p][:, :], hi, w_lo[:, cols], start=False, stop=False)
                    mm = pe.matmul(py[p][:, :], lo, w_hi[:, cols], start=False, stop=k == KD - 1)
                mm.then_inc(y_made, 1)

            pipelined(pe, BLOCKS, [(transpose_rows, 0), (multiply, 1)])

        @block.scalar
        def _(act):
            def keep_high(b, p):
                after(act, (t_made, b + 1), (y_made, b - 1), tick=act_tick)
                act.activation(rowsT_hi[:, p, :], pt[p][:, :], ACT.Copy).then_inc(hi_kept, 1)

            def rectify(b, p):
                after(act, (biased_made, b + 1), (stored[p], slot_full(b, p) - 16), tick=act_tick)
                act.activation(result[:, p, :], biased[:, p, :], ACT.Relu, scale=0.5).then_inc(result_made, 1)

            pipelined(act, BLOCKS, [(keep_high, 0), (rectify, 1)])

        @block.vector
        def _(dve):
            dve.wait_ge(bias_loaded, 16)

            def keep_low(b, p):
                after(dve, (hi_kept, b + 1), (y_made, b - 1), tick=dve_tick)
                dve.tensor_tensor(rowsT_lo[:, p, :], pt[p][:, :], rowsT_hi[:, p, :].bitcast(F32), ALU.subtract).then_inc(lo_kept, 1)

            def add_bias(b, p):
                at = dve.value_load(table[0:1, 1, bass.ds(b, 1)], min_val=0, max_val=(EXPERTS - 1) * DIM)
                after(dve, (y_made, b + 1), (result_made, b - 1), tick=dve_tick)
                dve.tensor_tensor(biased[:, p, :], py[p][:, :], bias[:, bass.ds(at, DIM)], ALU.add).then_inc(biased_made, 1)

            pipelined(dve, BLOCKS, [(keep_low, 0), (add_bias, 1)])


GUC = 2 * KD * INTER // TILES


def layer1_phase(nc, shared, a):
    with ExitStack() as stack:
        c = Ctx(nc, stack, "c_")
        sb, pb, sem = c.sb, c.pb, c.sem
        proj_hi, proj_lo = sb("proj_hi", [P, 2, KD * DIM], F32R), sb("proj_lo", [P, 2, KD * DIM], F32R)
        wk, wv = sb("wk", [P, KD, P]), sb("wv", [P, KD, P])
        ident, minus_half, own_head = sb("ident", [P, P]), sb("minus_half", [P, 1]), sb("own_head", [P, KVH])
        stage = sb("stage", [P, 2, 1024])
        x_in, x_out, xn, q_rows, qT, attn, ctxT = (sb(n, [P, 2, DIM]) for n in ("x_in", "x_out", "xn", "q_rows", "qT", "attn", "ctxT"))
        y_in, y_at = sb("y_in", [P, 2, 2, DIM]), sb("y_at", [P, 2, 2], I32)
        xT_hi, xT_lo, aT_hi, aT_lo = (sb(n, [P, 2, DIM], F32R) for n in ("xT_hi", "xT_lo", "aT_hi", "aT_lo"))
        kT, keys, values = sb("kT", [P, 2, P]), sb("keys", [P, 2, 2, DIM]), sb("values", [P, 2, 2, 4, 2, HD + 1])
        score, probT = sb("score", [P, 2, DIM]), sb("probT", [P, 2, DIM])
        smax, rsum = sb("smax", [P, 2, KVH]), sb("rsum", [P, 2, 2, KVH, 1])
        stats, mv, rstd = sb("stats", [P, 2, 6]), sb("mv", [P, 2, 2]), sb("rstd", [P, 2, 2])
        n_out, stats3, mv3, rstd3 = sb("n_out", [P, 2, DIM]), sb("stats3", [P, 2, 6]), sb("mv3", [P, 2, 2]), sb("rstd3", [P, 2, 2])
        ps, pt, po = ([pb(f"{n}{i}") for i in range(2)] for n in ("ps", "pt", "po"))
        pg, ph = pb("pg"), pb("ph")

        names = ("zeroed const_made weights_loaded proj_hi_made proj_lo_made gu_hi gu_lo x2_added x2_ready stat_step mv_ready rs_step "
                 "rs_ready xn_ready xt_made xhi_kept xlo_kept q_made q_kept kv_made kt_kept v_kept keys_ready s_made max_step "
                 "q_rows_kept qt_made s_shifted exp_done pt_made pt_kept o_made sum_step o_kept at_made ahi_kept alo_kept w_made x3_ready yat_ready")
        (zeroed, const_made, weights_loaded, proj_hi_made, proj_lo_made, gu_hi, gu_lo, x2_added, x2_ready, stat_step, mv_ready, rs_step,
         rs_ready, xn_ready, xt_made, xhi_kept, xlo_kept, q_made, q_kept, kv_made, kt_kept, v_kept, keys_ready, s_made, max_step,
         q_rows_kept, qt_made, s_shifted, exp_done, pt_made, pt_kept, o_made, sum_step, o_kept, at_made, ahi_kept, alo_kept, w_made, x3_ready,
         yat_ready) = (sem(n) for n in names.split())
        stat3_step, mv3_ready, rs3_step, rs3_ready, n_ready = (sem(n) for n in ("stat3_step", "mv3_ready", "rs3_step", "rs3_ready", "n_ready"))
        n_stored = [sem(f"n_stored{i}") for i in range(2)]
        proj_loaded = [sem(f"proj_loaded{i}") for i in range(4)]
        x1_loaded, ctx_loaded, y_loaded, gu_loaded, x2_stored, x2_loaded, x3_stored = (
            [sem(f"{n}{i}") for i in range(2)] for n in ("x1_loaded", "ctx_loaded", "y_loaded", "gu_loaded", "x2_stored", "x2_loaded", "x3_stored"))
        sp_tick, act_tick, pool_tick, pe_tick, dve_tick = (sem(e + "_tick") for e in ("sp", "act", "pool", "pe", "dve"))
        N_CONST = 6
        stack.callback(c.clear)
        block = stack.enter_context(nc.Block())
        wq_v = a["Wq"].rearrange("(k p) n -> p k n", p=P)
        wo_v = a["Wo"].rearrange("(k p) n -> p k n", p=P)

        @block.sync
        def _(sp):
            for n in range(4):
                if n >= 2:
                    sp.wait_ge(proj_lo_made, n - 1)
                src = (wq_v, wo_v)[n // 2][:, 2 * (n % 2):2 * (n % 2) + 2, :]
                sp.dma_start(stage[:, n % 2, :].rearrange("p (k n) -> p k n", k=2), src).then_inc(proj_loaded[n], 16)
                if n == 1:
                    sp.dma_start(wk[:, :, :], a["Wk"].rearrange("(k p) n -> p k n", p=P)).then_inc(weights_loaded, 16)
                    sp.dma_start(wv[:, :, :], a["Wv"].rearrange("(k p) n -> p k n", p=P)).then_inc(weights_loaded, 16)

            def load_x1(t, p):
                after(sp, (xn_ready, t - 1), (x2_stored[p], slot_full(t, p) - 16), tick=sp_tick)
                sp.dma_start(x_in[:, p, :], shared["x1"][t, :, :]).then_inc(x1_loaded[p], 16)

            def load_ctx(t, p):
                after(sp, (kv_made, t - 1), tick=sp_tick)
                sp.dma_start(ctxT[:, p, :], a["ctxT"][t, :, :]).then_inc(ctx_loaded[p], 16)

            def load_gate_up(t, p):
                after(sp, (gu_lo, t - 1), tick=sp_tick)
                if isinstance(t, int) and t < 2:
                    sp.wait_ge(proj_lo_made, 3 + t)
                sp.dma_start(stage[:, p, 0:GUC], a["gate_up"][t, :, :]).then_inc(gu_loaded[p], 16)

            def store_x2(t, p):
                after(sp, (x2_ready, t + 1), tick=sp_tick)
                sp.dma_start(shared["x2"][t, :, :], x_in[:, p, :]).then_inc(x2_stored[p], 16)

            def load_x2(t, p):
                after(sp, (x2_stored[p], slot_full(t, p)), (x3_stored[p], slot_full(t, p) - 16), (n_ready, t - 1), tick=sp_tick)
                sp.dma_start(x_out[:, p, :], shared["x2"][t, :, :]).then_inc(x2_loaded[p], 16)

            def store_x3(t, p):
                after(sp, (x3_ready, t + 1), tick=sp_tick)
                sp.dma_start(shared["x3"][t, :, :], x_out[:, p, :]).then_inc(x3_stored[p], 16)

            def store_norm(t, p):
                after(sp, (n_ready, t + 1), tick=sp_tick)
                sp.dma_start(shared["n3"][t, :, :], n_out[:, p, :]).then_inc(n_stored[p], 16)

            pipelined(sp, TILES, [(load_ctx, 1), (load_gate_up, 1), (store_x2, 2), (store_x3, 5), (store_norm, 5), (load_x2, 3), (load_x1, 0)])
            for i in range(2):
                sp.wait_ge(n_stored[i], 8 * TILES)
                sp.wait_ge(x3_stored[i], 8 * TILES)

        @block.gpsimd
        def _(pool):
            pool.memset(keys[:], 0.0).then_inc(const_made, 1)
            pool.memset(minus_half[:, :], -0.5).then_inc(const_made, 1)
            pool.memset(values[:], 0.0).then_inc(zeroed, 1)
            pool.memset(ident[:, :], 0.0).then_inc(zeroed, 1)
            pool.memset(own_head[:, :], 1.0).then_inc(zeroed, 1)
            pool.wait_ge(zeroed, 3)
            for r in range(2):
                pool.memset(values[64 * r:64 * r + 64, :, :, :, r, HD:HD + 1], 1.0).then_inc(const_made, 1)
                pool.wait_ge(const_made, 3 + r)
            pool.affine_select(out=ident[:, :], in_=ident[:, :], compare_op=ALU.not_equal, fill=1.0,
                               base=0, pattern=[[-1, P]], channel_multiplier=1).then_inc(const_made, 1)
            pool.affine_select(out=own_head[:, :], in_=own_head[:, :], compare_op=ALU.is_ge, fill=0.0,
                               base=0, pattern=[[-HD, KVH]], channel_multiplier=1).then_inc(zeroed, 1)
            pool.wait_ge(zeroed, 4)
            pool.affine_select(out=own_head[:, :], in_=own_head[:, :], compare_op=ALU.is_ge, fill=0.0,
                               base=HD - 1, pattern=[[HD, KVH]], channel_multiplier=-1).then_inc(const_made, 1)
            pool.wait_ge(const_made, N_CONST)

            def gather(t, p):
                after(pool, (x2_ready, t - 1), (y_loaded[p], 2 * slot_full(t, p) - 32), tick=pool_tick)
                pool.tensor_copy(y_at[:, p, :], shared["y_at"][:, bass.ds(2 * t, 2)]).then_inc(yat_ready, 1)
                after(pool, (yat_ready, t + 1), tick=pool_tick)
                for k in range(2):
                    pool.indirect_dma_start(out=y_in[:, p, k, :], out_offset=None, in_=shared["ys"],
                                            in_offset=bass.IndirectOffsetOnAxis(ap=y_at[:, p, k:k + 1], axis=0)).then_inc(y_loaded[p], 16)

            def add_first(t, p):
                after(pool, (x1_loaded[p], slot_full(t, p)), (y_loaded[p], 2 * slot_full(t, p)), tick=pool_tick)
                pool.tensor_tensor(x_in[:, p, :], x_in[:, p, :], y_in[:, p, 0, :], ALU.add).then_inc(x2_added, 1)

            def inverse_deviation(t, m, r, step, done):
                pool.tensor_scalar(m[:, 1:2], m[:, 1:2], EPS, None, ALU.add).then_inc(step, 1)
                after(pool, (step, 2 * t + 1), tick=pool_tick)
                pool.tensor_tensor(r[:, 0:1], m[:, 1:2], minus_half[:, :], ALU.pow).then_inc(step, 1)
                after(pool, (step, 2 * t + 2), tick=pool_tick)
                pool.tensor_scalar(r[:, 1:2], m[:, 0:1], -1.0, r[:, 0:1], ALU.mult, ALU.mult).then_inc(done, 1)

            def scale_x2(t, p):
                after(pool, (mv_ready, t + 1), (xn_ready, t - 1), tick=pool_tick)
                inverse_deviation(t, mv[:, p, :], rstd[:, p, :], rs_step, rs_ready)

            def scale_x3(t, p):
                after(pool, (mv3_ready, t + 1), (n_ready, t - 1), tick=pool_tick)
                inverse_deviation(t, mv3[:, p, :], rstd3[:, p, :], rs3_step, rs3_ready)

            def spread_keys(t, p):
                after(pool, (kt_kept, t + 1), (s_made, 4 * t - 4), tick=pool_tick)
                for b in range(2):
                    pool.tensor_tensor(keys[:, p, b, :].rearrange("p (h e) -> p h e", h=KVH),
                                       kT[:, p, 64 * b:64 * b + 64].rearrange("p (x e) -> p x e", x=1).to_broadcast([P, KVH, 64]),
                                       own_head[:, :].rearrange("p (h x) -> p h x", x=1).to_broadcast([P, KVH, 64]), ALU.mult).then_inc(keys_ready, 1)

            def low_part(t, p):
                after(pool, (gu_hi, t + 1), tick=pool_tick)
                dst = bass.ds(GUC * t, GUC)
                pool.tensor_tensor(shared["gu_lo"][:, dst], stage[:, p, 0:GUC], shared["gu_hi"][:, dst].bitcast(F32), ALU.subtract).then_inc(gu_lo, 1)

            pipelined(pool, TILES, [(add_first, 1), (scale_x2, 1), (scale_x3, 4), (gather, 0), (low_part, 2), (spread_keys, 2)])

        @block.scalar
        def _(act):
            for n in range(4):
                act.wait_ge(proj_loaded[n], 16)
                act.activation(proj_hi[:, n // 2, 1024 * (n % 2):1024 * (n % 2) + 1024], stage[:, n % 2, :], ACT.Copy).then_inc(proj_hi_made, 1)

            def keep_kT(t, p):
                after(act, (kv_made, t + 1), (keys_ready, 2 * t - 2), tick=act_tick)
                act.activation(kT[:, p, :], pg[:, 0:P], ACT.Copy).then_inc(kt_kept, 1)

            def norm_x(t, p):
                after(act, (rs_ready, t + 1), (xt_made, t - 1), tick=act_tick)
                act.activation(xn[:, p, :], x_in[:, p, :], ACT.Identity, scale=rstd[:, p, 0:1], bias=rstd[:, p, 1:2]).then_inc(xn_ready, 1)

            def norm_x3(t, p):
                after(act, (rs3_ready, t + 1), (n_stored[p], slot_full(t, p) - 16), tick=act_tick)
                act.activation(n_out[:, p, :], x_out[:, p, :], ACT.Identity, scale=rstd3[:, p, 0:1], bias=rstd3[:, p, 1:2]).then_inc(n_ready, 1)

            def keep_high_x(t, p):
                after(act, (xt_made, t + 1), (q_made, t - 1), tick=act_tick)
                act.activation(xT_hi[:, p, :], pg[:, :], ACT.Copy).then_inc(xhi_kept, 1)

            def keep_q_rows(t, p):
                after(act, (q_made, t + 1), (qt_made, t - 1), tick=act_tick)
                act.activation(q_rows[:, p, :], ph[:, :], ACT.Copy).then_inc(q_rows_kept, 1)

            def keep_q(t, p):
                after(act, (qt_made, t + 1), (s_made, 4 * t - 4), tick=act_tick)
                act.activation(qT[:, p, :].rearrange("p (b g q) -> p g b q", b=2, g=GROUP),
                               ph[:, :].rearrange("p (g b q) -> p g b q", g=GROUP, b=2), ACT.Copy).then_inc(q_kept, 1)

            def exponent(i):
                def stage_(t, p):
                    after(act, (s_shifted, 4 * t + i + 1), tick=act_tick)
                    act.activation(score[:, i % 2, :], score[:, i % 2, :], ACT.Exp, scale=SCALE1).then_inc(exp_done, 1)
                return stage_

            def keep_probT(i):
                def stage_(t, p):
                    after(act, (pt_made, 4 * t + i + 1), (o_made, 4 * t + i - 1), tick=act_tick)
                    act.activation(probT[:, i % 2, :], pt[i % 2][:, :], ACT.Copy).then_inc(pt_kept, 1)
                return stage_

            def keep_high_attn(t, p):
                after(act, (at_made, t + 1), (w_made, t - 1), tick=act_tick)
                act.activation(aT_hi[:, p, :].rearrange("p (g b q) -> p b g q", g=GROUP, b=2),
                               pg[:, :].rearrange("p (b g q) -> p b g q", b=2, g=GROUP), ACT.Copy).then_inc(ahi_kept, 1)

            def high_part(t, p):
                after(act, (gu_loaded[p], slot_full(t, p)), tick=act_tick)
                act.activation(shared["gu_hi"][:, bass.ds(GUC * t, GUC)], stage[:, p, 0:GUC], ACT.Copy).then_inc(gu_hi, 1)

            pipelined(act, TILES, [(keep_high_attn, 4), (exponent(0), 3), (exponent(1), 3), (keep_high_x, 2), (keep_probT(0), 3),
                                   (exponent(2), 3), (keep_probT(1), 3), (exponent(3), 3), (keep_kT, 2), (keep_probT(2), 3), (norm_x3, 4),
                                   (keep_probT(3), 3), (norm_x, 1), (keep_q_rows, 2), (high_part, 1), (keep_q, 2)])

        @block.tensor
        def _(pe):
            pe.wait_ge(const_made, N_CONST)
            pe.wait_ge(weights_loaded, 32)
            pe.wait_ge(proj_lo_made, 4)

            def transpose_x(t, p):
                after(pe, (ahi_kept, t - 1), (alo_kept, t - 1), (kt_kept, t), (v_kept, 4 * t), (xn_ready, t + 1), tick=pe_tick)
                for k in range(KD):
                    mm = pe.transpose(pg[:, P * k:P * k + P], xn[:, p, P * k:P * k + P], ident[:, :])
                mm.then_inc(xt_made, 1)

            def make_q(t, p):
                after(pe, (xhi_kept, t + 1), (xlo_kept, t + 1), (x3_ready, t - 1), tick=pe_tick)
                for k in range(KD):
                    hi, lo = xT_hi[:, p, P * k:P * k + P], xT_lo[:, p, P * k:P * k + P]
                    cols = slice(DIM * k, DIM * k + DIM)
                    pe.matmul(ph[:, :], hi, proj_hi[:, 0, cols], start=k == 0, stop=False)
                    pe.matmul(ph[:, :], hi, proj_lo[:, 0, cols], start=False, stop=False)
                    mm = pe.matmul(ph[:, :], lo, proj_hi[:, 0, cols], start=False, stop=k == KD - 1)
                mm.then_inc(q_made, 1)

            def transpose_q(t, p):
                after(pe, (q_rows_kept, t + 1), tick=pe_tick)
                for g in range(GROUP):
                    mm = pe.transpose(ph[:, P * g:P * g + P], q_rows[:, p, P * g:P * g + P], ident[:, :])
                mm.then_inc(qt_made, 1)

            def make_kv(t, p):
                after(pe, (ctx_loaded[p], slot_full(t, p)), (xhi_kept, t + 1), (xlo_kept, t + 1), tick=pe_tick)
                rows = ctxT[:, p, :].rearrange("p (k n) -> p k n", k=KD)
                for k in range(KD):
                    pe.matmul(pg[:, 0:P], wk[:, k, :], rows[:, k, :], start=k == 0, stop=k == KD - 1)
                for k in range(KD):
                    mm = pe.matmul(pg[:, P:2 * P], rows[:, k, :], wv[:, k, :], start=k == 0, stop=k == KD - 1)
                mm.then_inc(kv_made, 1)

            def scores(i):
                def stage_(t, p):
                    after(pe, (q_kept, t + 1), (keys_ready, 2 * t + 2), (s_shifted, 4 * t + i - 1), tick=pe_tick)
                    pe.matmul(ps[i % 2][:, :], qT[:, p, P * i:P * i + P], keys[:, p, i // 2, :], start=True, stop=True).then_inc(s_made, 1)
                return stage_

            def transpose_probs(i):
                def stage_(t, p):
                    after(pe, (exp_done, 4 * t + i + 1), (pt_kept, 4 * t + i - 1), tick=pe_tick)
                    for j in range(4):
                        mm = pe.transpose(pt[i % 2][:, P * j:P * j + P], score[:, i % 2, P * j:P * j + P], ident[:, :])
                    mm.then_inc(pt_made, 1)
                return stage_

            def attend(i):
                def stage_(t, p):
                    b = i // 2
                    after(pe, (pt_kept, 4 * t + i + 1), (o_kept, 2 * t + b - 1), tick=pe_tick)
                    for j in range(4):
                        at = 136 * (i % 2) + 34 * j
                        mm = pe.matmul(po[b][:, at:at + 34], probT[:, i % 2, P * j:P * j + P],
                                       values[:, p, b, j, :, :].rearrange("p r d -> p (r d)"), start=True, stop=True)
                    mm.then_inc(o_made, 1)
                return stage_

            def transpose_attn(t, p):
                after(pe, (o_kept, 2 * t + 2), (kt_kept, upto(t + 2, TILES)), (v_kept, 4 * upto(t + 2, TILES)), tick=pe_tick)
                for i in range(4):
                    mm = pe.transpose(pg[:, P * i:P * i + P], attn[:, p, P * i:P * i + P], ident[:, :])
                mm.then_inc(at_made, 1)

            def project(t, p):
                after(pe, (ahi_kept, t + 1), (alo_kept, t + 1), (q_kept, upto(t + 2, TILES)), tick=pe_tick)
                for g in range(GROUP):
                    hi, lo = aT_hi[:, p, P * g:P * g + P], aT_lo[:, p, P * g:P * g + P]
                    cols = slice(DIM * g, DIM * g + DIM)
                    pe.matmul(ph[:, :], hi, proj_hi[:, 1, cols], start=g == 0, stop=False)
                    pe.matmul(ph[:, :], hi, proj_lo[:, 1, cols], start=False, stop=False)
                    mm = pe.matmul(ph[:, :], lo, proj_hi[:, 1, cols], start=False, stop=g == GROUP - 1)
                mm.then_inc(w_made, 1)

            pipelined(pe, TILES, [(scores(0), 3), (transpose_attn, 4), (scores(1), 3), (project, 4), (transpose_x, 2), (transpose_probs(0), 3),
                                  (scores(2), 3), (transpose_probs(1), 3), (scores(3), 3), (attend(0), 3), (make_kv, 2), (transpose_probs(2), 3),
                                  (attend(1), 3), (transpose_probs(3), 3), (make_q, 2), (attend(2), 3), (transpose_q, 2), (attend(3), 3)])

        @block.vector
        def _(dve):
            dve.wait_ge(const_made, N_CONST)
            for n in range(4):
                dve.wait_ge(proj_hi_made, n + 1)
                cols = slice(1024 * (n % 2), 1024 * (n % 2) + 1024)
                dve.tensor_tensor(proj_lo[:, n // 2, cols], stage[:, n % 2, :], proj_hi[:, n // 2, cols].bitcast(F32), ALU.subtract).then_inc(proj_lo_made, 1)

            def add_second(t, p):
                after(dve, (x2_added, t + 1), tick=dve_tick)
                dve.tensor_tensor(x_in[:, p, :], x_in[:, p, :], y_in[:, p, 1, :], ALU.add).then_inc(x2_ready, 1)

            def sum_x2(t, p):
                after(dve, (x2_ready, t + 1), tick=dve_tick)
                dve.bn_stats(stats[:, p, :], x_in[:, p, :]).then_inc(stat_step, 1)

            def average_x2(t, p):
                after(dve, (stat_step, t + 1), (rs_ready, t - 1), tick=dve_tick)
                dve.bn_aggr(mv[:, p, :], stats[:, p, :]).then_inc(mv_ready, 1)

            def keep_low_x(t, p):
                after(dve, (xhi_kept, t + 1), (q_made, t - 1), tick=dve_tick)
                dve.tensor_tensor(xT_lo[:, p, :], pg[:, :], xT_hi[:, p, :].bitcast(F32), ALU.subtract).then_inc(xlo_kept, 1)

            def keep_values(t, p):
                after(dve, (kt_kept, t + 1), (o_made, 4 * t - 4), tick=dve_tick)
                for r in range(2):
                    for b in range(2):
                        made = pg[64 * b:64 * b + 64, P:2 * P].rearrange("p (j r d) -> p j r d", j=4, r=2)
                        dve.tensor_copy(values[64 * r:64 * r + 64, p, b, :, r, 0:HD], made[:, :, r, :]).then_inc(v_kept, 1)

            def score_rows(i):
                return ps[i % 2][:, :].rearrange("p (h e) -> p h e", h=KVH)

            def max_scores(i):
                def stage_(t, p):
                    after(dve, (s_made, 4 * t + i + 1), tick=dve_tick)
                    dve.tensor_reduce(smax[:, i % 2, :], score_rows(i), AX.X, ALU.max).then_inc(max_step, 1)
                return stage_

            def shift_scores(i):
                def stage_(t, p):
                    after(dve, (max_step, 4 * t + i + 1), (pt_made, 4 * t + i - 1), tick=dve_tick)
                    peak = smax[:, i % 2, :].rearrange("p (h x) -> p h x", x=1).to_broadcast([P, KVH, 64])
                    dve.tensor_tensor(score[:, i % 2, :].rearrange("p (h e) -> p h e", h=KVH), score_rows(i), peak, ALU.subtract).then_inc(s_shifted, 1)
                return stage_

            def heads(b):
                return po[b][:, 0:272].rearrange("p (c h d) -> p c h d", c=2, h=KVH)

            def invert_sums(b):
                def stage_(t, p):
                    after(dve, (o_made, 4 * t + 2 * b + 2), tick=dve_tick)
                    dve.reciprocal(rsum[:, b, :, :, :], heads(b)[:, :, :, HD:HD + 1]).then_inc(sum_step, 1)
                return stage_

            def keep_attn(b):
                def stage_(t, p):
                    after(dve, (sum_step, 2 * t + b + 1), (at_made, t - 1), tick=dve_tick)
                    dve.tensor_tensor(attn[:, p, 256 * b:256 * b + 256].rearrange("p (c h d) -> p c h d", c=2, h=KVH), heads(b)[:, :, :, 0:HD],
                                      rsum[:, b, :, :, :].to_broadcast([P, 2, KVH, HD]), ALU.mult).then_inc(o_kept, 1)
                return stage_

            def keep_low_attn(t, p):
                after(dve, (ahi_kept, t + 1), (w_made, t - 1), tick=dve_tick)
                order = "p (g b q) -> p b g q"
                dve.tensor_tensor(aT_lo[:, p, :].rearrange(order, g=GROUP, b=2), pg[:, :].rearrange("p (b g q) -> p b g q", b=2, g=GROUP),
                                  aT_hi[:, p, :].bitcast(F32).rearrange(order, g=GROUP, b=2), ALU.subtract).then_inc(alo_kept, 1)

            def add_attn(t, p):
                after(dve, (w_made, t + 1), (x2_loaded[p], slot_full(t, p)), tick=dve_tick)
                dve.tensor_tensor(x_out[:, p, :], ph[:, :], x_out[:, p, :], ALU.add).then_inc(x3_ready, 1)

            def sum_x3(t, p):
                after(dve, (x3_ready, t + 1), tick=dve_tick)
                dve.bn_stats(stats3[:, p, :], x_out[:, p, :]).then_inc(stat3_step, 1)

            def average_x3(t, p):
                after(dve, (stat3_step, t + 1), (rs3_ready, t - 1), tick=dve_tick)
                dve.bn_aggr(mv3[:, p, :], stats3[:, p, :]).then_inc(mv3_ready, 1)

            pipelined(dve, TILES, [(max_scores(0), 3), (keep_low_attn, 4), (shift_scores(0), 3), (max_scores(1), 3), (add_second, 1),
                                   (shift_scores(1), 3), (sum_x2, 1), (add_attn, 4), (average_x2, 1), (keep_low_x, 2), (max_scores(2), 3),
                                   (sum_x3, 4), (shift_scores(2), 3), (average_x3, 4), (max_scores(3), 3), (shift_scores(3), 3), (keep_values, 2),
                                   (invert_sums(0), 3), (keep_attn(0), 3), (invert_sums(1), 3), (keep_attn(1), 3)])


def ffn_phase(nc, shared, a, out):
    TOK, GROUPS, LAST = TG * P, TILES // TG, NI - 1
    with ExitStack() as stack:
        c = Ctx(nc, stack, "d_")
        sb, pb, sem = c.sb, c.pb, c.sem
        down_hi, down_lo = sb("down_hi", [P, NI, DIM], F32R), sb("down_lo", [P, NI, DIM], F32R)
        ident = sb("ident", [P, P])
        b_gate, b_up, minus_gate, b_down = sb("b_gate", [P, NI]), sb("b_up", [P, NI]), sb("minus_gate", [P, NI]), sb("b_down", [P, DIM])
        stage, n_in, x_res = sb("stage", [P, 2, DIM]), sb("n_in", [P, TG, DIM]), sb("x_res", [P, TG, DIM])
        nT_hi, nT_lo = sb("nT_hi", [P, KD, TOK], F32R), sb("nT_lo", [P, KD, TOK], F32R)
        expo, hid = sb("expo", [P, 2, TOK]), sb("hid", [P, 2, TOK])
        hid_hi, hid_lo = sb("hid_hi", [P, 2, TOK], F32R), sb("hid_lo", [P, 2, TOK], F32R)
        pgate, pup = [pb(f"pgate{i}") for i in range(2)], [pb(f"pup{i}") for i in range(2)]
        pdown = [pb(f"pdown{i}") for i in range(TG)]
        tbank = (pgate[1], pup[1])
        names = ("zeroed ident_made bias_loaded minus_made down_hi_made down_lo_made t_made nhi_kept nlo_kept gate_made up_made "
                 "expo_made expo_step gated hid_made hi_made lo_made down_done res_biased y_ready")
        (zeroed, ident_made, bias_loaded, minus_made, down_hi_made, down_lo_made, t_made, nhi_kept, nlo_kept, gate_made, up_made,
         expo_made, expo_step, gated, hid_made, hi_made, lo_made, down_done, res_biased, y_ready) = (sem(n) for n in names.split())
        n_loaded, res_loaded, stored = ([sem(f"{n}{i}") for i in range(TG)] for n in ("n_loaded", "res_loaded", "stored"))
        down_loaded = [sem(f"down_loaded{i}") for i in range(2)]
        sp_tick, act_tick, pool_tick, pe_tick, dve_tick = (sem(e + "_tick") for e in ("sp", "act", "pool", "pe", "dve"))
        stack.callback(c.clear)
        block = stack.enter_context(nc.Block())
        out_v = out.rearrange("(t b) s d -> t (b s) d", b=2)
        gu_hi, gu_lo = shared["gu_hi"], shared["gu_lo"]

        def width(i):
            return min(P, INTER - P * i)

        def read_before(g, i):
            return NI * g + i - (1 if i else 0)

        @block.sync
        def _(sp):
            def load(g):
                for n in range(TG):
                    after(sp, (t_made, TG * (g - 1) + n + 1), tick=sp_tick)
                    sp.dma_start(n_in[:, n, :], shared["n3"][TG * g + n, :, :]).then_inc(n_loaded[n], 16)

            def load_residual(g):
                for n in range(TG):
                    after(sp, (stored[n], 16 * g), tick=sp_tick)
                    sp.dma_start(x_res[:, n, :], shared["x3"][TG * g + n, :, :]).then_inc(res_loaded[n], 16)

            load(0)
            for buf, b in ((b_gate, "b_gate"), (b_up, "b_up")):
                sp.dma_start(buf[:, 0:LAST], a[b + "_main"]).then_inc(bias_loaded, 16)
                sp.dma_start(buf[0:width(LAST), LAST:NI], a[b + "_rest"]).then_inc(bias_loaded, 16)
            sp.dma_start(b_down[:, :], a["b_down"].partition_broadcast(P)).then_inc(bias_loaded, 16)
            for i in range(NI):
                if i >= 2:
                    sp.wait_ge(down_lo_made, i - 1)
                sp.dma_start(stage[0:width(i), i % 2, :], a["w_down"][P * i:P * i + width(i), :]).then_inc(down_loaded[i % 2], 16)
            load_residual(0)
            with sp.Fori(1, GROUPS) as g:
                load(g)
                load_residual(g)

        @block.gpsimd
        def _(pool):
            identity(pool, ident, zeroed, ident_made)
            pool.wait_ge(bias_loaded, 80)
            pool.tensor_scalar(minus_gate[:, 0:LAST], b_gate[:, 0:LAST], -1.0, None, ALU.mult).then_inc(minus_made, 1)
            pool.wait_ge(minus_made, 1)
            pool.tensor_scalar(minus_gate[0:width(LAST), LAST:NI], b_gate[0:width(LAST), LAST:NI], -1.0, None, ALU.mult).then_inc(minus_made, 1)
            for i in range(NI):
                pool.wait_ge(down_hi_made, i + 1)
                w = width(i)
                pool.tensor_tensor(down_lo[0:w, i, :], stage[0:w, i % 2, :], down_hi[0:w, i, :].bitcast(F32), ALU.subtract).then_inc(down_lo_made, 1)

            def group(g):
                for n in range(TG):
                    after(pool, (res_loaded[n], 16 * g + 16), tick=pool_tick)
                    pool.tensor_tensor(x_res[:, n, :], x_res[:, n, :], b_down[:, :], ALU.add).then_inc(res_biased, 1)
                for n in range(TG):
                    after(pool, (y_ready, TG * g + n + 1), tick=pool_tick)
                    pool.dma_start(out_v[TG * g + n, :, :], x_res[:, n, :]).then_inc(stored[n], 16)

            pool.wait_ge(minus_made, 2)
            with pool.Fori(0, GROUPS) as g:
                group(g)
            for n in range(TG):
                pool.wait_ge(stored[n], 16 * GROUPS)

        @block.scalar
        def _(act):
            act.wait_ge(minus_made, 2)

            def keep_high_n(g, n):
                after(act, (t_made, TG * g + n + 1), tick=act_tick)
                act.activation(nT_hi[:, :, P * n:P * n + P], tbank[n % 2][:, :].rearrange("p (k n) -> p k n", k=KD), ACT.Copy).then_inc(nhi_kept, 1)

            def exponent(g, i):
                w = width(i)
                after(act, (gate_made, NI * g + i + 1), (gated, read_before(g, i)), tick=act_tick)
                act.activation(expo[0:w, i % 2, :], pgate[i % 2][0:w, :], ACT.Exp, scale=-1.0, bias=minus_gate[0:w, i:i + 1]).then_inc(expo_made, 1)

            def keep_high(g, i):
                w = width(i)
                after(act, (hid_made, NI * g + i + 1), (down_done, read_before(g, i)), tick=act_tick)
                act.activation(hid_hi[0:w, i % 2, :], hid[0:w, i % 2, :], ACT.Copy).then_inc(hi_made, 1)

            def group(g):
                keep_high_n(g, 0)
                keep_high_n(g, 1)
                if not isinstance(g, int):
                    keep_high(g - 1, LAST)
                keep_high_n(g, 2)
                keep_high_n(g, 3)
                for i in range(NI):
                    if isinstance(g, int):
                        w = width(i)
                        act.wait_ge(down_loaded[i % 2], 16 * (i // 2 + 1))
                        act.activation(down_hi[0:w, i, :], stage[0:w, i % 2, :], ACT.Copy).then_inc(down_hi_made, 1)
                    exponent(g, i)
                    if i:
                        keep_high(g, i - 1)

            group(0)
            with act.Fori(1, GROUPS) as g:
                group(g)
            keep_high(GROUPS - 1, LAST)

        @block.tensor
        def _(pe):
            pe.wait_ge(ident_made, 1)

            def transpose_n(g, n):
                free = (nlo_kept, TG * g + n - 1) if n >= 2 else ((gated, hid_made)[n], NI * g - 1)
                after(pe, (n_loaded[n], 16 * g + 16), free, tick=pe_tick)
                for k in range(KD):
                    mm = pe.transpose(tbank[n % 2][:, P * k:P * k + P], n_in[:, n, P * k:P * k + P], ident[:, :])
                mm.then_inc(t_made, 1)

            def product(g, i, which, bank, read, made):
                w = width(i)
                after(pe, (read, read_before(g, i)), tick=pe_tick)
                for k in range(KD):
                    cols = slice((which * KD + k) * INTER + P * i, (which * KD + k) * INTER + P * i + w)
                    pe.matmul(bank[0:w, :], gu_hi[:, cols], nT_hi[:, k, :], start=k == 0, stop=False)
                    pe.matmul(bank[0:w, :], gu_hi[:, cols], nT_lo[:, k, :], start=False, stop=False)
                    mm = pe.matmul(bank[0:w, :], gu_lo[:, cols], nT_hi[:, k, :], start=False, stop=k == KD - 1)
                mm.then_inc(made, 1)

            def down(g, i):
                w = width(i)
                after(pe, (hi_made, NI * g + i + 1), (lo_made, NI * g + i + 1), tick=pe_tick)
                if isinstance(g, int) and g == 0:
                    pe.wait_ge(down_lo_made, i + 1)
                for n in range(TG):
                    if i == 0:
                        after(pe, (y_ready, TG * (g - 1) + n + 1), tick=pe_tick)
                    hi, lo = hid_hi[0:w, i % 2, P * n:P * n + P], hid_lo[0:w, i % 2, P * n:P * n + P]
                    pe.matmul(pdown[n][:, :], hi, down_hi[0:w, i, :], start=i == 0, stop=False)
                    pe.matmul(pdown[n][:, :], hi, down_lo[0:w, i, :], start=False, stop=False)
                    mm = pe.matmul(pdown[n][:, :], lo, down_hi[0:w, i, :], start=False, stop=i == LAST)
                mm.then_inc(down_done, 1)

            def group(g):
                for n in range(TG):
                    transpose_n(g, n)
                if not isinstance(g, int):
                    down(g - 1, LAST)
                after(pe, (nlo_kept, TG * g + TG), tick=pe_tick)
                for i in range(NI):
                    product(g, i, 0, pgate[i % 2], gated, gate_made)
                    product(g, i, 1, pup[i % 2], hid_made, up_made)
                    if i:
                        down(g, i - 1)

            group(0)
            pe.wait_ge(down_lo_made, NI)
            with pe.Fori(1, GROUPS) as g:
                group(g)
            down(GROUPS - 1, LAST)

        @block.vector
        def _(dve):
            dve.wait_ge(minus_made, 2)

            def keep_low_n(g, n):
                after(dve, (nhi_kept, TG * g + n + 1), tick=dve_tick)
                cols = slice(P * n, P * n + P)
                dve.tensor_tensor(nT_lo[:, :, cols], tbank[n % 2][:, :].rearrange("p (k n) -> p k n", k=KD), nT_hi[:, :, cols].bitcast(F32),
                                  ALU.subtract).then_inc(nlo_kept, 1)

            def activate(g, i):
                w, n = width(i), NI * g + i
                e, h = expo[0:w, i % 2, :], hid[0:w, i % 2, :]
                after(dve, (expo_made, n + 1), tick=dve_tick)
                dve.tensor_scalar(e, e, 1.0, None, ALU.add).then_inc(expo_step, 1)
                after(dve, (expo_step, 2 * n + 1), tick=dve_tick)
                dve.reciprocal(e, e).then_inc(expo_step, 1)
                after(dve, (expo_step, 2 * n + 2), (hi_made, read_before(g, i)), (lo_made, read_before(g, i)), tick=dve_tick)
                dve.scalar_tensor_tensor(h, pgate[i % 2][0:w, :], b_gate[0:w, i:i + 1], e, ALU.add, ALU.mult).then_inc(gated, 1)
                after(dve, (gated, n + 1), (up_made, n + 1), tick=dve_tick)
                dve.scalar_tensor_tensor(h, pup[i % 2][0:w, :], b_up[0:w, i:i + 1], h, ALU.add, ALU.mult).then_inc(hid_made, 1)

            def keep_low(g, i):
                w = width(i)
                after(dve, (hi_made, NI * g + i + 1), (down_done, read_before(g, i)), tick=dve_tick)
                dve.tensor_tensor(hid_lo[0:w, i % 2, :], hid[0:w, i % 2, :], hid_hi[0:w, i % 2, :].bitcast(F32), ALU.subtract).then_inc(lo_made, 1)

            def finish(g):
                after(dve, (down_done, NI * g + NI), tick=dve_tick)
                for n in range(TG):
                    after(dve, (res_biased, TG * g + n + 1), tick=dve_tick)
                    dve.tensor_tensor(x_res[:, n, :], pdown[n][:, :], x_res[:, n, :], ALU.add).then_inc(y_ready, 1)

            def group(g):
                keep_low_n(g, 0)
                keep_low_n(g, 1)
                if not isinstance(g, int):
                    keep_low(g - 1, LAST)
                keep_low_n(g, 2)
                keep_low_n(g, 3)
                if not isinstance(g, int):
                    finish(g - 1)
                for i in range(NI):
                    activate(g, i)
                    keep_low(g, i) if i < LAST else None

            group(0)
            with dve.Fori(1, GROUPS) as g:
                group(g)
            keep_low(GROUPS - 1, LAST)
            finish(GROUPS - 1)


def build(nc, a, out, phases=4):
    with ExitStack() as stack:
        def sb(name, shape, dt=F32):
            return stack.enter_context(nc.sbuf_tensor(name, shape, dt))

        def dram(name, shape):
            return nc.dram_tensor(name, shape, F32, kind="Internal").ap()

        shared = {
            "xs": dram("expert_rows", [EXPERTS * REGION, DIM]), "ys": dram("expert_results", [BLOCKS * P, DIM]),
            "x1": dram("x_after_attention0", [TILES, P, DIM]), "x3": dram("x_after_attention1", [TILES, P, DIM]),
            "n3": dram("norm_after_attention1", [TILES, P, DIM]),
            "last": sb("last", [P, 1]), "table": sb("table", [P, 2, BLOCKS], I32), "y_at": sb("y_at", [P, 2 * TILES], I32),
        }
        shared["x2"] = dram("x_after_experts", [TILES, P, DIM])
        with ExitStack() as moe:
            shared["w_hi"] = moe.enter_context(nc.sbuf_tensor("expert_w_hi", [P, EXPERTS * EW], F32R))
            shared["w_lo"] = moe.enter_context(nc.sbuf_tensor("expert_w_lo", [P, EXPERTS * EW], F32R))
            layer0_phase(nc, shared, {k: a[v] for k, v in dict(
                x="x", ctx="ctx_4096", Wq="L0_xattn_Wq", bq="L0_xattn_bq", Wk="L0_xattn_Wk", bk="L0_xattn_bk",
                Wv="L0_xattn_Wv", bv="L0_xattn_bv", Wo="L0_xattn_Wo", bo="L0_xattn_bo",
                W_gate="L0_ffn_W_gate", b_gate="L0_ffn_b_gate", W_e="L0_ffn_W_e").items()})
            if phases < 2:
                return
            expert_phase(nc, shared, a["L0_ffn_b_e"])
        if phases < 3:
            return
        shared["gu_hi"] = sb("gate_up_hi", [P, 2 * KD * INTER], F32R)
        shared["gu_lo"] = sb("gate_up_lo", [P, 2 * KD * INTER], F32R)
        layer1_phase(nc, shared, {"ctxT": a["ctxT"], "gate_up": a["gate_up"], "Wq": a["L1_xattn_Wq"], "Wk": a["L1_xattn_Wk"],
                                  "Wv": a["L1_xattn_Wv"], "Wo": a["L1_xattn_Wo"]})
        if phases < 4:
            return
        ffn_phase(nc, shared, {"w_down": a["L1_ffn_w_down"], "b_down": a["L1_ffn_b_down"],
                               **{k: a[k] for k in ("b_gate_main", "b_gate_rest", "b_up_main", "b_up_rest")}}, out)


TRANSPOSED = ("L0_xattn_Wq", "L0_xattn_Wk", "L0_xattn_Wv", "L0_xattn_Wo", "L1_ffn_w_gate", "L1_ffn_w_up", "L1_ffn_w_down")


def layout(inputs):
    import numpy as np
    a = {n: np.asarray(x) for n, x in inputs.items()}
    a = {n: x.T if n in TRANSPOSED else x for n, x in a.items()}
    a["ctxT"] = a["ctx_4096"].reshape(TILES, P, KD, P).transpose(0, 3, 2, 1).reshape(TILES, P, DIM)
    a["L1_xattn_Wq"] = a["L1_xattn_Wq"].reshape(DIM, KVH, GROUP, HD).transpose(0, 2, 1, 3).reshape(DIM, DIM)
    a["L1_xattn_Wo"] = a["L1_xattn_Wo"].reshape(KVH, GROUP, HD, DIM).transpose(1, 0, 2, 3).reshape(DIM, DIM)
    both = np.stack([a.pop("L1_ffn_w_gate"), a.pop("L1_ffn_w_up")])
    a["gate_up"] = both.reshape(2, KD, P, 2, INTER // 2).transpose(0, 1, 3, 2, 4).reshape(TILES, P, INTER // 2)
    for b in ("gate", "up"):
        bias, full = a.pop("L1_ffn_b_" + b), INTER // P
        a[f"b_{b}_main"] = bias[:full * P].reshape(full, P).T
        a[f"b_{b}_rest"] = bias[full * P:].reshape(-1, 1)
    return {n: np.ascontiguousarray(x) for n, x in a.items()}


def kernel(**inputs):
    import numpy as np
    from concourse import bacc
    from concourse.bass_utils import run_bass_kernel_spmd

    nc = bacc.Bacc("TRN2", target_bir_lowering=False, num_devices=1)
    arrays = layout(inputs)
    args = {n: nc.dram_tensor(n, x.shape, mybir.dt.from_np(x.dtype), kind="ExternalInput").ap() for n, x in arrays.items()}
    out = nc.dram_tensor("out", (BATCH, SEQ, DIM), F32, kind="ExternalOutput").ap()
    build(nc, args, out)
    result = run_bass_kernel_spmd(nc, [arrays], core_ids=[0])
    return result.results[0]["out"]
```

```python
import concourse.bass as bass
from concourse import mybir
from contextlib import ExitStack

F32 = mybir.dt.float32
F32R = mybir.dt.float32r
BF16 = mybir.dt.bfloat16
I32 = mybir.dt.int32
U32 = mybir.dt.uint32
ALU = mybir.AluOpType
ACT = mybir.ActivationFunctionType
AX = mybir.AxisListType

P = 128
BATCH, SEQ, DIM = 32, 64, 512
TILES = BATCH * SEQ // P
KD = DIM // P
EPS = 1e-5

H0 = 8
LH = DIM // H0
SCALE0 = LH ** -0.5

EXPERTS = 8
EW = KD * DIM
REGION = BATCH * SEQ + P
BLOCKS = 2 * TILES + EXPERTS - 1

KVH, GROUP, HD = 8, 4, 16
SCALE1 = HD ** -0.5
INTER = 1376
NI = -(-INTER // P)
TG = 4


def after(eng, *counts, tick):
    for n, (sem, value) in enumerate(counts):
        if not isinstance(value, int):
            eng.wait_ge(sem, value)
            if n == len(counts) - 1 or eng.engine == mybir.EngineType.SP:
                eng.sem_inc(tick, 1)
        elif value > 0:
            eng.wait_ge(sem, value)


def slot_full(t, par):
    return 16 * (t // 2 + 1) if isinstance(t, int) else t * 8 + (16 - 8 * par)


def upto(t, tiles):
    return min(t, tiles) if isinstance(t, int) else t


def pipelined(eng, tiles, stages):
    last_lag = max(lag for _, lag in stages)
    first = last_lag + 2 + last_lag % 2
    until = first + (tiles - first) // 2 * 2

    def peeled(s):
        for stage, lag in stages:
            if 0 <= s - lag < tiles:
                stage(s - lag, (s - lag) % 2)

    for s in range(first):
        peeled(s)
    with eng.Fori(first // 2, until // 2) as i:
        for odd in range(2):
            for stage, lag in stages:
                stage(2 * i + (odd - lag), (odd - lag) % 2)
    for s in range(until, tiles + last_lag):
        peeled(s)


class Ctx:

    def __init__(self, nc, stack, prefix):
        self.nc, self.stack, self.prefix = nc, stack, prefix
        self.sems = []

    def sb(self, name, shape, dt=F32):
        return self.stack.enter_context(self.nc.sbuf_tensor(self.prefix + name, shape, dt))

    def pb(self, name):
        return self.stack.enter_context(self.nc.psum_tensor(self.prefix + name, [P, 512], F32))

    def sem(self, name):
        self.sems.append(self.stack.enter_context(self.nc.semaphore(self.prefix + name)))
        return self.sems[-1]

    def clear(self):
        with self.nc.Block() as block:
            @block.gpsimd
            def _(pool):
                numbers = sorted(s.num for s in self.sems)
                first = 0
                for n in range(1, len(numbers) + 1):
                    if n == len(numbers) or numbers[n] != numbers[n - 1] + 1:
                        pool.sem_clear(range(numbers[first], numbers[n - 1] + 1))
                        first = n


def block_diagonal(ap):
    return ap[0:64, 0:64], ap[64:128, 64:128]


def layer0_phase(nc, shared, a):
    with ExitStack() as stack:
        c = Ctx(nc, stack, "a_")
        sb, pb, sem = c.sb, c.pb, c.sem
        wq, wk, wv, wo = (sb(n, [P, P]) for n in ("wq", "wk", "wv", "wo"))
        bq, bk = sb("bq", [P, 64]), sb("bk", [P, 64])
        bv, bo = sb("bv", [P, 1]), sb("bo", [P, 1])
        wg, bg = sb("wg", [P, KD, EXPERTS]), sb("bg", [P, EXPERTS])
        ident = sb("ident", [P, P])
        ctx_in, x_in, x_res, xn, xn2 = (sb(n, [P, 2, DIM]) for n in ("ctx_in", "x_in", "x_res", "xn", "xn2"))
        qT, kT, score, probT, attn, xT = (sb(n, [P, 2, DIM]) for n in ("qT", "kT", "score", "probT", "attn", "xT"))
        minus_half = sb("minus_half", [P, 1])
        v = sb("v", [P, 2, H0, LH + 1])
        wstage = sb("wstage", [P, 2, 1024])
        stats, mv, rstd = sb("stats", [P, 2, 6]), sb("mv", [P, 2, 2]), sb("rstd", [P, 2, 2])
        stats2, mv2, rstd2 = sb("stats2", [P, 2, 6]), sb("mv2", [P, 2, 2]), sb("rstd2", [P, 2, 2])
        smax = sb("smax", [P, 2, 8])
        rsum = sb("rsum", [P, 2, 2, 4, 1])
        logit, top8, chosen = sb("logit", [P, 2, 8]), sb("top8", [P, 2, 8]), sb("chosen", [P, 2, 8], U32)
        both, rank = sb("both", [P, 2, 8], BF16), sb("rank", [P, 2, 8])
        picked = sb("picked", [P, 2, 2, 8])
        ati = sb("ati", [P, 2, 2], I32)
        seen = sb("seen", [P, 8])
        seenb = sb("seenb", [P, 8], BF16)
        expert_no, region_at = sb("expert_no", [P, 8]), sb("region_at", [P, 8])
        before, ones = sb("before", [P, P], BF16), sb("ones", [P, P], BF16)
        zero_rows = sb("zero_rows", [P, DIM])
        k128, below = sb("k128", [P, 8, 16]), sb("below", [P, 8, 8])
        counts, nblk, start, end = sb("counts", [P, 8]), sb("nblk", [P, 8]), sb("start", [P, 8]), sb("end", [P, 8])
        over, lower = sb("over", [P, 8, 16]), sb("lower", [P, 8, 8])
        blk, passed, bstart = sb("blk", [P, BLOCKS]), sb("passed", [P, BLOCKS, 8]), sb("bstart", [P, BLOCKS])
        bexp, table = sb("bexp", [P, BLOCKS]), sb("table", [P, 2, BLOCKS])
        n128, behind, row0, change, shift = sb("n128", [P, 8]), sb("behind", [P, 8]), sb("row0", [P, 9]), sb("change", [P, 8]), sb("shift", [P, 8])
        at_kept2 = sb("at_kept2", [P, 2 * TILES])
        moved = sb("moved", [P, TILES * 2, 8])
        at_kept, hot_kept = sb("at_kept", [P, TILES, 2]), sb("hot_kept", [P, TILES, 2, 8])

        pkq, pv, ps, pt, py, pr = (pb(n) for n in ("pkq", "pv", "ps", "pt", "py", "pr"))
        po = stack.enter_context(nc.psum_tensor("a_po", [P, 2, 512], F32))
        N_CONST = 14

        k_consts, q_consts, v_consts, o_consts, gate_consts = (sem(n + "_consts") for n in ("k", "q", "v", "o", "gate"))
        zeroed, ident0, made_const, front_zeroed = sem("zeroed"), sem("ident0"), sem("made_const"), sem("front_zeroed")
        ctx_loaded = [sem(f"ctx_loaded{i}") for i in range(2)]
        x_loaded = [sem(f"x_loaded{i}") for i in range(2)]
        res_loaded = [sem(f"res_loaded{i}") for i in range(2)]
        w_loaded = [sem(f"w_loaded{i}") for i in range(2)]
        x1_stored = [sem(f"x1_stored{i}") for i in range(2)]
        scattered = [sem(f"scattered{i}") for i in range(2)]
        w_hi, w_lo = sem("w_hi"), sem("w_lo")
        k_made, k_kept, q_made, q_kept = sem("k_made"), sem("k_kept"), sem("q_made"), sem("q_kept")
        v_made, v_kept, s_made, s_shifted, exp_done = sem("v_made"), sem("v_kept"), sem("s_made"), sem("s_shifted"), sem("exp_done")
        pt_made, pt_kept, o_made, o_kept = sem("pt_made"), sem("pt_kept"), sem("o_made"), sem("o_kept")
        y_made, x1_ready, xn_ready, xn2_ready = sem("y_made"), sem("x1_ready"), sem("xn_ready"), sem("xn2_ready")
        xt_made, xt_kept, l_made, both_ready = sem("xt_made"), sem("xt_kept"), sem("l_made"), sem("both_ready")
        r_made, at_ready, count_made = sem("r_made"), sem("at_ready"), sem("count_made")
        norm_step, norm2_step, max_step, sum_step = sem("norm_step"), sem("norm2_step"), sem("max_step"), sem("sum_step")
        mv_ready, mv2_ready, rs_step, rs2_step, rs_ready, rs2_ready = (sem(n) for n in ("mv_ready", "mv2_ready", "rs_step", "rs2_step", "rs_ready", "rs2_ready"))
        choose_step, place_step, table_step = sem("choose_step"), sem("place_step"), sem("table_step")
        sp_tick, act_tick, pool_tick, pe_tick, dve_tick = (sem(e + "_tick") for e in ("sp", "act", "pool", "pe", "dve"))
        stack.callback(c.clear)
        block = stack.enter_context(nc.Block())

        x_v = a["x"].rearrange("(t b) s d -> t (b s) d", b=2)
        c_v = a["ctx"].rearrange("(t b) s d -> t (b s) d", b=2)
        w_v = a["W_e"].rearrange("e (k p) h -> p (e k) h", p=P)

        def first(t, eng, *waits):
            if isinstance(t, int) and t == 0:
                for sem_, value in waits:
                    eng.wait_ge(sem_, value)

        @block.sync
        def _(sp):
            def load_consts():
                sp.wait_ge(zeroed, 4)
                for buf, w, b, bias, loaded in ((wv, "Wv", bv, "bv", v_consts), (wo, "Wo", bo, "bo", o_consts)):
                    for half, part in enumerate(block_diagonal(buf)):
                        sp.dma_start(part, a[w]).then_inc(loaded, 16)
                        sp.dma_start(b[64 * half:64 * half + 64, :], a[bias].rearrange("(p a) -> p a", a=1)).then_inc(loaded, 16)

            def load_gate_consts():
                sp.dma_start(bg[:, :], a["b_gate"].partition_broadcast(P)).then_inc(gate_consts, 16)
                sp.dma_start(wg[:, :, :], a["W_gate"].rearrange("(k p) e -> p k e", p=P)).then_inc(gate_consts, 16)

            def load_ctx(t, p):
                after(sp, (v_made, t - 1), tick=sp_tick)
                sp.dma_start(ctx_in[:, p, :], c_v[t, :, :]).then_inc(ctx_loaded[p], 16)
                if isinstance(t, int) and t < 2:
                    (load_consts, load_gate_consts)[t]()

            def load_x(t, p):
                after(sp, (xn_ready, t - 1), tick=sp_tick)
                sp.dma_start(x_in[:, p, :], x_v[t, :, :]).then_inc(x_loaded[p], 16)

            def load_weights(t, p):
                after(sp, (w_lo, t - 1), tick=sp_tick)
                sp.dma_start(wstage[:, p, :].rearrange("p (k h) -> p k h", k=2), w_v[:, bass.ds(2 * t, 2), :]).then_inc(w_loaded[p], 16)

            def load_residual(t, p):
                after(sp, (xn2_ready, t - 1), (x1_stored[p], slot_full(t, p) - 16), tick=sp_tick)
                sp.dma_start(x_res[:, p, :], x_v[t, :, :]).then_inc(res_loaded[p], 16)

            def store_x1(t, p):
                after(sp, (x1_ready, t + 1), tick=sp_tick)
                sp.dma_start(shared["x1"][t, :, :], x_res[:, p, :]).then_inc(x1_stored[p], 16)

            pipelined(sp, TILES, [(load_residual, 3), (load_x, 0), (load_ctx, 0), (load_weights, 1), (store_x1, 4)])
            sp.wait_ge(front_zeroed, 16)
            for i in range(2):
                sp.wait_ge(x1_stored[i], 8 * TILES)

        @block.gpsimd
        def _(pool):
            for buf in (wk, wv, wq, wo):
                pool.memset(buf[:, :], 0.0).then_inc(zeroed, 1)
            pool.memset(v[:, :, :, LH:LH + 1], 1.0).then_inc(made_const, 1)
            pool.memset(zero_rows[:, :], 0.0).then_inc(made_const, 1)
            pool.memset(ones[:, :], 1.0).then_inc(made_const, 1)
            pool.memset(seenb[:, :], 0.0).then_inc(made_const, 1)
            pool.memset(seen[:, :], 0.0).then_inc(made_const, 1)
            for buf, pattern, base in ((expert_no, [[1, 8]], 0), (region_at, [[REGION, 8]], P),
                                       (k128, [[0, 8], [P, 16]], 0), (blk, [[1, BLOCKS]], 0)):
                pool.iota(buf[:], pattern, base=base, channel_multiplier=0,
                          allow_small_or_imprecise_dtypes=True).then_inc(made_const, 1)
            pool.memset(minus_half[:, :], -0.5).then_inc(made_const, 1)
            pool.memset(row0[:, 8:9], 0.0).then_inc(made_const, 1)
            pool.memset(ident[:, :], 0.0).then_inc(ident0, 1)
            pool.memset(before[:, :], 1.0).then_inc(ident0, 1)
            pool.memset(below[:, :, :], 1.0).then_inc(ident0, 1)
            pool.wait_ge(ident0, 3)
            pool.affine_select(out=ident[:, :], in_=ident[:, :], compare_op=ALU.not_equal, fill=1.0,
                               base=0, pattern=[[-1, P]], channel_multiplier=1).then_inc(made_const, 1)
            pool.affine_select(out=before[:, :], in_=before[:, :], compare_op=ALU.is_ge, fill=0.0,
                               base=-1, pattern=[[1, P]], channel_multiplier=-1).then_inc(made_const, 1)
            pool.affine_select(out=below[:, :, :], in_=below[:, :, :], compare_op=ALU.is_ge, fill=0.0,
                               base=-1, pattern=[[1, 8], [-1, 8]], channel_multiplier=0).then_inc(made_const, 1)

            def inverse_deviation(t, m, r, step, done):
                pool.tensor_scalar(m[:, 1:2], m[:, 1:2], EPS, None, ALU.add).then_inc(step, 1)
                after(pool, (step, 2 * t + 1), tick=pool_tick)
                pool.tensor_tensor(r[:, 0:1], m[:, 1:2], minus_half[:, :], ALU.pow).then_inc(step, 1)
                after(pool, (step, 2 * t + 2), tick=pool_tick)
                pool.tensor_scalar(r[:, 1:2], m[:, 0:1], -1.0, r[:, 0:1], ALU.mult, ALU.mult).then_inc(done, 1)

            def scale_x(t, p):
                after(pool, (mv_ready, t + 1), (xn_ready, t - 1), tick=pool_tick)
                inverse_deviation(t, mv[:, p, :], rstd[:, p, :], rs_step, rs_ready)

            def scale_x1(t, p):
                after(pool, (mv2_ready, t + 1), (xn2_ready, t - 1), tick=pool_tick)
                inverse_deviation(t, mv2[:, p, :], rstd2[:, p, :], rs2_step, rs2_ready)

            def low_part(t, p):
                after(pool, (w_hi, t + 1), tick=pool_tick)
                dst = bass.ds(1024 * t, 1024)
                pool.tensor_tensor(shared["w_lo"][:, dst], wstage[:, p, :], shared["w_hi"][:, dst].bitcast(F32), ALU.subtract).then_inc(w_lo, 1)

            def scatter(t, p):
                after(pool, (at_ready, t + 1), tick=pool_tick)
                for k in range(2):
                    pool.indirect_dma_start(out=shared["xs"], out_offset=bass.IndirectOffsetOnAxis(ap=ati[:, p, k:k + 1], axis=0),
                                            in_=xn2[:, p, :], in_offset=None).then_inc(scattered[p], 16)

            pipelined(pool, TILES, [(scatter, 5), (scale_x, 0), (scale_x1, 3), (low_part, 2)])
            for i in range(2):
                pool.wait_ge(scattered[i], 16 * TILES)

        @block.scalar
        def _(act):
            act.wait_ge(zeroed, 4)
            for buf, w, b, loaded in ((wk, "Wk", (bk, "bk"), k_consts), (wq, "Wq", (bq, "bq"), q_consts)):
                for part in block_diagonal(buf):
                    act.dma_start(part, a[w]).then_inc(loaded, 16)
                act.dma_start(b[0][:, :], a[b[1]].partition_broadcast(P)).then_inc(loaded, 16)
            act.wait_ge(made_const, N_CONST)

            def keep_v(t, p):
                first(t, act, (v_consts, 64))
                after(act, (v_made, t + 1), (o_made, t - 1), tick=act_tick)
                act.activation(v[:, p, :, 0:LH], pv[:, :].rearrange("p (h l) -> p h l", h=H0), ACT.Identity, bias=bv[:, 0:1]).then_inc(v_kept, 1)

            def norm_x(t, p):
                after(act, (rs_ready, t + 1), (q_made, t - 1), tick=act_tick)
                act.activation(xn[:, p, :], x_in[:, p, :], ACT.Identity, scale=rstd[:, p, 0:1], bias=rstd[:, p, 1:2]).then_inc(xn_ready, 1)

            def norm_x1(t, p):
                after(act, (rs2_ready, t + 1), (xt_made, t - 1), (scattered[p], 2 * slot_full(t, p) - 32), tick=act_tick)
                act.activation(xn2[:, p, :], x_res[:, p, :], ACT.Identity, scale=rstd2[:, p, 0:1], bias=rstd2[:, p, 1:2]).then_inc(xn2_ready, 1)

            def exponent(t, p):
                after(act, (s_shifted, t + 1), tick=act_tick)
                act.activation(score[:, p, :], score[:, p, :], ACT.Exp, scale=SCALE0).then_inc(exp_done, 1)

            def keep_probT(t, p):
                after(act, (pt_made, t + 1), (o_made, t - 1), tick=act_tick)
                act.activation(probT[:, p, :], pt[:, :], ACT.Copy).then_inc(pt_kept, 1)

            def keep_xT(t, p):
                after(act, (xt_made, t + 1), (l_made, t - 1), tick=act_tick)
                act.activation(xT[:, p, :], pt[:, :], ACT.Copy).then_inc(xt_kept, 1)
                if isinstance(t, int) and t == 0:
                    act.dma_start(shared["xs"].rearrange("(e r) d -> r e d", e=EXPERTS)[0:P, :, :],
                                  zero_rows[:, :].rearrange("p (x d) -> p x d", x=1).to_broadcast([P, EXPERTS, DIM])).then_inc(front_zeroed, 16)

            def high_part(t, p):
                after(act, (w_loaded[p], slot_full(t, p)), tick=act_tick)
                act.activation(shared["w_hi"][:, bass.ds(1024 * t, 1024)], wstage[:, p, :], ACT.Copy).then_inc(w_hi, 1)

            pipelined(act, TILES, [(keep_xT, 4), (keep_probT, 2), (keep_v, 1), (high_part, 1), (norm_x, 0), (norm_x1, 3), (exponent, 1)])

        @block.tensor
        def _(pe):
            pe.wait_ge(made_const, N_CONST)

            def make_k(t, p):
                first(t, pe, (k_consts, 48))
                after(pe, (ctx_loaded[p], slot_full(t, p)), (q_kept, t), tick=pe_tick)
                for j in range(4):
                    mm = pe.matmul(pkq[:, P * j:P * j + P], ctx_in[:, p, P * j:P * j + P], wk[:, :], start=True, stop=True)
                mm.then_inc(k_made, 1)

            def make_v(t, p):
                first(t, pe, (v_consts, 64))
                after(pe, (v_kept, t), tick=pe_tick)
                pe.matmul(pv[:, :], wv[:, :], ctx_in[:, p, :], start=True, stop=True).then_inc(v_made, 1)

            def make_q(t, p):
                first(t, pe, (q_consts, 48))
                after(pe, (xn_ready, t + 1), (k_kept, t + 1), tick=pe_tick)
                for j in range(4):
                    mm = pe.matmul(pkq[:, P * j:P * j + P], xn[:, p, P * j:P * j + P], wq[:, :], start=True, stop=True)
                mm.then_inc(q_made, 1)

            def make_scores(t, p):
                after(pe, (q_kept, t + 1), (s_shifted, t), tick=pe_tick)
                for j in range(4):
                    for b in range(2):
                        for r in range(2):
                            rows, cols = slice(64 * r, 64 * r + 64), slice(P * j + 64 * b, P * j + 64 * b + 64)
                            mm = pe.matmul(ps[rows, cols], qT[rows, p, cols], kT[rows, p, cols], start=True, stop=True)
                mm.then_inc(s_made, 1)

            def transpose_probs(t, p):
                after(pe, (exp_done, t + 1), (xt_kept, t - 1), tick=pe_tick)
                for j in range(4):
                    mm = pe.transpose(pt[:, P * j:P * j + P], score[:, p, P * j:P * j + P], ident[:, :])
                mm.then_inc(pt_made, 1)

            def make_attn(t, p):
                after(pe, (pt_kept, t + 1), (v_kept, t + 1), (o_kept, t), tick=pe_tick)
                for h in range(H0):
                    for b in range(2):
                        rows = slice(64 * b, 64 * b + 64)
                        mm = pe.matmul(po[rows, h // 4, 65 * (h % 4):65 * (h % 4) + 65], probT[rows, p, 64 * h:64 * h + 64],
                                       v[rows, p, h, :], start=True, stop=True)
                mm.then_inc(o_made, 1)

            def project(t, p):
                first(t, pe, (o_consts, 64))
                after(pe, (o_kept, t + 1), (x1_ready, t), tick=pe_tick)
                pe.matmul(py[:, :], wo[:, :], attn[:, p, :], start=True, stop=True).then_inc(y_made, 1)

            def transpose_x(t, p):
                after(pe, (xn2_ready, t + 1), (pt_kept, upto(t + 2, TILES)), tick=pe_tick)
                for j in range(4):
                    mm = pe.transpose(pt[:, P * j:P * j + P], xn2[:, p, P * j:P * j + P], ident[:, :])
                mm.then_inc(xt_made, 1)

            def make_logits(t, p):
                first(t, pe, (gate_consts, 32))
                after(pe, (xt_kept, t + 1), (place_step, 5 * t - 4), tick=pe_tick)
                for j in range(4):
                    mm = pe.matmul(pr[:, 0:8], xT[:, p, P * j:P * j + P], wg[:, j, :], start=j == 0, stop=j == 3)
                mm.then_inc(l_made, 1)

            def make_rank(t, p):
                after(pe, (both_ready, t + 1), (place_step, 5 * t - 2), tick=pe_tick)
                pe.matmul(pr[:, 0:8], before[:, :], both[:, p, :], start=True, stop=False)
                pe.matmul(pr[:, 0:8], ones[:, :], seenb[:, :], start=False, stop=True).then_inc(r_made, 1)

            pipelined(pe, TILES, [(make_q, 1), (transpose_x, 4), (make_rank, 5), (project, 3), (transpose_probs, 2), (make_logits, 4),
                                  (make_v, 1), (make_scores, 1), (make_k, 0), (make_attn, 2)])
            pe.wait_ge(at_ready, TILES)
            pe.matmul(pr[:, 0:8], ones[:, :], seenb[:, :], start=True, stop=True).then_inc(count_made, 1)

        @block.vector
        def _(dve):
            dve.wait_ge(made_const, N_CONST)

            def sum_x(t, p):
                after(dve, (x_loaded[p], slot_full(t, p)), tick=dve_tick)
                dve.bn_stats(stats[:, p, :], x_in[:, p, :]).then_inc(norm_step, 1)

            def average_x(t, p):
                after(dve, (norm_step, t + 1), (rs_ready, t - 1), tick=dve_tick)
                dve.bn_aggr(mv[:, p, :], stats[:, p, :]).then_inc(mv_ready, 1)

            def by_position(ap):
                return ap.rearrange("p (j o) -> p j o", o=64)

            def keep_k(t, p):
                first(t, dve, (k_consts, 48))
                after(dve, (k_made, t + 1), (s_made, t - 1), tick=dve_tick)
                dve.tensor_tensor(by_position(kT[:, p, :]), by_position(pkq[:, :]), every_bk, ALU.add).then_inc(k_kept, 1)

            def keep_q(t, p):
                first(t, dve, (q_consts, 48))
                after(dve, (q_made, t + 1), (s_made, t - 1), tick=dve_tick)
                dve.tensor_tensor(by_position(qT[:, p, :]), by_position(pkq[:, :]), every_bq, ALU.add).then_inc(q_kept, 1)

            every_bk, every_bq = (b[:, :].rearrange("p (x o) -> p x o", x=1).to_broadcast([P, 8, 64]) for b in (bk, bq))

            def max_scores(t, p):
                after(dve, (s_made, t + 1), tick=dve_tick)
                dve.tensor_reduce(smax[:, p, :], ps[:, :].rearrange("p (g e) -> p g e", g=8), AX.X, ALU.max).then_inc(max_step, 1)

            def shift_scores(t, p):
                after(dve, (pt_made, t - 1), (max_step, t + 1), tick=dve_tick)
                peak = smax[:, p, :].rearrange("p (g x) -> p g x", x=1).to_broadcast([P, 8, 64])
                dve.tensor_tensor(score[:, p, :].rearrange("p (g e) -> p g e", g=8), ps[:, :].rearrange("p (g e) -> p g e", g=8), peak, ALU.subtract).then_inc(s_shifted, 1)

            def heads():
                return po[:, :, 0:260].rearrange("p b (h l) -> p b h l", h=4)

            def invert_sums(t, p):
                after(dve, (o_made, t + 1), tick=dve_tick)
                dve.reciprocal(rsum[:, p, :, :], heads()[:, :, :, 64:65]).then_inc(sum_step, 1)

            def keep_attn(t, p):
                after(dve, (y_made, t - 1), (sum_step, t + 1), tick=dve_tick)
                dve.tensor_tensor(attn[:, p, :].rearrange("p (b h l) -> p b h l", b=2, h=4), heads()[:, :, :, 0:64],
                                  rsum[:, p, :, :].to_broadcast([P, 2, 4, 64]), ALU.mult).then_inc(o_kept, 1)

            def add_residual(t, p):
                first(t, dve, (o_consts, 64))
                after(dve, (y_made, t + 1), (res_loaded[p], slot_full(t, p)), tick=dve_tick)
                dve.scalar_tensor_tensor(x_res[:, p, :], py[:, :], bo[:, 0:1], x_res[:, p, :], ALU.add, ALU.add).then_inc(x1_ready, 1)

            def sum_x1(t, p):
                after(dve, (x1_ready, t + 1), tick=dve_tick)
                dve.bn_stats(stats2[:, p, :], x_res[:, p, :]).then_inc(norm2_step, 1)

            def average_x1(t, p):
                after(dve, (norm2_step, t + 1), (rs2_ready, t - 1), tick=dve_tick)
                dve.bn_aggr(mv2[:, p, :], stats2[:, p, :]).then_inc(mv2_ready, 1)

            def add_gate_bias(t, p):
                first(t, dve, (gate_consts, 32))
                after(dve, (l_made, t + 1), tick=dve_tick)
                dve.tensor_tensor(logit[:, p, :], pr[:, 0:8], bg[:, :], ALU.add).then_inc(choose_step, 1)

            def sort_logits(t, p):
                after(dve, (choose_step, 4 * t + 1), tick=dve_tick)
                dve.max(top8[:, p, :], logit[:, p, :]).then_inc(choose_step, 1)

            def find_experts(t, p):
                after(dve, (choose_step, 4 * t + 2), tick=dve_tick)
                dve.max_index(chosen[:, p, :], top8[:, p, :], logit[:, p, :]).then_inc(choose_step, 1)

            def mark_experts(t, p):
                after(dve, (choose_step, 4 * t + 3), tick=dve_tick)
                dve.tensor_tensor(hot_kept[:, t, :, :], chosen[:, p, 0:2].rearrange("p (k x) -> p k x", x=1).to_broadcast([P, 2, 8]),
                                  expert_no[:, :].rearrange("p (x e) -> p x e", x=1).to_broadcast([P, 2, 8]), ALU.is_equal).then_inc(choose_step, 1)

            def add_marks(t, p):
                after(dve, (choose_step, 4 * t + 4), (r_made, t), tick=dve_tick)
                dve.tensor_tensor(both[:, p, :], hot_kept[:, t, 0, :], hot_kept[:, t, 1, :], ALU.add).then_inc(both_ready, 1)

            def add_region(t, p):
                after(dve, (r_made, t + 1), tick=dve_tick)
                dve.tensor_tensor(rank[:, p, :], pr[:, 0:8], region_at[:, :], ALU.add).then_inc(place_step, 1)
                dve.tensor_tensor(seen[:, :], seen[:, :], both[:, p, :], ALU.add).then_inc(place_step, 1)

            def pick_ranks(t, p):
                after(dve, (place_step, 5 * t + 2), tick=dve_tick)
                dve.tensor_copy(seenb[:, :], seen[:, :]).then_inc(place_step, 1)
                dve.tensor_tensor(picked[:, p, :, :], hot_kept[:, t, :, :], rank[:, p, :].rearrange("p (x e) -> p x e", x=1).to_broadcast([P, 2, 8]), ALU.mult).then_inc(place_step, 1)

            def sum_ranks(t, p):
                after(dve, (place_step, 5 * t + 4), tick=dve_tick)
                dve.tensor_reduce(at_kept[:, t, :], picked[:, p, :, :], AX.X, ALU.add).then_inc(place_step, 1)

            def round_ranks(t, p):
                after(dve, (place_step, 5 * t + 5), (scattered[p], 2 * slot_full(t, p) - 32), tick=dve_tick)
                dve.tensor_copy(ati[:, p, :], at_kept[:, t, :]).then_inc(at_ready, 1)

            pipelined(dve, TILES, [(keep_q, 1), (add_region, 5), (pick_ranks, 5), (add_residual, 3), (sum_ranks, 5), (sum_x, 0), (round_ranks, 5),
                                   (sum_x1, 3), (average_x, 0), (average_x1, 3), (add_gate_bias, 4), (max_scores, 1), (sort_logits, 4),
                                   (shift_scores, 1), (find_experts, 4), (keep_k, 0), (mark_experts, 4), (invert_sums, 2), (add_marks, 4),
                                   (keep_attn, 2)])

            steps = [0]

            def step(ins):
                steps[0] += 1
                ins.then_inc(table_step, 1)

            def then(ins):
                step(ins)
                dve.wait_ge(table_step, steps[0])

            def spread(ap, rows):
                return ap.rearrange("p (x e) -> p x e", x=1).to_broadcast([P, rows, 8])

            def each(ap, n):
                return ap.rearrange("p (e x) -> p e x", x=1).to_broadcast([P, ap.shape[1], n])

            dve.wait_ge(count_made, 1)
            then(dve.tensor_copy(counts[:, :], pr[:, 0:8]))
            step(dve.tensor_tensor(behind[:, :], counts[:, :], region_at[:, :], ALU.add))
            then(dve.tensor_tensor(over[:, :, :], each(counts[:, :], 16), k128[:, :, :], ALU.is_gt))
            then(dve.tensor_reduce(nblk[:, :], over[:, :, :], AX.X, ALU.add))
            step(dve.tensor_scalar(n128[:, :], nblk[:, :], float(P), None, ALU.mult))
            then(dve.tensor_tensor(lower[:, :, :], below[:, :, :], spread(nblk[:, :], 8), ALU.mult))
            step(dve.tensor_tensor(row0[:, 0:8], behind[:, :], n128[:, :], ALU.subtract))
            then(dve.tensor_reduce(start[:, :], lower[:, :, :], AX.X, ALU.add))
            then(dve.tensor_tensor(end[:, :], start[:, :], nblk[:, :], ALU.add))
            step(dve.tensor_tensor(change[:, :], row0[:, 1:9], row0[:, 0:8], ALU.subtract))
            then(dve.tensor_scalar(shared["last"][:, :], end[:, 7:8], -1.0, None, ALU.add))
            step(dve.tensor_tensor(change[:, :], change[:, :], n128[:, :], ALU.subtract))
            then(dve.tensor_scalar(blk[:, :], blk[:, :], shared["last"][:, 0:1], None, ALU.min))
            then(dve.tensor_tensor(passed[:, :, :], each(blk[:, :], 8), spread(end[:, :], BLOCKS), ALU.is_ge))
            then(dve.tensor_reduce(bexp[:, :], passed[:, :, :], AX.X, ALU.add))
            then(dve.tensor_tensor(passed[:, :, :], passed[:, :, :], spread(change[:, :], BLOCKS), ALU.mult))
            step(dve.tensor_scalar(table[:, 1, :], bexp[:, :], float(DIM), None, ALU.mult))
            then(dve.tensor_reduce(bstart[:, :], passed[:, :, :], AX.X, ALU.add))
            step(dve.scalar_tensor_tensor(shift[:, :], start[:, :], float(P), row0[:, 0:8], ALU.mult, ALU.subtract))
            then(dve.scalar_tensor_tensor(bstart[:, :], blk[:, :], float(P), bstart[:, :], ALU.mult, ALU.add))
            step(dve.tensor_tensor(moved[:, :, :], hot_kept[:, :, :, :].rearrange("p t k e -> p (t k) e"), spread(shift[:, :], 2 * TILES), ALU.mult))
            then(dve.tensor_scalar(table[:, 0, :], bstart[:, :], row0[:, 0:1], None, ALU.add))
            step(dve.tensor_reduce(at_kept2[:, :], moved[:, :, :], AX.X, ALU.add))
            then(dve.tensor_copy(shared["table"][:, :, :], table[:, :, :]))
            then(dve.tensor_tensor(at_kept2[:, :], at_kept2[:, :], at_kept[:, :, :].rearrange("p t k -> p (t k)"), ALU.add))
            then(dve.tensor_copy(shared["y_at"][:, :], at_kept2[:, :]))


def identity(pool, buf, zeroed, made):
    pool.memset(buf[:, :], 0.0).then_inc(zeroed, 1)
    pool.wait_ge(zeroed, 1)
    pool.affine_select(out=buf[:, :], in_=buf[:, :], compare_op=ALU.not_equal, fill=1.0,
                       base=0, pattern=[[-1, P]], channel_multiplier=1).then_inc(made, 1)


def expert_phase(nc, shared, b_e):
    with ExitStack() as stack:
        c = Ctx(nc, stack, "b_")
        sb, pb, sem = c.sb, c.pb, c.sem
        bias, ident = sb("bias", [P, EXPERTS * DIM]), sb("ident", [P, P])
        rows, biased, result = sb("rows", [P, 2, DIM]), sb("biased", [P, 2, DIM]), sb("result", [P, 2, DIM])
        rowsT_hi, rowsT_lo = sb("rowsT_hi", [P, 2, DIM], F32R), sb("rowsT_lo", [P, 2, DIM], F32R)
        pt, py = [pb(f"pt{i}") for i in range(2)], [pb(f"py{i}") for i in range(2)]
        bias_loaded, zeroed, ident_made = sem("bias_loaded"), sem("zeroed"), sem("ident_made")
        rows_loaded, stored = [sem(f"rows_loaded{i}") for i in range(2)], [sem(f"stored{i}") for i in range(2)]
        t_made, hi_kept, lo_kept, y_made = sem("t_made"), sem("hi_kept"), sem("lo_kept"), sem("y_made")
        biased_made, result_made = sem("biased_made"), sem("result_made")
        sp_tick, act_tick, pe_tick, dve_tick = (sem(e + "_tick") for e in ("sp", "act", "pe", "dve"))
        w_hi, w_lo, table = shared["w_hi"], shared["w_lo"], shared["table"]
        y_v = shared["ys"].rearrange("(b p) h -> b p h", p=P)
        stack.callback(c.clear)
        block = stack.enter_context(nc.Block())

        @block.sync
        def _(sp):
            def load(b, p):
                row = sp.value_load(table[0:1, 0, bass.ds(b, 1)], min_val=0, max_val=EXPERTS * REGION - P)
                after(sp, (t_made, b - 1), tick=sp_tick)
                sp.dma_start(rows[:, p, :], shared["xs"][bass.ds(row, P), :]).then_inc(rows_loaded[p], 16)
                if isinstance(b, int) and b == 1:
                    sp.dma_start(bias[:, :], b_e.rearrange("e h -> (e h)").partition_broadcast(P)).then_inc(bias_loaded, 16)

            def store(b, p):
                after(sp, (result_made, b + 1), tick=sp_tick)
                sp.dma_start(y_v[b, :, :], result[:, p, :]).then_inc(stored[p], 16)

            pipelined(sp, BLOCKS, [(load, 0), (store, 3)])
            for i in range(2):
                sp.wait_ge(stored[i], 16 * ((BLOCKS + 1 - i) // 2))

        @block.gpsimd
        def _(pool):
            identity(pool, ident, zeroed, ident_made)

        @block.tensor
        def _(pe):
            pe.wait_ge(ident_made, 1)

            def transpose_rows(b, p):
                after(pe, (rows_loaded[p], slot_full(b, p)), (lo_kept, b - 1), tick=pe_tick)
                for k in range(KD):
                    mm = pe.transpose(pt[p][:, P * k:P * k + P], rows[:, p, P * k:P * k + P], ident[:, :])
                mm.then_inc(t_made, 1)

            expert_at = [None]

            def find_expert(b, p):
                expert_at[0] = pe.value_load(table[0:1, 1, bass.ds(b, 1)], min_val=0, max_val=(EXPERTS - 1) * DIM)

            def multiply(b, p):
                after(pe, (biased_made, b - 1), (hi_kept, b + 1), tick=pe_tick)
                for k in range(KD):
                    hi, cols = rowsT_hi[:, p, P * k:P * k + P], bass.ds(expert_at[0] * KD + k * DIM, DIM)
                    pe.matmul(py[p][:, :], hi, w_hi[:, cols], start=k == 0, stop=False)
                    pe.matmul(py[p][:, :], hi, w_lo[:, cols], start=False, stop=False)
                after(pe, (lo_kept, b + 1), tick=pe_tick)
                for k in range(KD):
                    lo, cols = rowsT_lo[:, p, P * k:P * k + P], bass.ds(expert_at[0] * KD + k * DIM, DIM)
                    mm = pe.matmul(py[p][:, :], lo, w_hi[:, cols], start=False, stop=k == KD - 1)
                mm.then_inc(y_made, 1)

            pipelined(pe, BLOCKS, [(find_expert, 1), (transpose_rows, 0), (multiply, 1)])

        @block.scalar
        def _(act):
            def keep_high(b, p):
                after(act, (t_made, b + 1), (y_made, b - 1), tick=act_tick)
                act.activation(rowsT_hi[:, p, :], pt[p][:, :], ACT.Copy).then_inc(hi_kept, 1)

            def rectify(b, p):
                after(act, (biased_made, b + 1), (stored[p], slot_full(b, p) - 16), tick=act_tick)
                act.activation(result[:, p, :], biased[:, p, :], ACT.Relu, scale=0.5).then_inc(result_made, 1)

            pipelined(act, BLOCKS, [(keep_high, 0), (rectify, 2)])

        @block.vector
        def _(dve):
            def keep_low(b, p):
                after(dve, (hi_kept, b + 1), (y_made, b - 1), tick=dve_tick)
                dve.tensor_tensor(rowsT_lo[:, p, :], pt[p][:, :], rowsT_hi[:, p, :].bitcast(F32), ALU.subtract).then_inc(lo_kept, 1)

            def add_bias(b, p):
                at = dve.value_load(table[0:1, 1, bass.ds(b, 1)], min_val=0, max_val=(EXPERTS - 1) * DIM)
                if isinstance(b, int) and b == 0:
                    dve.wait_ge(bias_loaded, 16)
                after(dve, (y_made, b + 1), (result_made, b - 1), tick=dve_tick)
                dve.tensor_tensor(biased[:, p, :], py[p][:, :], bias[:, bass.ds(at, DIM)], ALU.add).then_inc(biased_made, 1)

            pipelined(dve, BLOCKS, [(keep_low, 0), (add_bias, 1)])


GUC = 2 * KD * INTER // TILES


def layer1_phase(nc, shared, a):
    with ExitStack() as stack:
        c = Ctx(nc, stack, "c_")
        sb, pb, sem = c.sb, c.pb, c.sem
        proj_hi, proj_lo = sb("proj_hi", [P, 2, KD * DIM], F32R), sb("proj_lo", [P, 2, KD * DIM], F32R)
        wk, wv = sb("wk", [P, KD, P]), sb("wv", [P, KD, P])
        ident, minus_half, own_head = sb("ident", [P, P]), sb("minus_half", [P, 1]), sb("own_head", [P, KVH])
        stage = sb("stage", [P, 2, 1024])
        x_in, x_out, xn, q_rows, qT, attn, ctxT = (sb(n, [P, 2, DIM]) for n in ("x_in", "x_out", "xn", "q_rows", "qT", "attn", "ctxT"))
        y_in, y_at = sb("y_in", [P, 2, 2, DIM]), sb("y_at", [P, 2, 2], I32)
        xT_hi, xT_lo, aT_hi, aT_lo = (sb(n, [P, 2, DIM], F32R) for n in ("xT_hi", "xT_lo", "aT_hi", "aT_lo"))
        kT, keys, values = sb("kT", [P, 2, P]), sb("keys", [P, 2, 2, DIM]), sb("values", [P, 2, 2, 4, 2, HD + 1])
        score, probT = sb("score", [P, 2, DIM]), sb("probT", [P, 2, DIM])
        smax, rsum = sb("smax", [P, 2, KVH]), sb("rsum", [P, 2, 2, KVH, 1])
        stats, mv, rstd = sb("stats", [P, 2, 6]), sb("mv", [P, 2, 2]), sb("rstd", [P, 2, 2])
        n_out, stats3, mv3, rstd3 = sb("n_out", [P, 2, DIM]), sb("stats3", [P, 2, 6]), sb("mv3", [P, 2, 2]), sb("rstd3", [P, 2, 2])
        ps, pt, po = ([pb(f"{n}{i}") for i in range(2)] for n in ("ps", "pt", "po"))
        pg, ph = pb("pg"), pb("ph")

        names = ("zeroed const_made weights_loaded proj_hi_made proj_lo_made gu_hi gu_lo x2_added x2_ready stat_step mv_ready rs_step "
                 "rs_ready xn_ready xt_made xhi_kept xlo_kept q_made q_kept kv_made kt_kept v_kept keys_ready s_made max_step "
                 "q_rows_kept qt_made s_shifted exp_done pt_made pt_kept o_made sum_step o_kept at_made ahi_kept alo_kept w_made x3_ready yat_ready")
        (zeroed, const_made, weights_loaded, proj_hi_made, proj_lo_made, gu_hi, gu_lo, x2_added, x2_ready, stat_step, mv_ready, rs_step,
         rs_ready, xn_ready, xt_made, xhi_kept, xlo_kept, q_made, q_kept, kv_made, kt_kept, v_kept, keys_ready, s_made, max_step,
         q_rows_kept, qt_made, s_shifted, exp_done, pt_made, pt_kept, o_made, sum_step, o_kept, at_made, ahi_kept, alo_kept, w_made, x3_ready,
         yat_ready) = (sem(n) for n in names.split())
        stat3_step, mv3_ready, rs3_step, rs3_ready, n_ready = (sem(n) for n in ("stat3_step", "mv3_ready", "rs3_step", "rs3_ready", "n_ready"))
        n_stored = [sem(f"n_stored{i}") for i in range(2)]
        proj_loaded = [sem(f"proj_loaded{i}") for i in range(4)]
        x1_loaded, ctx_loaded, y_loaded, gu_loaded, x2_stored, x2_loaded, x3_stored = (
            [sem(f"{n}{i}") for i in range(2)] for n in ("x1_loaded", "ctx_loaded", "y_loaded", "gu_loaded", "x2_stored", "x2_loaded", "x3_stored"))
        sp_tick, act_tick, pool_tick, pe_tick, dve_tick = (sem(e + "_tick") for e in ("sp", "act", "pool", "pe", "dve"))
        N_CONST = 6
        stack.callback(c.clear)
        block = stack.enter_context(nc.Block())
        wq_v = a["Wq"].rearrange("(k p) n -> p k n", p=P)
        wo_v = a["Wo"].rearrange("(k p) n -> p k n", p=P)

        def first(t):
            return isinstance(t, int) and t == 0

        @block.sync
        def _(sp):
            def load_weights():
                for n in range(4):
                    if n >= 2:
                        sp.wait_ge(proj_lo_made, n - 1)
                    src = (wq_v, wo_v)[n // 2][:, 2 * (n % 2):2 * (n % 2) + 2, :]
                    sp.dma_start(stage[:, n % 2, :].rearrange("p (k n) -> p k n", k=2), src).then_inc(proj_loaded[n], 16)
                    if n == 1:
                        sp.dma_start(wk[:, :, :], a["Wk"].rearrange("(k p) n -> p k n", p=P)).then_inc(weights_loaded, 16)
                        sp.dma_start(wv[:, :, :], a["Wv"].rearrange("(k p) n -> p k n", p=P)).then_inc(weights_loaded, 16)

            def load_x1_rows(t, p):
                after(sp, (xn_ready, t - 1), (x2_stored[p], slot_full(t, p) - 16), tick=sp_tick)
                sp.dma_start(x_in[:, p, :], shared["x1"][t, :, :]).then_inc(x1_loaded[p], 16)

            def load_x1(t, p):
                if first(t):
                    load_x1_rows(0, 0)
                    load_x1_rows(1, 1)
                    load_weights()
                elif not (isinstance(t, int) and t == 1):
                    load_x1_rows(t, p)

            def load_ctx(t, p):
                after(sp, (kv_made, t - 1), tick=sp_tick)
                sp.dma_start(ctxT[:, p, :], a["ctxT"][t, :, :]).then_inc(ctx_loaded[p], 16)

            def load_gate_up(t, p):
                after(sp, (gu_lo, t - 1), tick=sp_tick)
                if isinstance(t, int) and t < 2:
                    sp.wait_ge(proj_lo_made, 3 + t)
                sp.dma_start(stage[:, p, 0:GUC], a["gate_up"][t, :, :]).then_inc(gu_loaded[p], 16)

            def store_x2(t, p):
                after(sp, (x2_ready, t + 1), tick=sp_tick)
                sp.dma_start(shared["x2"][t, :, :], x_in[:, p, :]).then_inc(x2_stored[p], 16)

            def load_x2(t, p):
                after(sp, (x2_stored[p], slot_full(t, p)), (x3_stored[p], slot_full(t, p) - 16), (n_ready, t - 1), tick=sp_tick)
                sp.dma_start(x_out[:, p, :], shared["x2"][t, :, :]).then_inc(x2_loaded[p], 16)

            def store_x3(t, p):
                after(sp, (x3_ready, t + 1), tick=sp_tick)
                sp.dma_start(shared["x3"][t, :, :], x_out[:, p, :]).then_inc(x3_stored[p], 16)

            def store_norm(t, p):
                after(sp, (n_ready, t + 1), tick=sp_tick)
                sp.dma_start(shared["n3"][t, :, :], n_out[:, p, :]).then_inc(n_stored[p], 16)

            pipelined(sp, TILES, [(load_ctx, 1), (load_gate_up, 2), (store_x2, 2), (store_x3, 5), (store_norm, 5), (load_x2, 3), (load_x1, 0)])
            for i in range(2):
                sp.wait_ge(n_stored[i], 8 * TILES)
                sp.wait_ge(x3_stored[i], 8 * TILES)

        @block.gpsimd
        def _(pool):
            def make_constants():
                pool.memset(keys[:], 0.0).then_inc(const_made, 1)
                pool.memset(minus_half[:, :], -0.5).then_inc(const_made, 1)
                pool.memset(values[:], 0.0).then_inc(zeroed, 1)
                pool.memset(ident[:, :], 0.0).then_inc(zeroed, 1)
                pool.memset(own_head[:, :], 1.0).then_inc(zeroed, 1)
                pool.wait_ge(zeroed, 3)
                for r in range(2):
                    pool.memset(values[64 * r:64 * r + 64, :, :, :, r, HD:HD + 1], 1.0).then_inc(const_made, 1)
                    pool.wait_ge(const_made, 3 + r)
                pool.affine_select(out=ident[:, :], in_=ident[:, :], compare_op=ALU.not_equal, fill=1.0,
                                   base=0, pattern=[[-1, P]], channel_multiplier=1).then_inc(const_made, 1)
                pool.affine_select(out=own_head[:, :], in_=own_head[:, :], compare_op=ALU.is_ge, fill=0.0,
                                   base=0, pattern=[[-HD, KVH]], channel_multiplier=1).then_inc(zeroed, 1)
                pool.wait_ge(zeroed, 4)
                pool.affine_select(out=own_head[:, :], in_=own_head[:, :], compare_op=ALU.is_ge, fill=0.0,
                                   base=HD - 1, pattern=[[HD, KVH]], channel_multiplier=-1).then_inc(const_made, 1)
                pool.wait_ge(const_made, N_CONST)

            def gather_rows(t, p):
                after(pool, (x2_ready, t - 1), (y_loaded[p], 2 * slot_full(t, p) - 32), tick=pool_tick)
                pool.tensor_copy(y_at[:, p, :], shared["y_at"][:, bass.ds(2 * t, 2)]).then_inc(yat_ready, 1)
                after(pool, (yat_ready, t + 1), tick=pool_tick)
                for k in range(2):
                    pool.indirect_dma_start(out=y_in[:, p, k, :], out_offset=None, in_=shared["ys"],
                                            in_offset=bass.IndirectOffsetOnAxis(ap=y_at[:, p, k:k + 1], axis=0)).then_inc(y_loaded[p], 16)

            def gather(t, p):
                if first(t):
                    gather_rows(0, 0)
                    gather_rows(1, 1)
                    make_constants()
                elif not (isinstance(t, int) and t == 1):
                    gather_rows(t, p)

            def add_first(t, p):
                after(pool, (x1_loaded[p], slot_full(t, p)), (y_loaded[p], 2 * slot_full(t, p)), tick=pool_tick)
                pool.tensor_tensor(x_in[:, p, :], x_in[:, p, :], y_in[:, p, 0, :], ALU.add).then_inc(x2_added, 1)

            def inverse_deviation(t, m, r, step, done):
                pool.tensor_scalar(m[:, 1:2], m[:, 1:2], EPS, None, ALU.add).then_inc(step, 1)
                after(pool, (step, 2 * t + 1), tick=pool_tick)
                pool.tensor_tensor(r[:, 0:1], m[:, 1:2], minus_half[:, :], ALU.pow).then_inc(step, 1)
                after(pool, (step, 2 * t + 2), tick=pool_tick)
                pool.tensor_scalar(r[:, 1:2], m[:, 0:1], -1.0, r[:, 0:1], ALU.mult, ALU.mult).then_inc(done, 1)

            def scale_x2(t, p):
                after(pool, (mv_ready, t + 1), (xn_ready, t - 1), tick=pool_tick)
                inverse_deviation(t, mv[:, p, :], rstd[:, p, :], rs_step, rs_ready)

            def scale_x3(t, p):
                after(pool, (mv3_ready, t + 1), (n_ready, t - 1), tick=pool_tick)
                inverse_deviation(t, mv3[:, p, :], rstd3[:, p, :], rs3_step, rs3_ready)

            def spread_keys(t, p):
                after(pool, (kt_kept, t + 1), (s_made, 4 * t - 4), tick=pool_tick)
                for b in range(2):
                    pool.tensor_tensor(keys[:, p, b, :].rearrange("p (h e) -> p h e", h=KVH),
                                       kT[:, p, 64 * b:64 * b + 64].rearrange("p (x e) -> p x e", x=1).to_broadcast([P, KVH, 64]),
                                       own_head[:, :].rearrange("p (h x) -> p h x", x=1).to_broadcast([P, KVH, 64]), ALU.mult).then_inc(keys_ready, 1)

            def low_part(t, p):
                after(pool, (gu_hi, t + 1), tick=pool_tick)
                dst = bass.ds(GUC * t, GUC)
                pool.tensor_tensor(shared["gu_lo"][:, dst], stage[:, p, 0:GUC], shared["gu_hi"][:, dst].bitcast(F32), ALU.subtract).then_inc(gu_lo, 1)

            pipelined(pool, TILES, [(add_first, 1), (scale_x2, 1), (scale_x3, 4), (gather, 0), (low_part, 3), (spread_keys, 2)])

        @block.scalar
        def _(act):
            def high_weights(n):
                act.wait_ge(proj_loaded[n], 16)
                act.activation(proj_hi[:, n // 2, 1024 * (n % 2):1024 * (n % 2) + 1024], stage[:, n % 2, :], ACT.Copy).then_inc(proj_hi_made, 1)

            high_weights(0)
            high_weights(1)

            def keep_kT(t, p):
                after(act, (kv_made, t + 1), (keys_ready, 2 * t - 2), tick=act_tick)
                act.activation(kT[:, p, :], pg[:, 0:P], ACT.Copy).then_inc(kt_kept, 1)

            def norm_x(t, p):
                after(act, (rs_ready, t + 1), (xt_made, t - 1), tick=act_tick)
                act.activation(xn[:, p, :], x_in[:, p, :], ACT.Identity, scale=rstd[:, p, 0:1], bias=rstd[:, p, 1:2]).then_inc(xn_ready, 1)
                if first(t):
                    high_weights(2)
                    high_weights(3)

            def norm_x3(t, p):
                after(act, (rs3_ready, t + 1), (n_stored[p], slot_full(t, p) - 16), tick=act_tick)
                act.activation(n_out[:, p, :], x_out[:, p, :], ACT.Identity, scale=rstd3[:, p, 0:1], bias=rstd3[:, p, 1:2]).then_inc(n_ready, 1)

            def keep_high_x(t, p):
                after(act, (xt_made, t + 1), (q_made, t - 1), tick=act_tick)
                act.activation(xT_hi[:, p, :], pg[:, :], ACT.Copy).then_inc(xhi_kept, 1)

            def keep_q_rows(t, p):
                after(act, (q_made, t + 1), (qt_made, t - 1), tick=act_tick)
                act.activation(q_rows[:, p, :], ph[:, :], ACT.Copy).then_inc(q_rows_kept, 1)

            def keep_q(t, p):
                after(act, (qt_made, t + 1), (s_made, 4 * t - 4), tick=act_tick)
                act.activation(qT[:, p, :].rearrange("p (b g q) -> p g b q", b=2, g=GROUP),
                               ph[:, :].rearrange("p (g b q) -> p g b q", g=GROUP, b=2), ACT.Copy).then_inc(q_kept, 1)

            def exponent(i):
                def stage_(t, p):
                    after(act, (s_shifted, 4 * t + i + 1), tick=act_tick)
                    act.activation(score[:, i % 2, :], score[:, i % 2, :], ACT.Exp, scale=SCALE1).then_inc(exp_done, 1)
                return stage_

            def keep_probT(i):
                def stage_(t, p):
                    after(act, (pt_made, 4 * t + i + 1), (o_made, 4 * t + i - 1), tick=act_tick)
                    act.activation(probT[:, i % 2, :], pt[i % 2][:, :], ACT.Copy).then_inc(pt_kept, 1)
                return stage_

            def keep_high_attn(t, p):
                after(act, (at_made, t + 1), (w_made, t - 1), tick=act_tick)
                act.activation(aT_hi[:, p, :].rearrange("p (g b q) -> p b g q", g=GROUP, b=2),
                               pg[:, :].rearrange("p (b g q) -> p b g q", b=2, g=GROUP), ACT.Copy).then_inc(ahi_kept, 1)

            def high_part(t, p):
                after(act, (gu_loaded[p], slot_full(t, p)), tick=act_tick)
                act.activation(shared["gu_hi"][:, bass.ds(GUC * t, GUC)], stage[:, p, 0:GUC], ACT.Copy).then_inc(gu_hi, 1)

            pipelined(act, TILES, [(keep_high_attn, 4), (exponent(0), 3), (exponent(1), 3), (keep_high_x, 2), (keep_probT(0), 3),
                                   (exponent(2), 3), (keep_probT(1), 3), (exponent(3), 3), (keep_kT, 2), (keep_probT(2), 3), (norm_x3, 4),
                                   (keep_probT(3), 3), (norm_x, 1), (keep_q_rows, 2), (high_part, 2), (keep_q, 2)])

        @block.tensor
        def _(pe):
            pe.wait_ge(const_made, N_CONST)

            def transpose_x(t, p):
                after(pe, (ahi_kept, t - 1), (alo_kept, t - 1), (kt_kept, t), (v_kept, 4 * t), (xn_ready, t + 1), tick=pe_tick)
                for k in range(KD):
                    mm = pe.transpose(pg[:, P * k:P * k + P], xn[:, p, P * k:P * k + P], ident[:, :])
                mm.then_inc(xt_made, 1)

            def product(which, hi, lo, lo_kept):
                for k in range(KD):
                    rows, cols = slice(P * k, P * k + P), slice(DIM * k, DIM * k + DIM)
                    pe.matmul(ph[:, :], hi[:, rows], proj_hi[:, which, cols], start=k == 0, stop=False)
                    pe.matmul(ph[:, :], hi[:, rows], proj_lo[:, which, cols], start=False, stop=False)
                after(pe, lo_kept, tick=pe_tick)
                for k in range(KD):
                    rows, cols = slice(P * k, P * k + P), slice(DIM * k, DIM * k + DIM)
                    mm = pe.matmul(ph[:, :], lo[:, rows], proj_hi[:, which, cols], start=False, stop=k == KD - 1)
                return mm

            def make_q(t, p):
                if first(t):
                    pe.wait_ge(proj_lo_made, 2)
                after(pe, (x3_ready, t - 1), (xhi_kept, t + 1), tick=pe_tick)
                product(0, xT_hi[:, p, :], xT_lo[:, p, :], (xlo_kept, t + 1)).then_inc(q_made, 1)

            def transpose_q(t, p):
                after(pe, (q_rows_kept, t + 1), tick=pe_tick)
                for g in range(GROUP):
                    mm = pe.transpose(ph[:, P * g:P * g + P], q_rows[:, p, P * g:P * g + P], ident[:, :])
                mm.then_inc(qt_made, 1)

            def make_kv(t, p):
                if first(t):
                    pe.wait_ge(weights_loaded, 32)
                after(pe, (ctx_loaded[p], slot_full(t, p)), (xhi_kept, t + 1), (xlo_kept, t + 1), tick=pe_tick)
                rows = ctxT[:, p, :].rearrange("p (k n) -> p k n", k=KD)
                for k in range(KD):
                    pe.matmul(pg[:, 0:P], wk[:, k, :], rows[:, k, :], start=k == 0, stop=k == KD - 1)
                for k in range(KD):
                    mm = pe.matmul(pg[:, P:2 * P], rows[:, k, :], wv[:, k, :], start=k == 0, stop=k == KD - 1)
                mm.then_inc(kv_made, 1)

            def scores(i):
                def stage_(t, p):
                    after(pe, (q_kept, t + 1), (keys_ready, 2 * t + 2), (s_shifted, 4 * t + i - 1), tick=pe_tick)
                    pe.matmul(ps[i % 2][:, :], qT[:, p, P * i:P * i + P], keys[:, p, i // 2, :], start=True, stop=True).then_inc(s_made, 1)
                return stage_

            def transpose_probs(i):
                def stage_(t, p):
                    after(pe, (exp_done, 4 * t + i + 1), (pt_kept, 4 * t + i - 1), tick=pe_tick)
                    for j in range(4):
                        mm = pe.transpose(pt[i % 2][:, P * j:P * j + P], score[:, i % 2, P * j:P * j + P], ident[:, :])
                    mm.then_inc(pt_made, 1)
                return stage_

            def attend(i):
                def stage_(t, p):
                    b = i // 2
                    after(pe, (pt_kept, 4 * t + i + 1), (o_kept, 2 * t + b - 1), tick=pe_tick)
                    for j in range(4):
                        at = 136 * (i % 2) + 34 * j
                        mm = pe.matmul(po[b][:, at:at + 34], probT[:, i % 2, P * j:P * j + P],
                                       values[:, p, b, j, :, :].rearrange("p r d -> p (r d)"), start=True, stop=True)
                    mm.then_inc(o_made, 1)
                return stage_

            def transpose_attn(t, p):
                after(pe, (o_kept, 2 * t + 2), (kt_kept, upto(t + 2, TILES)), (v_kept, 4 * upto(t + 2, TILES)), tick=pe_tick)
                for i in range(4):
                    mm = pe.transpose(pg[:, P * i:P * i + P], attn[:, p, P * i:P * i + P], ident[:, :])
                mm.then_inc(at_made, 1)

            def project(t, p):
                if first(t):
                    pe.wait_ge(proj_lo_made, 4)
                after(pe, (q_kept, upto(t + 2, TILES)), (ahi_kept, t + 1), tick=pe_tick)
                product(1, aT_hi[:, p, :], aT_lo[:, p, :], (alo_kept, t + 1)).then_inc(w_made, 1)

            pipelined(pe, TILES, [(scores(0), 3), (transpose_attn, 4), (scores(1), 3), (project, 4), (transpose_x, 2), (transpose_probs(0), 3),
                                  (scores(2), 3), (transpose_probs(1), 3), (scores(3), 3), (attend(0), 3), (make_kv, 2), (transpose_probs(2), 3),
                                  (attend(1), 3), (transpose_probs(3), 3), (make_q, 2), (attend(2), 3), (transpose_q, 2), (attend(3), 3)])

        @block.vector
        def _(dve):
            def low_weights(n):
                dve.wait_ge(proj_hi_made, n + 1)
                cols = slice(1024 * (n % 2), 1024 * (n % 2) + 1024)
                dve.tensor_tensor(proj_lo[:, n // 2, cols], stage[:, n % 2, :], proj_hi[:, n // 2, cols].bitcast(F32), ALU.subtract).then_inc(proj_lo_made, 1)

            low_weights(0)
            low_weights(1)

            def add_second(t, p):
                after(dve, (x2_added, t + 1), tick=dve_tick)
                dve.tensor_tensor(x_in[:, p, :], x_in[:, p, :], y_in[:, p, 1, :], ALU.add).then_inc(x2_ready, 1)

            def sum_x2(t, p):
                after(dve, (x2_ready, t + 1), tick=dve_tick)
                dve.bn_stats(stats[:, p, :], x_in[:, p, :]).then_inc(stat_step, 1)

            def average_x2(t, p):
                after(dve, (stat_step, t + 1), (rs_ready, t - 1), tick=dve_tick)
                dve.bn_aggr(mv[:, p, :], stats[:, p, :]).then_inc(mv_ready, 1)
                if first(t):
                    low_weights(2)
                    low_weights(3)

            def keep_low_x(t, p):
                after(dve, (xhi_kept, t + 1), (q_made, t - 1), tick=dve_tick)
                dve.tensor_tensor(xT_lo[:, p, :], pg[:, :], xT_hi[:, p, :].bitcast(F32), ALU.subtract).then_inc(xlo_kept, 1)

            def keep_values(t, p):
                if first(t):
                    dve.wait_ge(const_made, N_CONST)
                after(dve, (kt_kept, t + 1), (o_made, 4 * t - 4), tick=dve_tick)
                for r in range(2):
                    for b in range(2):
                        made = pg[64 * b:64 * b + 64, P:2 * P].rearrange("p (j r d) -> p j r d", j=4, r=2)
                        dve.tensor_copy(values[64 * r:64 * r + 64, p, b, :, r, 0:HD], made[:, :, r, :]).then_inc(v_kept, 1)

            def score_rows(i):
                return ps[i % 2][:, :].rearrange("p (h e) -> p h e", h=KVH)

            def max_scores(i):
                def stage_(t, p):
                    after(dve, (s_made, 4 * t + i + 1), tick=dve_tick)
                    dve.tensor_reduce(smax[:, i % 2, :], score_rows(i), AX.X, ALU.max).then_inc(max_step, 1)
                return stage_

            def shift_scores(i):
                def stage_(t, p):
                    after(dve, (max_step, 4 * t + i + 1), (pt_made, 4 * t + i - 1), tick=dve_tick)
                    peak = smax[:, i % 2, :].rearrange("p (h x) -> p h x", x=1).to_broadcast([P, KVH, 64])
                    dve.tensor_tensor(score[:, i % 2, :].rearrange("p (h e) -> p h e", h=KVH), score_rows(i), peak, ALU.subtract).then_inc(s_shifted, 1)
                return stage_

            def heads(b):
                return po[b][:, 0:272].rearrange("p (c h d) -> p c h d", c=2, h=KVH)

            def invert_sums(b):
                def stage_(t, p):
                    after(dve, (o_made, 4 * t + 2 * b + 2), tick=dve_tick)
                    dve.reciprocal(rsum[:, b, :, :, :], heads(b)[:, :, :, HD:HD + 1]).then_inc(sum_step, 1)
                return stage_

            def keep_attn(b):
                def stage_(t, p):
                    after(dve, (sum_step, 2 * t + b + 1), (at_made, t - 1), tick=dve_tick)
                    dve.tensor_tensor(attn[:, p, 256 * b:256 * b + 256].rearrange("p (c h d) -> p c h d", c=2, h=KVH), heads(b)[:, :, :, 0:HD],
                                      rsum[:, b, :, :, :].to_broadcast([P, 2, KVH, HD]), ALU.mult).then_inc(o_kept, 1)
                return stage_

            def keep_low_attn(t, p):
                after(dve, (ahi_kept, t + 1), (w_made, t - 1), tick=dve_tick)
                order = "p (g b q) -> p b g q"
                dve.tensor_tensor(aT_lo[:, p, :].rearrange(order, g=GROUP, b=2), pg[:, :].rearrange("p (b g q) -> p b g q", b=2, g=GROUP),
                                  aT_hi[:, p, :].bitcast(F32).rearrange(order, g=GROUP, b=2), ALU.subtract).then_inc(alo_kept, 1)

            def add_attn(t, p):
                after(dve, (w_made, t + 1), (x2_loaded[p], slot_full(t, p)), tick=dve_tick)
                dve.tensor_tensor(x_out[:, p, :], ph[:, :], x_out[:, p, :], ALU.add).then_inc(x3_ready, 1)

            def sum_x3(t, p):
                after(dve, (x3_ready, t + 1), tick=dve_tick)
                dve.bn_stats(stats3[:, p, :], x_out[:, p, :]).then_inc(stat3_step, 1)

            def average_x3(t, p):
                after(dve, (stat3_step, t + 1), (rs3_ready, t - 1), tick=dve_tick)
                dve.bn_aggr(mv3[:, p, :], stats3[:, p, :]).then_inc(mv3_ready, 1)

            pipelined(dve, TILES, [(max_scores(0), 3), (keep_low_attn, 4), (shift_scores(0), 3), (max_scores(1), 3), (add_second, 1),
                                   (shift_scores(1), 3), (sum_x2, 1), (add_attn, 4), (average_x2, 1), (keep_low_x, 2), (max_scores(2), 3),
                                   (sum_x3, 4), (shift_scores(2), 3), (average_x3, 4), (max_scores(3), 3), (shift_scores(3), 3), (keep_values, 2),
                                   (invert_sums(0), 3), (keep_attn(0), 3), (invert_sums(1), 3), (keep_attn(1), 3)])


def ffn_phase(nc, shared, a, out):
    TOK, GROUPS, LAST = TG * P, TILES // TG, NI - 1
    with ExitStack() as stack:
        c = Ctx(nc, stack, "d_")
        sb, pb, sem = c.sb, c.pb, c.sem
        down_hi, down_lo = sb("down_hi", [P, NI, DIM], F32R), sb("down_lo", [P, NI, DIM], F32R)
        ident = sb("ident", [P, P])
        b_gate, b_up, minus_gate, b_down = sb("b_gate", [P, NI]), sb("b_up", [P, NI]), sb("minus_gate", [P, NI]), sb("b_down", [P, DIM])
        stage, n_in, x_res = sb("stage", [P, 2, DIM]), sb("n_in", [P, TG, DIM]), sb("x_res", [P, TG, DIM])
        nT_hi, nT_lo = sb("nT_hi", [P, KD, TOK], F32R), sb("nT_lo", [P, KD, TOK], F32R)
        expo, hid = sb("expo", [P, 2, TOK]), sb("hid", [P, 2, TOK])
        hid_hi, hid_lo = sb("hid_hi", [P, 2, TOK], F32R), sb("hid_lo", [P, 2, TOK], F32R)
        pgate, pup = [pb(f"pgate{i}") for i in range(2)], [pb(f"pup{i}") for i in range(2)]
        pdown = [pb(f"pdown{i}") for i in range(TG)]
        tbank = (pgate[1], pup[1])
        names = ("zeroed ident_made bias_loaded minus_made down_hi_made down_lo_made t_made nhi_kept nlo_kept gate_made up_made "
                 "expo_made expo_step gated hid_made hi_made lo_made down_done bank_done res_biased y_ready")
        (zeroed, ident_made, bias_loaded, minus_made, down_hi_made, down_lo_made, t_made, nhi_kept, nlo_kept, gate_made, up_made,
         expo_made, expo_step, gated, hid_made, hi_made, lo_made, down_done, bank_done, res_biased, y_ready) = (sem(n) for n in names.split())
        n_loaded, res_loaded, stored = ([sem(f"{n}{i}") for i in range(TG)] for n in ("n_loaded", "res_loaded", "stored"))
        down_loaded = [sem(f"down_loaded{i}") for i in range(2)]
        sp_tick, act_tick, pool_tick, pe_tick, dve_tick = (sem(e + "_tick") for e in ("sp", "act", "pool", "pe", "dve"))
        stack.callback(c.clear)
        block = stack.enter_context(nc.Block())
        out_v = out.rearrange("(t b) s d -> t (b s) d", b=2)
        gu_hi, gu_lo = shared["gu_hi"], shared["gu_lo"]

        def width(i):
            return min(P, INTER - P * i)

        def read_before(g, i):
            return NI * g + i - (1 if i else 0)

        def down_before(g, i):
            return (down_done, LAST * g + i - 1) if i else (bank_done, TG * g)

        @block.sync
        def _(sp):
            def load(g):
                for n in range(TG):
                    after(sp, (t_made, TG * (g - 1) + n + 1), tick=sp_tick)
                    sp.dma_start(n_in[:, n, :], shared["n3"][TG * g + n, :, :]).then_inc(n_loaded[n], 16)

            def store(g, n):
                after(sp, (y_ready, TG * g + n + 1), tick=sp_tick)
                sp.dma_start(out_v[TG * g + n, :, :], x_res[:, n, :]).then_inc(stored[n], 16)

            def load_residual(g):
                for n in range(TG):
                    after(sp, (stored[n], 16 * g), tick=sp_tick)
                    sp.dma_start(x_res[:, n, :], shared["x3"][TG * g + n, :, :]).then_inc(res_loaded[n], 16)

            load(0)
            for buf, b in ((b_gate, "b_gate"), (b_up, "b_up")):
                sp.dma_start(buf[:, 0:LAST], a[b + "_main"]).then_inc(bias_loaded, 16)
                sp.dma_start(buf[0:width(LAST), LAST:NI], a[b + "_rest"]).then_inc(bias_loaded, 16)
            sp.dma_start(b_down[:, :], a["b_down"].partition_broadcast(P)).then_inc(bias_loaded, 16)
            for i in range(NI):
                if i >= 2:
                    sp.wait_ge(down_lo_made, i - 1)
                sp.dma_start(stage[0:width(i), i % 2, :], a["w_down"][P * i:P * i + width(i), :]).then_inc(down_loaded[i % 2], 16)
            load_residual(0)
            with sp.Fori(1, GROUPS) as g:
                load(g)
                for n in range(TG):
                    store(g - 1, n)
                load_residual(g)
            for n in range(TG):
                store(GROUPS - 1, n)
            for n in range(TG):
                sp.wait_ge(stored[n], 16 * GROUPS)

        @block.gpsimd
        def _(pool):
            identity(pool, ident, zeroed, ident_made)
            pool.wait_ge(bias_loaded, 80)
            pool.tensor_scalar(minus_gate[:, 0:LAST], b_gate[:, 0:LAST], -1.0, None, ALU.mult).then_inc(minus_made, 1)
            pool.wait_ge(minus_made, 1)
            pool.tensor_scalar(minus_gate[0:width(LAST), LAST:NI], b_gate[0:width(LAST), LAST:NI], -1.0, None, ALU.mult).then_inc(minus_made, 1)
            for i in range(NI):
                pool.wait_ge(down_hi_made, i + 1)
                w = width(i)
                pool.tensor_tensor(down_lo[0:w, i, :], stage[0:w, i % 2, :], down_hi[0:w, i, :].bitcast(F32), ALU.subtract).then_inc(down_lo_made, 1)

            def group(g):
                for n in range(TG):
                    after(pool, (res_loaded[n], 16 * g + 16), tick=pool_tick)
                    pool.tensor_tensor(x_res[:, n, :], x_res[:, n, :], b_down[:, :], ALU.add).then_inc(res_biased, 1)

            pool.wait_ge(minus_made, 2)
            with pool.Fori(0, GROUPS) as g:
                group(g)

        @block.scalar
        def _(act):
            def keep_high_n(g, n):
                after(act, (t_made, TG * g + n + 1), tick=act_tick)
                act.activation(nT_hi[:, :, P * n:P * n + P], tbank[n % 2][:, :].rearrange("p (k n) -> p k n", k=KD), ACT.Copy).then_inc(nhi_kept, 1)

            def exponent(g, i):
                w = width(i)
                if isinstance(g, int) and i == 0:
                    act.wait_ge(minus_made, 2)
                after(act, (gate_made, NI * g + i + 1), (gated, read_before(g, i)), tick=act_tick)
                act.activation(expo[0:w, i % 2, :], pgate[i % 2][0:w, :], ACT.Exp, scale=-1.0, bias=minus_gate[0:w, i:i + 1]).then_inc(expo_made, 1)

            def keep_high(g, i):
                w = width(i)
                after(act, (hid_made, NI * g + i + 1), down_before(g, i), tick=act_tick)
                act.activation(hid_hi[0:w, i % 2, :], hid[0:w, i % 2, :], ACT.Copy).then_inc(hi_made, 1)

            def group(g):
                keep_high_n(g, 0)
                keep_high_n(g, 1)
                if not isinstance(g, int):
                    keep_high(g - 1, LAST)
                keep_high_n(g, 2)
                keep_high_n(g, 3)
                for i in range(NI):
                    if isinstance(g, int):
                        w = width(i)
                        act.wait_ge(down_loaded[i % 2], 16 * (i // 2 + 1))
                        act.activation(down_hi[0:w, i, :], stage[0:w, i % 2, :], ACT.Copy).then_inc(down_hi_made, 1)
                    exponent(g, i)
                    if i:
                        keep_high(g, i - 1)

            group(0)
            with act.Fori(1, GROUPS) as g:
                group(g)
            keep_high(GROUPS - 1, LAST)

        @block.tensor
        def _(pe):
            pe.wait_ge(ident_made, 1)

            def transpose_n(g, n):
                free = (nlo_kept, TG * g + n - 1) if n >= 2 else ((gated, hid_made)[n], NI * g - 1)
                after(pe, (n_loaded[n], 16 * g + 16), free, tick=pe_tick)
                for k in range(KD):
                    mm = pe.transpose(tbank[n % 2][:, P * k:P * k + P], n_in[:, n, P * k:P * k + P], ident[:, :])
                mm.then_inc(t_made, 1)

            def product(g, i, which, bank, read, made):
                w = width(i)
                after(pe, (read, read_before(g, i)), tick=pe_tick)
                for k in range(KD):
                    cols = slice((which * KD + k) * INTER + P * i, (which * KD + k) * INTER + P * i + w)
                    pe.matmul(bank[0:w, :], gu_hi[:, cols], nT_hi[:, k, :], start=k == 0, stop=False)
                    pe.matmul(bank[0:w, :], gu_hi[:, cols], nT_lo[:, k, :], start=False, stop=False)
                    mm = pe.matmul(bank[0:w, :], gu_lo[:, cols], nT_hi[:, k, :], start=False, stop=k == KD - 1)
                mm.then_inc(made, 1)

            def down(g, i):
                w = width(i)
                after(pe, (hi_made, NI * g + i + 1), tick=pe_tick)
                if isinstance(g, int) and g == 0:
                    pe.wait_ge(down_lo_made, i + 1)
                for n in range(TG):
                    if i == 0:
                        after(pe, (y_ready, TG * (g - 1) + n + 1), tick=pe_tick)
                    hi = hid_hi[0:w, i % 2, P * n:P * n + P]
                    pe.matmul(pdown[n][:, :], hi, down_hi[0:w, i, :], start=i == 0, stop=False)
                    pe.matmul(pdown[n][:, :], hi, down_lo[0:w, i, :], start=False, stop=False)
                after(pe, (lo_made, NI * g + i + 1), tick=pe_tick)
                for n in range(TG):
                    lo = hid_lo[0:w, i % 2, P * n:P * n + P]
                    mm = pe.matmul(pdown[n][:, :], lo, down_hi[0:w, i, :], start=False, stop=i == LAST)
                    if i == LAST:
                        mm.then_inc(bank_done, 1)
                if i < LAST:
                    mm.then_inc(down_done, 1)

            def group(g):
                for n in range(TG):
                    transpose_n(g, n)
                if not isinstance(g, int):
                    down(g - 1, LAST)
                after(pe, (nlo_kept, TG * g + TG), tick=pe_tick)
                for i in range(NI):
                    product(g, i, 0, pgate[i % 2], gated, gate_made)
                    product(g, i, 1, pup[i % 2], hid_made, up_made)
                    if 0 < i < LAST - 1:
                        down(g, i - 1)
                down(g, LAST - 2)
                down(g, LAST - 1)

            group(0)
            pe.wait_ge(down_lo_made, NI)
            with pe.Fori(1, GROUPS) as g:
                group(g)
            down(GROUPS - 1, LAST)

        @block.vector
        def _(dve):
            def keep_low_n(g, n):
                after(dve, (nhi_kept, TG * g + n + 1), tick=dve_tick)
                cols = slice(P * n, P * n + P)
                dve.tensor_tensor(nT_lo[:, :, cols], tbank[n % 2][:, :].rearrange("p (k n) -> p k n", k=KD), nT_hi[:, :, cols].bitcast(F32),
                                  ALU.subtract).then_inc(nlo_kept, 1)

            def activate(g, i):
                w, n = width(i), NI * g + i
                e, h = expo[0:w, i % 2, :], hid[0:w, i % 2, :]
                if isinstance(g, int) and i == 0:
                    dve.wait_ge(bias_loaded, 80)
                after(dve, (expo_made, n + 1), tick=dve_tick)
                dve.tensor_scalar(e, e, 1.0, None, ALU.add).then_inc(expo_step, 1)
                after(dve, (expo_step, 2 * n + 1), tick=dve_tick)
                dve.reciprocal(e, e).then_inc(expo_step, 1)
                after(dve, (expo_step, 2 * n + 2), (hi_made, read_before(g, i)), (lo_made, read_before(g, i)), tick=dve_tick)
                dve.scalar_tensor_tensor(h, pgate[i % 2][0:w, :], b_gate[0:w, i:i + 1], e, ALU.add, ALU.mult).then_inc(gated, 1)
                after(dve, (gated, n + 1), (up_made, n + 1), tick=dve_tick)
                dve.scalar_tensor_tensor(h, pup[i % 2][0:w, :], b_up[0:w, i:i + 1], h, ALU.add, ALU.mult).then_inc(hid_made, 1)

            def keep_low(g, i):
                w = width(i)
                after(dve, (hi_made, NI * g + i + 1), down_before(g, i), tick=dve_tick)
                dve.tensor_tensor(hid_lo[0:w, i % 2, :], hid[0:w, i % 2, :], hid_hi[0:w, i % 2, :].bitcast(F32), ALU.subtract).then_inc(lo_made, 1)

            def finish(g):
                for n in range(TG):
                    after(dve, (bank_done, TG * g + n + 1), (res_biased, TG * g + n + 1), tick=dve_tick)
                    dve.tensor_tensor(x_res[:, n, :], pdown[n][:, :], x_res[:, n, :], ALU.add).then_inc(y_ready, 1)

            def group(g):
                keep_low_n(g, 0)
                keep_low_n(g, 1)
                if not isinstance(g, int):
                    keep_low(g - 1, LAST)
                keep_low_n(g, 2)
                keep_low_n(g, 3)
                if not isinstance(g, int):
                    finish(g - 1)
                for i in range(NI):
                    activate(g, i)
                    keep_low(g, i) if i < LAST else None

            group(0)
            with dve.Fori(1, GROUPS) as g:
                group(g)
            keep_low(GROUPS - 1, LAST)
            finish(GROUPS - 1)


def build(nc, a, out, phases=4):
    with ExitStack() as stack:
        def sb(name, shape, dt=F32):
            return stack.enter_context(nc.sbuf_tensor(name, shape, dt))

        def dram(name, shape):
            return nc.dram_tensor(name, shape, F32, kind="Internal").ap()

        shared = {
            "xs": dram("expert_rows", [EXPERTS * REGION, DIM]), "ys": dram("expert_results", [BLOCKS * P, DIM]),
            "x1": dram("x_after_attention0", [TILES, P, DIM]), "x3": dram("x_after_attention1", [TILES, P, DIM]),
            "n3": dram("norm_after_attention1", [TILES, P, DIM]),
            "last": sb("last", [P, 1]), "table": sb("table", [P, 2, BLOCKS], I32), "y_at": sb("y_at", [P, 2 * TILES], I32),
        }
        shared["x2"] = dram("x_after_experts", [TILES, P, DIM])
        with ExitStack() as moe:
            shared["w_hi"] = moe.enter_context(nc.sbuf_tensor("expert_w_hi", [P, EXPERTS * EW], F32R))
            shared["w_lo"] = moe.enter_context(nc.sbuf_tensor("expert_w_lo", [P, EXPERTS * EW], F32R))
            layer0_phase(nc, shared, {k: a[v] for k, v in dict(
                x="x", ctx="ctx_4096", Wq="L0_xattn_Wq", bq="L0_xattn_bq", Wk="L0_xattn_Wk", bk="L0_xattn_bk",
                Wv="L0_xattn_Wv", bv="L0_xattn_bv", Wo="L0_xattn_Wo", bo="L0_xattn_bo",
                W_gate="L0_ffn_W_gate", b_gate="L0_ffn_b_gate", W_e="L0_ffn_W_e").items()})
            if phases < 2:
                return
            expert_phase(nc, shared, a["L0_ffn_b_e"])
        if phases < 3:
            return
        shared["gu_hi"] = sb("gate_up_hi", [P, 2 * KD * INTER], F32R)
        shared["gu_lo"] = sb("gate_up_lo", [P, 2 * KD * INTER], F32R)
        layer1_phase(nc, shared, {"ctxT": a["ctxT"], "gate_up": a["gate_up"], "Wq": a["L1_xattn_Wq"], "Wk": a["L1_xattn_Wk"],
                                  "Wv": a["L1_xattn_Wv"], "Wo": a["L1_xattn_Wo"]})
        if phases < 4:
            return
        ffn_phase(nc, shared, {"w_down": a["L1_ffn_w_down"], "b_down": a["L1_ffn_b_down"],
                               **{k: a[k] for k in ("b_gate_main", "b_gate_rest", "b_up_main", "b_up_rest")}}, out)


TRANSPOSED = ("L0_xattn_Wq", "L0_xattn_Wk", "L0_xattn_Wv", "L0_xattn_Wo", "L1_ffn_w_gate", "L1_ffn_w_up", "L1_ffn_w_down")


def layout(inputs):
    import numpy as np
    a = {n: np.asarray(x) for n, x in inputs.items()}
    a = {n: x.T if n in TRANSPOSED else x for n, x in a.items()}
    a["ctxT"] = a["ctx_4096"].reshape(TILES, P, KD, P).transpose(0, 3, 2, 1).reshape(TILES, P, DIM)
    a["L1_xattn_Wq"] = a["L1_xattn_Wq"].reshape(DIM, KVH, GROUP, HD).transpose(0, 2, 1, 3).reshape(DIM, DIM)
    a["L1_xattn_Wo"] = a["L1_xattn_Wo"].reshape(KVH, GROUP, HD, DIM).transpose(1, 0, 2, 3).reshape(DIM, DIM)
    both = np.stack([a.pop("L1_ffn_w_gate"), a.pop("L1_ffn_w_up")])
    a["gate_up"] = both.reshape(2, KD, P, 2, INTER // 2).transpose(0, 1, 3, 2, 4).reshape(TILES, P, INTER // 2)
    for b in ("gate", "up"):
        bias, full = a.pop("L1_ffn_b_" + b), INTER // P
        a[f"b_{b}_main"] = bias[:full * P].reshape(full, P).T
        a[f"b_{b}_rest"] = bias[full * P:].reshape(-1, 1)
    return {n: np.ascontiguousarray(x) for n, x in a.items()}


def kernel(**inputs):
    import numpy as np
    from concourse import bacc
    from concourse.bass_utils import run_bass_kernel_spmd

    nc = bacc.Bacc("TRN2", target_bir_lowering=False, num_devices=1)
    arrays = layout(inputs)
    args = {n: nc.dram_tensor(n, x.shape, mybir.dt.from_np(x.dtype), kind="ExternalInput").ap() for n, x in arrays.items()}
    out = nc.dram_tensor("out", (BATCH, SEQ, DIM), F32, kind="ExternalOutput").ap()
    build(nc, args, out)
    result = run_bass_kernel_spmd(nc, [arrays], core_ids=[0])
    return result.results[0]["out"]
```
